# Optimizing a Trainium2 kernel written in Bass

```python
import numpy as np
import jax
import jax.numpy as jnp

def _softmax(x, axis=-1):
    return jax.nn.softmax(x, axis=axis)

def _gelu(x):
    return jax.nn.gelu(x, approximate=True)

def _silu(x):
    return jax.nn.silu(x)

def _sigmoid(x):
    return jax.nn.sigmoid(x)

def _layernorm(x, axis=-1, eps=1e-05):
    m = jnp.mean(x, axis=axis, keepdims=True)
    v = jnp.var(x, axis=axis, keepdims=True)
    return (x - m) / jnp.sqrt(v + eps)

def _scatter_add(tgt, idx, src, axis=0):
    return tgt.at[idx].add(src)

def _segment_sum(src, seg, n):
    return jax.ops.segment_sum(src, seg, n)
kernel_name = 'mk_audio_tower_d4_tok_audfeat768_r4_c13787'

def setup_inputs(seed: int=0):
    np.random.seed(seed)
    _w = jnp.asarray

    def _rec_inputs():
        import jax
        import jax.numpy as jnp
        _rk = jax.random.key(seed)
        x = -4.65018e-05 + 0.999886 * jax.random.normal(jax.random.fold_in(_rk, 1), (2, 2048, 192), jnp.float32)
        return x
    x = _rec_inputs()

    def _L0_tok_setup():
        import jax, jax.numpy as jnp
        import numpy as np
        POOL_SIZE = 2
        STRIDE = 2
        CHANNELS = 192
        key = jax.random.key(seed)
        k1, = jax.random.split(key, 1)
        x = jax.random.normal(k1, (8, 2048, CHANNELS), dtype=jnp.float32)
        w = jnp.eye(CHANNELS, dtype=jnp.float32) * 2.0
        return {'x': x, 'w': w}
    _L0_tok_all = _L0_tok_setup()
    _L0_tok_in = {k: v for k, v in _L0_tok_all.items() if k in ('w',)}
    del _L0_tok_all

    def _L0_attn_setup():
        import jax, jax.numpy as jnp
        import numpy as np
        B, T, D = (2, 1024, 192)
        H, HD = (6, D // 6)
        key = jax.random.key(seed)
        ks = jax.random.split(key, 8)
        s = 0.02
        return {'x': jax.random.normal(ks[0], (B, T, D), dtype=jnp.float32), 'Wq': jax.random.normal(ks[1], (D, D), dtype=jnp.float32) * s, 'Wk': jax.random.normal(ks[2], (D, D), dtype=jnp.float32) * s, 'Wv': jax.random.normal(ks[3], (D, D), dtype=jnp.float32) * s, 'Wo': jax.random.normal(ks[4], (D, D), dtype=jnp.float32) * s, 'anchor_w': jax.random.normal(ks[5], (H, HD, 6), dtype=jnp.float32) * s, 'anchors': jnp.sign(jax.random.normal(ks[6], (H, 6), dtype=jnp.float32)), 'lam': jnp.full((H,), 0.1, dtype=jnp.float32)}
    _L0_attn_all = _L0_attn_setup()
    _L0_attn_in = {k: v for k, v in _L0_attn_all.items() if k in ('Wq', 'Wk', 'Wv', 'Wo', 'anchor_w', 'anchors', 'lam')}
    del _L0_attn_all

    def _L0_ffn_setup():
        import jax, jax.numpy as jnp
        import numpy as np
        B, S, D = (2, 512, 192)
        E, K, F = (8, 2, 384)

        def _swiglu(xf, wg, wu, wd):
            return jax.nn.silu(xf @ wg.T) * (xf @ wu.T) @ wd.T
        key = jax.random.key(seed)
        ks = jax.random.split(key, 9)
        scale = 0.02
        x = jax.random.normal(ks[0], (B, S, D), dtype=jnp.float32)
        w_router = jax.random.normal(ks[1], (E, D), dtype=jnp.float32) * scale
        expert_bias = jnp.zeros((E,), dtype=jnp.float32)
        Wg = jax.random.normal(ks[2], (E, F, D), dtype=jnp.float32) * scale
        Wu = jax.random.normal(ks[3], (E, F, D), dtype=jnp.float32) * scale
        Wd = jax.random.normal(ks[4], (E, D, F), dtype=jnp.float32) * scale
        sg = jax.random.normal(ks[5], (F, D), dtype=jnp.float32) * scale
        su = jax.random.normal(ks[6], (F, D), dtype=jnp.float32) * scale
        sd = jax.random.normal(ks[7], (D, F), dtype=jnp.float32) * scale
        return {'x': x, 'w_router': w_router, 'expert_bias': expert_bias, 'Wg': Wg, 'Wu': Wu, 'Wd': Wd, 'sg': sg, 'su': su, 'sd': sd}
    _L0_ffn_all = _L0_ffn_setup()
    _L0_ffn_in = {k: v for k, v in _L0_ffn_all.items() if k in ('w_router', 'expert_bias', 'Wg', 'Wu', 'Wd', 'sg', 'su', 'sd')}
    del _L0_ffn_all

    def _L1_attn_setup():
        import jax, jax.numpy as jnp
        import numpy as np
        EMBED_DIM = 192
        SEQ_LEN = 256
        BATCH = 16
        ALPHA = 0.99
        key = jax.random.key(seed)
        k_x, k_w, k_b = jax.random.split(key, 3)
        d = EMBED_DIM
        x = jax.random.normal(k_x, (BATCH, SEQ_LEN, d), dtype=jnp.float32)
        lim = 1.0 / np.sqrt(d)
        W_qkv = jax.random.uniform(k_w, (3 * d, d), dtype=jnp.float32, minval=-lim, maxval=lim)
        b_qkv = jax.random.uniform(k_b, (3 * d,), dtype=jnp.float32, minval=-lim, maxval=lim)
        return {'x': x, 'W_qkv': W_qkv, 'b_qkv': b_qkv}
    _L1_attn_all = _L1_attn_setup()
    _L1_attn_in = {k: v for k, v in _L1_attn_all.items() if k in ('W_qkv', 'b_qkv')}
    del _L1_attn_all

    def _L1_ffn_setup():
        import jax, jax.numpy as jnp
        import numpy as np
        B, S, H, I = (4, 512, 192, 384)
        E, K = (3, 2)
        INIT = 0.02

        def _expert(x, gw, uw, dw):
            return jax.nn.silu(x @ gw) * (x @ uw) @ dw
        key = jax.random.key(seed)
        ks = jax.random.split(key, 8)
        f32 = jnp.float32
        return {'x': jax.random.normal(ks[0], (B, S, H), f32), 'shared_gate': jax.random.normal(ks[1], (H, I), f32) * INIT, 'shared_up': jax.random.normal(ks[2], (H, I), f32) * INIT, 'shared_down': jax.random.normal(ks[3], (I, H), f32) * INIT, 'routed_gate': jax.random.normal(ks[4], (E, H, I), f32) * INIT, 'routed_up': jax.random.normal(ks[5], (E, H, I), f32) * INIT, 'routed_down': jax.random.normal(ks[6], (E, I, H), f32) * INIT, 'router_w': jax.random.normal(ks[7], (H, E), f32) * INIT, 'routing_bias': jnp.zeros((E,), f32)}
    _L1_ffn_all = _L1_ffn_setup()
    _L1_ffn_in = {k: v for k, v in _L1_ffn_all.items() if k in ('shared_gate', 'shared_up', 'shared_down', 'routed_gate', 'routed_up', 'routed_down', 'router_w', 'routing_bias')}
    del _L1_ffn_all

    def _L2_attn_setup():
        import jax, jax.numpy as jnp
        import numpy as np
        LN_EPS = 1e-12

        def _layer_norm(y, g, b):
            m = jnp.mean(y, -1, keepdims=True)
            v = jnp.var(y, -1, keepdims=True)
            return (y - m) * jax.lax.rsqrt(v + LN_EPS) * g + b
        key = jax.random.key(seed)
        ks = jax.random.split(key, 8)
        B, L, E, K = (4, 256, 192, 12)
        I = 4 * E
        std = 0.02
        return {'x': jax.random.normal(ks[0], (B, L, E), jnp.float32), 'mu': jax.random.normal(ks[1], (K, E), jnp.float32) * std, 'val_w': jax.random.normal(ks[2], (E, E), jnp.float32) * std, 'val_b': jnp.zeros((E,), jnp.float32), 'w1': jax.random.normal(ks[3], (E, I), jnp.float32) * std, 'b1': jnp.zeros((I,), jnp.float32), 'w2': jax.random.normal(ks[4], (I, E), jnp.float32) * std, 'b2': jnp.zeros((E,), jnp.float32), 'ln_g': jnp.ones((E,), jnp.float32), 'ln_b': jnp.zeros((E,), jnp.float32)}
    _L2_attn_all = _L2_attn_setup()
    _L2_attn_in = {k: v for k, v in _L2_attn_all.items() if k in ('mu', 'val_w', 'val_b', 'w1', 'b1', 'w2', 'b2', 'ln_g', 'ln_b')}
    del _L2_attn_all

    def _L2_ffn_setup():
        import jax, jax.numpy as jnp
        import numpy as np
        B, S, H, D, E = (4, 512, 192, 256, 8)
        TOP_K = 2
        EPS = 1e-08
        LN_EPS = 1e-05

        def _gelu(t):
            return jax.nn.gelu(t, approximate=False)

        def _layer_norm(t, gamma, beta):
            mu = jnp.mean(t, axis=-1, keepdims=True)
            var = jnp.mean(jnp.square(t - mu), axis=-1, keepdims=True)
            return (t - mu) * jax.lax.rsqrt(var + LN_EPS) * gamma + beta
        key = jax.random.key(seed)
        ks = jax.random.split(key, 8)
        x = jax.random.normal(ks[0], (B, S, H), dtype=jnp.float32)
        w1 = jax.random.normal(ks[1], (H, H // 2), dtype=jnp.float32) * 0.02
        b1 = jnp.zeros((H // 2,), dtype=jnp.float32)
        w2 = jax.random.normal(ks[2], (H // 2, E), dtype=jnp.float32) * 0.02
        b2 = jnp.zeros((E,), dtype=jnp.float32)
        a_dn = float(np.sqrt(6.0 / (H + D)))
        a_up = float(np.sqrt(6.0 / (D + H)))
        down_w = jax.random.uniform(ks[3], (E, H, D), dtype=jnp.float32, minval=-a_dn, maxval=a_dn)
        down_b = jnp.zeros((E, D), dtype=jnp.float32)
        up_w = jax.random.uniform(ks[4], (E, D, H), dtype=jnp.float32, minval=-a_up, maxval=a_up)
        gamma = jnp.ones((H,), dtype=jnp.float32)
        beta = jnp.zeros((H,), dtype=jnp.float32)
        return {'x': x, 'w1': w1, 'b1': b1, 'w2': w2, 'b2': b2, 'down_w': down_w, 'down_b': down_b, 'up_w': up_w, 'gamma': gamma, 'beta': beta}
    _L2_ffn_all = _L2_ffn_setup()
    _L2_ffn_in = {k: v for k, v in _L2_ffn_all.items() if k in ('w1', 'b1', 'w2', 'b2', 'down_w', 'down_b', 'up_w', 'gamma', 'beta')}
    del _L2_ffn_all

    def _L3_attn_setup():
        import jax, jax.numpy as jnp
        import numpy as np
        NUM_HEADS = 12
        BITS_A = 8
        BITS_S = 4
        QMIN = -2 ** (BITS_A - 1)
        QMAX = 2 ** (BITS_A - 1) - 1

        def fake_quant(x, scale, qmin=QMIN, qmax=QMAX):
            q = jnp.clip(jnp.round(x / scale), qmin, qmax) * scale
            return x + jax.lax.stop_gradient(q - x)

        def int_log_softmax(attn, scale):
            scale = scale.reshape(())
            x_int = attn / scale
            x_int = x_int - jnp.max(x_int, axis=-1, keepdims=True)
            n = 30
            x0_int = jnp.floor(-0.6931 / scale)
            x_int = jnp.maximum(x_int, n * x0_int)
            qq = jnp.floor(x_int / x0_int)
            r = x_int - x0_int * qq
            c0, c1, c2 = (0.35815147, 0.96963238, 1.0)
            b_int = jnp.floor(c1 / c0 / scale)
            c_int = jnp.floor(c2 / c0 / scale ** 2)
            exp_int = jnp.maximum(jnp.floor((r * (r + b_int) + c_int) * 2.0 ** (n - qq)), 0.0)
            exp_sum = jnp.sum(exp_int, axis=-1, keepdims=True)
            ratio = jnp.round(exp_sum / jnp.maximum(exp_int, 1.0))
            lf = jnp.floor(jnp.log2(jnp.maximum(ratio, 1.0)))
            big = jnp.where(ratio - 2.0 ** lf >= 2.0 ** (lf - 1.0), lf + 1.0, lf)
            mask = (big >= 2 ** BITS_S) | (exp_int <= 0.0)
            qlog = jnp.clip(big, 0.0, 2.0 ** BITS_S - 1.0)
            deq = jnp.where(mask, 0.0, 2.0 ** (-qlog))
            soft = jax.nn.softmax(attn, axis=-1)
            return soft + jax.lax.stop_gradient(deq - soft)
        key = jax.random.key(seed)
        ks = jax.random.split(key, 3)
        B, N, C = (32, 197, 192)
        x = jax.random.normal(ks[0], (B, N, C), jnp.float32)
        w_qkv = jax.random.normal(ks[1], (3 * C, C), jnp.float32) * C ** (-0.5)
        w_proj = jax.random.normal(ks[2], (C, C), jnp.float32) * C ** (-0.5)
        b_proj = jnp.zeros((C,), jnp.float32)
        s_wqkv = jnp.max(jnp.abs(w_qkv), axis=1) / QMAX
        s_wproj = jnp.max(jnp.abs(w_proj), axis=1) / QMAX
        s_act1 = jnp.array([0.05], jnp.float32)
        s_attn = jnp.array([0.05], jnp.float32)
        s_act2 = jnp.array([0.02], jnp.float32)
        s_act3 = jnp.array([0.02], jnp.float32)
        return dict(x=x, w_qkv=w_qkv, w_proj=w_proj, b_proj=b_proj, s_wqkv=s_wqkv, s_wproj=s_wproj, s_act1=s_act1, s_attn=s_attn, s_act2=s_act2, s_act3=s_act3)
    _L3_attn_all = _L3_attn_setup()
    _L3_attn_in = {k: v for k, v in _L3_attn_all.items() if k in ('w_qkv', 'w_proj', 'b_proj', 's_wqkv', 's_wproj', 's_act1', 's_attn', 's_act2', 's_act3')}
    del _L3_attn_all

    def _L3_ffn_setup():
        import jax, jax.numpy as jnp
        import numpy as np
        TOP_K = 2
        key = jax.random.key(seed)
        ks = jax.random.split(key, 5)
        B, S, D, H, E = (1, 512, 192, 768, 8)
        x = jax.random.normal(ks[0], (B, S, D), dtype=jnp.float32)
        gate_w = jax.random.normal(ks[1], (E, D), dtype=jnp.float32) * 0.02
        w1 = jax.random.normal(ks[2], (E, D, H), dtype=jnp.float32) * 0.02
        b1 = jnp.zeros((E, H), dtype=jnp.float32)
        w2 = jax.random.normal(ks[3], (E, H, D), dtype=jnp.float32) * 0.02
        b2 = jnp.zeros((E, D), dtype=jnp.float32)
        return {'x': x, 'gate_w': gate_w, 'w1': w1, 'b1': b1, 'w2': w2, 'b2': b2}
    _L3_ffn_all = _L3_ffn_setup()
    _L3_ffn_in = {k: v for k, v in _L3_ffn_all.items() if k in ('gate_w', 'w1', 'b1', 'w2', 'b2')}
    del _L3_ffn_all
    return {'x': x, 'L0_tok_w': _L0_tok_in['w'], 'L0_attn_Wq': _L0_attn_in['Wq'], 'L0_attn_Wk': _L0_attn_in['Wk'], 'L0_attn_Wv': _L0_attn_in['Wv'], 'L0_attn_Wo': _L0_attn_in['Wo'], 'L0_attn_anchor_w': _L0_attn_in['anchor_w'], 'L0_attn_anchors': _L0_attn_in['anchors'], 'L0_attn_lam': _L0_attn_in['lam'], 'L0_ffn_w_router': _L0_ffn_in['w_router'], 'L0_ffn_expert_bias': _L0_ffn_in['expert_bias'], 'L0_ffn_Wg': _L0_ffn_in['Wg'], 'L0_ffn_Wu': _L0_ffn_in['Wu'], 'L0_ffn_Wd': _L0_ffn_in['Wd'], 'L0_ffn_sg': _L0_ffn_in['sg'], 'L0_ffn_su': _L0_ffn_in['su'], 'L0_ffn_sd': _L0_ffn_in['sd'], 'L1_attn_W_qkv': _L1_attn_in['W_qkv'], 'L1_attn_b_qkv': _L1_attn_in['b_qkv'], 'L1_ffn_shared_gate': _L1_ffn_in['shared_gate'], 'L1_ffn_shared_up': _L1_ffn_in['shared_up'], 'L1_ffn_shared_down': _L1_ffn_in['shared_down'], 'L1_ffn_routed_gate': _L1_ffn_in['routed_gate'], 'L1_ffn_routed_up': _L1_ffn_in['routed_up'], 'L1_ffn_routed_down': _L1_ffn_in['routed_down'], 'L1_ffn_router_w': _L1_ffn_in['router_w'], 'L1_ffn_routing_bias': _L1_ffn_in['routing_bias'], 'L2_attn_mu': _L2_attn_in['mu'], 'L2_attn_val_w': _L2_attn_in['val_w'], 'L2_attn_val_b': _L2_attn_in['val_b'], 'L2_attn_w1': _L2_attn_in['w1'], 'L2_attn_b1': _L2_attn_in['b1'], 'L2_attn_w2': _L2_attn_in['w2'], 'L2_attn_b2': _L2_attn_in['b2'], 'L2_attn_ln_g': _L2_attn_in['ln_g'], 'L2_attn_ln_b': _L2_attn_in['ln_b'], 'L2_ffn_w1': _L2_ffn_in['w1'], 'L2_ffn_b1': _L2_ffn_in['b1'], 'L2_ffn_w2': _L2_ffn_in['w2'], 'L2_ffn_b2': _L2_ffn_in['b2'], 'L2_ffn_down_w': _L2_ffn_in['down_w'], 'L2_ffn_down_b': _L2_ffn_in['down_b'], 'L2_ffn_up_w': _L2_ffn_in['up_w'], 'L2_ffn_gamma': _L2_ffn_in['gamma'], 'L2_ffn_beta': _L2_ffn_in['beta'], 'L3_attn_w_qkv': _L3_attn_in['w_qkv'], 'L3_attn_w_proj': _L3_attn_in['w_proj'], 'L3_attn_b_proj': _L3_attn_in['b_proj'], 'L3_attn_s_wqkv': _L3_attn_in['s_wqkv'], 'L3_attn_s_wproj': _L3_attn_in['s_wproj'], 'L3_attn_s_act1': _L3_attn_in['s_act1'], 'L3_attn_s_attn': _L3_attn_in['s_attn'], 'L3_attn_s_act2': _L3_attn_in['s_act2'], 'L3_attn_s_act3': _L3_attn_in['s_act3'], 'L3_ffn_gate_w': _L3_ffn_in['gate_w'], 'L3_ffn_w1': _L3_ffn_in['w1'], 'L3_ffn_b1': _L3_ffn_in['b1'], 'L3_ffn_w2': _L3_ffn_in['w2'], 'L3_ffn_b2': _L3_ffn_in['b2']}

def reference(x, L0_tok_w, L0_attn_Wq, L0_attn_Wk, L0_attn_Wv, L0_attn_Wo, L0_attn_anchor_w, L0_attn_anchors, L0_attn_lam, L0_ffn_w_router, L0_ffn_expert_bias, L0_ffn_Wg, L0_ffn_Wu, L0_ffn_Wd, L0_ffn_sg, L0_ffn_su, L0_ffn_sd, L1_attn_W_qkv, L1_attn_b_qkv, L1_ffn_shared_gate, L1_ffn_shared_up, L1_ffn_shared_down, L1_ffn_routed_gate, L1_ffn_routed_up, L1_ffn_routed_down, L1_ffn_router_w, L1_ffn_routing_bias, L2_attn_mu, L2_attn_val_w, L2_attn_val_b, L2_attn_w1, L2_attn_b1, L2_attn_w2, L2_attn_b2, L2_attn_ln_g, L2_attn_ln_b, L2_ffn_w1, L2_ffn_b1, L2_ffn_w2, L2_ffn_b2, L2_ffn_down_w, L2_ffn_down_b, L2_ffn_up_w, L2_ffn_gamma, L2_ffn_beta, L3_attn_w_qkv, L3_attn_w_proj, L3_attn_b_proj, L3_attn_s_wqkv, L3_attn_s_wproj, L3_attn_s_act1, L3_attn_s_attn, L3_attn_s_act2, L3_attn_s_act3, L3_ffn_gate_w, L3_ffn_w1, L3_ffn_b1, L3_ffn_w2, L3_ffn_b2):
    import jax
    import jax.numpy as jnp

    def _L0_tok_ref(x, w):
        import jax, jax.numpy as jnp
        import numpy as np
        POOL_SIZE = 2
        STRIDE = 2
        CHANNELS = 192
        B, S, C = x.shape
        n_windows = (S - POOL_SIZE) // STRIDE + 1
        window = jnp.stack([x[:, i::STRIDE, :][:, :n_windows, :] for i in range(POOL_SIZE)], axis=2)
        scores = jnp.einsum('bnpc,cd->bnpd', window, w)
        weights = jax.nn.softmax(scores, axis=2)
        return jnp.sum(weights * window, axis=2)

    def _L0_attn_ref(x, Wq, Wk, Wv, Wo, anchor_w, anchors, lam):
        import jax, jax.numpy as jnp
        import numpy as np
        B, T, D = (2, 1024, 192)
        H, HD = (6, D // 6)
        b, t, d = x.shape
        scale = HD ** (-0.5)
        q = (x @ Wq.T).reshape(b, t, H, HD).transpose(0, 2, 1, 3)
        k = (x @ Wk.T).reshape(b, t, H, HD).transpose(0, 2, 1, 3)
        v = (x @ Wv.T).reshape(b, t, H, HD).transpose(0, 2, 1, 3)
        scores = jnp.einsum('bhqd,bhkd->bhqk', q, k) * scale
        anchor_h = jnp.einsum('hde,he->hd', anchor_w, anchors)
        anchor_sim = jnp.einsum('bhtd,hd->bht', q, anchor_h)
        scores = scores + (lam[None, :, None] * anchor_sim)[..., None]
        attn = jax.nn.softmax(scores, axis=-1)
        out = jnp.einsum('bhqk,bhkd->bhqd', attn, v)
        out = out.transpose(0, 2, 1, 3).reshape(b, t, d)
        return out @ Wo.T

    def _L0_ffn_ref(x, w_router, expert_bias, Wg, Wu, Wd, sg, su, sd):
        import jax, jax.numpy as jnp
        import numpy as np
        B, S, D = (2, 512, 192)
        E, K, F = (8, 2, 384)

        def _swiglu(xf, wg, wu, wd):
            return jax.nn.silu(xf @ wg.T) * (xf @ wu.T) @ wd.T
        b, s, d = x.shape
        xf = x.reshape(-1, d)
        T = xf.shape[0]
        e = w_router.shape[0]
        logits = xf @ w_router.T
        scores = jax.nn.softmax(logits, axis=-1)
        selection = scores + expert_bias[None, :]
        _, top_idx = jax.lax.top_k(selection, K)
        top_s = jnp.take_along_axis(scores, top_idx, axis=-1)
        top_s = top_s / (jnp.sum(top_s, axis=-1, keepdims=True) + 1e-09)
        comb = jnp.zeros((T, e), dtype=x.dtype).at[jnp.arange(T)[:, None], top_idx].add(top_s)

        def body(acc, p):
            wg, wu, wd, c = p
            return (acc + c[:, None] * _swiglu(xf, wg, wu, wd), None)
        routed, _ = jax.lax.scan(body, jnp.zeros_like(xf), (Wg, Wu, Wd, comb.T))
        out = routed + _swiglu(xf, sg, su, sd)
        return out.reshape(b, s, d)

    def _L1_attn_ref(x, W_qkv, b_qkv):
        import jax, jax.numpy as jnp
        import numpy as np
        EMBED_DIM = 192
        SEQ_LEN = 256
        BATCH = 16
        ALPHA = 0.99
        bs, sl, d = x.shape
        qkv = x @ W_qkv.T + b_qkv
        q, k, v = jnp.split(qkv, 3, axis=-1)
        idx = jnp.arange(sl)
        diff = idx[:, None] - idx[None, :]
        M = jnp.where(diff >= 0, jnp.float32(ALPHA) ** diff.astype(jnp.float32), 0.0)
        dim_sqrt = jnp.asarray(d, jnp.float32) ** 0.5
        scores = jnp.einsum('bsd,btd->bst', q, k) / dim_sqrt * M
        out = jnp.einsum('bst,btd->bsd', scores, v)
        return out

    def _L1_ffn_ref(x, shared_gate, shared_up, shared_down, routed_gate, routed_up, routed_down, router_w, routing_bias):
        import jax, jax.numpy as jnp
        import numpy as np
        B, S, H, I = (4, 512, 192, 384)
        E, K = (3, 2)
        INIT = 0.02

        def _expert(x, gw, uw, dw):
            return jax.nn.silu(x @ gw) * (x @ uw) @ dw
        shared_out = _expert(x, shared_gate, shared_up, shared_down)
        routing_probs = jax.nn.sigmoid(x @ router_w + routing_bias)
        scores, indices = jax.lax.top_k(routing_probs, K)
        scores = scores / scores.sum(axis=-1, keepdims=True)
        combine_w = (jax.nn.one_hot(indices, E, dtype=x.dtype) * scores[..., None]).sum(axis=-2)
        g = jnp.einsum('bsh,ehi->ebsi', x, routed_gate)
        u = jnp.einsum('bsh,ehi->ebsi', x, routed_up)
        h = jax.nn.silu(g) * u
        out_e = jnp.einsum('ebsi,eih->ebsh', h, routed_down)
        combined = jnp.einsum('ebsh,bse->bsh', out_e, combine_w)
        return shared_out + combined

    def _L2_attn_ref(x, mu, val_w, val_b, w1, b1, w2, b2, ln_g, ln_b):
        import jax, jax.numpy as jnp
        import numpy as np
        LN_EPS = 1e-12

        def _layer_norm(y, g, b):
            m = jnp.mean(y, -1, keepdims=True)
            v = jnp.var(y, -1, keepdims=True)
            return (y - m) * jax.lax.rsqrt(v + LN_EPS) * g + b
        B, L, E = x.shape
        K = mu.shape[0]
        EOK = E // K
        k2 = jnp.sum(x * x, -1)
        xmu = jnp.einsum('ble,ke->blk', x, mu)
        mu2 = jnp.sum(mu * mu, -1)
        q2 = k2[:, :, None] + 2.0 * xmu + mu2[None, None, :]
        xx = jnp.einsum('ble,bme->blm', x, x)
        muk = jnp.einsum('ke,bme->bkm', mu, x)
        scores = -(q2[..., None] - 2.0 * (xx[:, :, None, :] + muk[:, None, :, :]) + k2[:, None, None, :]) / E
        att = jax.nn.softmax(scores, axis=-1)
        xv = (x @ val_w + val_b).reshape(B, L, K, EOK)
        xsel = jnp.einsum('blkm,bmkd->blkd', att, xv).reshape(B, L, E)
        h = x + xsel
        inter = jax.nn.gelu(h @ w1 + b1, approximate=False)
        y = inter @ w2 + b2 + h
        return _layer_norm(y, ln_g, ln_b)

    def _L2_ffn_ref(x, w1, b1, w2, b2, down_w, down_b, up_w, gamma, beta):
        import jax, jax.numpy as jnp
        import numpy as np
        B, S, H, D, E = (4, 512, 192, 256, 8)
        TOP_K = 2
        EPS = 1e-08
        LN_EPS = 1e-05

        def _gelu(t):
            return jax.nn.gelu(t, approximate=False)

        def _layer_norm(t, gamma, beta):
            mu = jnp.mean(t, axis=-1, keepdims=True)
            var = jnp.mean(jnp.square(t - mu), axis=-1, keepdims=True)
            return (t - mu) * jax.lax.rsqrt(var + LN_EPS) * gamma + beta
        logits = _gelu(x @ w1 + b1) @ w2 + b2
        routing = jax.nn.softmax(logits, axis=-1)
        topv, topi = jax.lax.top_k(routing, TOP_K)
        sparse = jnp.sum(jax.nn.one_hot(topi, E, dtype=routing.dtype) * topv[..., None], axis=-2)
        sparse = sparse / (jnp.sum(sparse, axis=-1, keepdims=True) + EPS)
        z = _gelu(jnp.einsum('bsh,ehd->bsed', x, down_w) + down_b)
        expert_out = jnp.einsum('bsed,edh->bseh', z, up_w)
        moe_out = jnp.einsum('bseh,bse->bsh', expert_out, sparse)
        return _layer_norm(x + moe_out, gamma, beta)

    def _L3_attn_ref(x, w_qkv, w_proj, b_proj, s_wqkv, s_wproj, s_act1, s_attn, s_act2, s_act3):
        import jax, jax.numpy as jnp
        import numpy as np
        NUM_HEADS = 12
        BITS_A = 8
        BITS_S = 4
        QMIN = -2 ** (BITS_A - 1)
        QMAX = 2 ** (BITS_A - 1) - 1

        def fake_quant(x, scale, qmin=QMIN, qmax=QMAX):
            q = jnp.clip(jnp.round(x / scale), qmin, qmax) * scale
            return x + jax.lax.stop_gradient(q - x)

        def int_log_softmax(attn, scale):
            scale = scale.reshape(())
            x_int = attn / scale
            x_int = x_int - jnp.max(x_int, axis=-1, keepdims=True)
            n = 30
            x0_int = jnp.floor(-0.6931 / scale)
            x_int = jnp.maximum(x_int, n * x0_int)
            qq = jnp.floor(x_int / x0_int)
            r = x_int - x0_int * qq
            c0, c1, c2 = (0.35815147, 0.96963238, 1.0)
            b_int = jnp.floor(c1 / c0 / scale)
            c_int = jnp.floor(c2 / c0 / scale ** 2)
            exp_int = jnp.maximum(jnp.floor((r * (r + b_int) + c_int) * 2.0 ** (n - qq)), 0.0)
            exp_sum = jnp.sum(exp_int, axis=-1, keepdims=True)
            ratio = jnp.round(exp_sum / jnp.maximum(exp_int, 1.0))
            lf = jnp.floor(jnp.log2(jnp.maximum(ratio, 1.0)))
            big = jnp.where(ratio - 2.0 ** lf >= 2.0 ** (lf - 1.0), lf + 1.0, lf)
            mask = (big >= 2 ** BITS_S) | (exp_int <= 0.0)
            qlog = jnp.clip(big, 0.0, 2.0 ** BITS_S - 1.0)
            deq = jnp.where(mask, 0.0, 2.0 ** (-qlog))
            soft = jax.nn.softmax(attn, axis=-1)
            return soft + jax.lax.stop_gradient(deq - soft)
        B, N, C = x.shape
        H = NUM_HEADS
        d = C // H
        sc = d ** (-0.5)
        wq = fake_quant(w_qkv, s_wqkv[:, None])
        h = x @ wq.T
        h = fake_quant(h, s_act1)
        qkv = h.reshape(B, N, 3, H, d).transpose(2, 0, 3, 1, 4)
        q, k, v = (qkv[0], qkv[1], qkv[2])
        attn = jnp.einsum('bhqd,bhkd->bhqk', q, k) * sc
        attn = fake_quant(attn, s_attn)
        p = int_log_softmax(attn, s_attn)
        o = jnp.einsum('bhqk,bhkd->bhqd', p, v)
        o = o.transpose(0, 2, 1, 3).reshape(B, N, C)
        o = fake_quant(o, s_act2)
        wp = fake_quant(w_proj, s_wproj[:, None])
        o = o @ wp.T + b_proj
        o = fake_quant(o, s_act3)
        return o

    def _L3_ffn_ref(x, gate_w, w1, b1, w2, b2):
        import jax, jax.numpy as jnp
        import numpy as np
        TOP_K = 2
        B, S, D = x.shape
        E, _, H = w1.shape
        T = B * S
        K = TOP_K
        xf = x.reshape(T, D)
        logits = xf @ gate_w.T
        probs = jax.nn.softmax(logits, axis=-1)
        top_w, top_i = jax.lax.top_k(probs, K)
        top_w = top_w / (jnp.sum(top_w, axis=-1, keepdims=True) + 1e-09)
        flat_e = top_i.reshape(-1)
        flat_w = top_w.reshape(-1)
        tok_idx = jnp.repeat(jnp.arange(T), K)
        order = jnp.argsort(flat_e)
        se = flat_e[order]
        pt = tok_idx[order]
        pw = flat_w[order]
        counts = jax.ops.segment_sum(jnp.ones(T * K, jnp.int32), se, num_segments=E)
        starts = jnp.concatenate([jnp.zeros((1,), jnp.int32), jnp.cumsum(counts)[:-1]])
        pos = jnp.arange(T * K) - starts[se]
        cap = T * K
        padded = jnp.zeros((E, cap, D), x.dtype).at[se, pos].set(xf[pt])
        hidden = jax.nn.gelu(jnp.einsum('ecd,edh->ech', padded, w1) + b1[:, None, :], approximate=False)
        out = jnp.einsum('ech,ehd->ecd', hidden, w2) + b2[:, None, :]
        expert_out = out[se, pos] * pw[:, None]
        final = jnp.zeros((T, D), x.dtype).at[pt].add(expert_out)
        return final.reshape(B, S, D)
    h = _L0_tok_ref(x, L0_tok_w)
    h = h + _L0_attn_ref(_layernorm(h, axis=-1), L0_attn_Wq, L0_attn_Wk, L0_attn_Wv, L0_attn_Wo, L0_attn_anchor_w, L0_attn_anchors, L0_attn_lam)
    h = h + _L0_ffn_ref(_layernorm(h, axis=-1), L0_ffn_w_router, L0_ffn_expert_bias, L0_ffn_Wg, L0_ffn_Wu, L0_ffn_Wd, L0_ffn_sg, L0_ffn_su, L0_ffn_sd)
    h = h + _L1_attn_ref(_layernorm(h, axis=-1), L1_attn_W_qkv, L1_attn_b_qkv)
    h = h + _L1_ffn_ref(_layernorm(h, axis=-1), L1_ffn_shared_gate, L1_ffn_shared_up, L1_ffn_shared_down, L1_ffn_routed_gate, L1_ffn_routed_up, L1_ffn_routed_down, L1_ffn_router_w, L1_ffn_routing_bias)
    h = h + _L2_attn_ref(_layernorm(h, axis=-1), L2_attn_mu, L2_attn_val_w, L2_attn_val_b, L2_attn_w1, L2_attn_b1, L2_attn_w2, L2_attn_b2, L2_attn_ln_g, L2_attn_ln_b)
    h = h + _L2_ffn_ref(_layernorm(h, axis=-1), L2_ffn_w1, L2_ffn_b1, L2_ffn_w2, L2_ffn_b2, L2_ffn_down_w, L2_ffn_down_b, L2_ffn_up_w, L2_ffn_gamma, L2_ffn_beta)
    h = h + _L3_attn_ref(_layernorm(h, axis=-1), L3_attn_w_qkv, L3_attn_w_proj, L3_attn_b_proj, L3_attn_s_wqkv, L3_attn_s_wproj, L3_attn_s_act1, L3_attn_s_attn, L3_attn_s_act2, L3_attn_s_act3)
    h = h + _L3_ffn_ref(_layernorm(h, axis=-1), L3_ffn_gate_w, L3_ffn_w1, L3_ffn_b1, L3_ffn_w2, L3_ffn_b2)
    return h

_drawn_inputs = setup_inputs


def setup_inputs(seed=0):
    import zlib

    import numpy as np

    out = dict(_drawn_inputs(seed))
    spreads = {'L0_attn_lam': (0.10000000149011612, 0.6),
     'L0_ffn_expert_bias': (0.0, 0.343),
     'L1_ffn_routing_bias': (0.0, 0.8),
     'L2_attn_val_b': (0.0, 0.702),
     'L2_attn_b1': (0.0, 2.0),
     'L2_attn_b2': (0.0, 0.549),
     'L2_attn_ln_g': (1.0, 0.6),
     'L2_attn_ln_b': (0.0, 0.546),
     'L2_ffn_b1': (0.0, 0.48),
     'L2_ffn_b2': (0.0, 0.1),
     'L2_ffn_down_b': (0.0, 1.972),
     'L2_ffn_gamma': (1.0, 0.6),
     'L2_ffn_beta': (0.0, 0.84),
     'L3_attn_b_proj': (0.0, 0.836),
     'L3_ffn_b1': (0.0, 0.8),
     'L3_ffn_b2': (0.0, 1.31)}
    factors = {'L0_attn_Wq': 8.0,
     'L0_attn_Wk': 8.0,
     'L0_attn_Wv': 8.0,
     'L0_attn_Wo': 7.847,
     'L0_attn_anchor_w': 200.0,
     'L0_attn_anchors': 200.0,
     'L0_ffn_w_router': 7.012,
     'L0_ffn_Wg': 2.867,
     'L0_ffn_Wu': 2.825,
     'L0_ffn_Wd': 2.893,
     'L1_ffn_shared_gate': 6.697,
     'L1_ffn_shared_up': 6.217,
     'L1_ffn_shared_down': 6.277,
     'L1_ffn_routed_gate': 8.0,
     'L1_ffn_routed_up': 8.0,
     'L1_ffn_routed_down': 8.0,
     'L1_ffn_router_w': 8.0,
     'L2_attn_mu': 200.0,
     'L2_attn_val_w': 6.877,
     'L3_attn_s_wqkv': 64.0,
     'L3_attn_s_wproj': 64.0,
     'L3_ffn_gate_w': 2.848,
     'L3_ffn_w1': 4.076,
     'L3_ffn_w2': 3.791,
     'L2_attn_w1': 4.423,
     'L2_ffn_w1': 2.891,
     'L3_attn_w_qkv': 3.677,
     'L3_attn_w_proj': 3.789}
    for name, (base, spread) in spreads.items():
        noise = np.random.default_rng([zlib.crc32(name.encode()), seed]).standard_normal(out[name].shape)
        drawn = base * np.exp(spread * noise) if base else spread * noise
        out[name] = jnp.asarray(drawn.astype(out[name].dtype))
    for name, factor in factors.items():
        out[name] = (out[name] * factor).astype(out[name].dtype)
    return out
```

```python
from contextlib import ExitStack

import concourse.bass as bass
from concourse import mybir

ALU = mybir.AluOpType
ACT = mybir.ActivationFunctionType
AXX = mybir.AxisListType.X
F32 = mybir.dt.float32
BF16 = mybir.dt.bfloat16
I16 = mybir.dt.int16
I32 = mybir.dt.int32
ds = bass.ds

P = 128
D = 192
KP, KC = 96, 2
BATCH, SEQ = 2, 1024
TOK = BATCH * SEQ
TILES = TOK // P
BLOCK = 512
NBLK = TOK // BLOCK
TPB = BLOCK // P
TPS = SEQ // P
BANK = 512
LN_EPS = 1e-5


class Own:

    def __init__(self, eng, sem):
        self.eng, self.sem, self.start, self.base, self.n = eng, sem, 0, 0, 0

    def step(self, instruction):
        instruction.then_inc(self.sem, 1)
        self.n += 1
        self.eng.wait_ge(self.sem, self.base + self.n)

    def enter(self, i, per):
        self.start, self.base, self.n, self.per = self.start + self.n, self.start + self.n + i * per, 0, per

    def leave(self, times):
        assert self.n == self.per, (self.n, self.per)
        self.start += times * self.per
        self.base, self.n = self.start, 0


class Phase:

    def __init__(self, nc, name):
        self.nc, self.name, self.stack, self.sems = nc, name, ExitStack(), []

    def sbuf(self, name, shape, dtype=F32):
        return self.stack.enter_context(self.nc.sbuf_tensor(self.name + name, shape, dtype))

    def psum(self, name, shape, dtype=F32):
        return self.stack.enter_context(self.nc.psum_tensor(self.name + name, shape, dtype))

    def semaphore(self, name):
        self.sems.append(self.nc.alloc_semaphore(self.name + name))
        return self.sems[-1]

    def __enter__(self):
        return self

    def __exit__(self, *failure):
        if failure[0] is None:
            self.nc.clear_and_free_semaphores(self.sems)
            self.nc.all_engine_barrier()
        self.stack.close()


def flat(t):
    return t[:, :, :].rearrange("p a b -> p (a b)")


def wide(ap, n):
    a = ap.unsqueeze(2)
    return a.to_broadcast([a.shape[0], a.shape[1], n])


def across(ap, n):
    a = ap.unsqueeze(1)
    return a.to_broadcast([a.shape[0], n, a.shape[2]])


def pool_phase(nc, k, x, tok_w):
    with Phase(nc, "po_") as phase:
        sb, ps, sem = phase.sbuf, phase.psum, phase.semaphore
        pairs = sb("pairs", [P, TILES, 2, D])
        w = sb("w", [KP, KC, D])
        diff = sb("diff", [P, 2, TPB, D])
        diffT = sb("diffT", [KP, 2, KC, BLOCK])
        gate = sb("gate", [P, 2, TPB, D])
        scaled = sb("scaled", [P, 2, TPB, D])
        psT = ps("psT", [P, 2, KC, BANK])
        psS = ps("psS", [P, 2, 2, BANK])
        x_in = [sem(f"x_in{g}") for g in range(NBLK)]
        w_in, ident0, ident1 = sem("w_in"), sem("ident0"), sem("ident1")
        diff_ready, transposed, diffT_ready = sem("diff_ready"), sem("transposed"), sem("diffT_ready")
        scores_ready, gate_ready, scaled_ready, h_ready = (
            sem("scores_ready"), sem("gate_ready"), sem("scaled_ready"), sem("h_ready"))
        xv = x.rearrange("b (n i) d -> (b n) i d", i=2).rearrange("(t p) i d -> p t i d", p=P)

        with nc.Block() as block:
            @block.sync
            def _(sp):
                sp.dma_start(w[:, :, :], tok_w).then_inc(w_in, 16)
                for g in range(NBLK):
                    sp.dma_start(pairs[:, g * TPB:(g + 1) * TPB], xv[:, g * TPB:(g + 1) * TPB]).then_inc(x_in[g], 16)

            @block.gpsimd
            def _(pool):
                pool.memset(k.ident[:, :], 0.0).then_inc(ident0, 1)
                pool.wait_ge(ident0, 1)
                pool.affine_select(out=k.ident[:, :], in_=k.ident[:, :], compare_op=ALU.not_equal, fill=1.0, base=0,
                                   pattern=[[-1, P]], channel_multiplier=1).then_inc(ident1, 1)
                pool.memset(k.minus_half[:, :], -0.5).then_inc(ident0, 1)
                for e in range(8):
                    last = pool.memset(k.rank[:, e:e + 1], float(8 - e))
                last.then_inc(ident0, 1)
                pool.wait_ge(ident1, 1)
                pool.tensor_copy(k.ident16[:, :], k.ident[:, :]).then_inc(ident0, 1)
                pool.wait_ge(ident0, 4)

            @block.vector
            def _(dve):
                def difference(g):
                    dve.wait_ge(x_in[g], 16)
                    if g >= 2:
                        dve.wait_ge(transposed, g - 1)
                        dve.wait_ge(scaled_ready, g - 1)
                    t = slice(g * TPB, (g + 1) * TPB)
                    dve.tensor_tensor(diff[:, g % 2], pairs[:, t, 0], pairs[:, t, 1], ALU.subtract).then_inc(diff_ready, 1)

                def combine(g):
                    t = slice(g * TPB, (g + 1) * TPB)
                    dve.wait_ge(diff_ready, g + 1)
                    dve.wait_ge(gate_ready, g + 1)
                    if g >= 2:
                        dve.wait_ge(h_ready, g - 1)
                    dve.tensor_tensor(scaled[:, g % 2], gate[:, g % 2], diff[:, g % 2], ALU.mult).then_inc(scaled_ready, 1)
                    dve.wait_ge(scaled_ready, g + 1)
                    dve.tensor_tensor(k.h[:, t], scaled[:, g % 2], pairs[:, t, 1], ALU.add).then_inc(h_ready, 1)

                difference(0)
                for g in range(1, NBLK):
                    difference(g)
                    combine(g - 1)
                combine(NBLK - 1)

            @block.tensor
            def _(pe):
                pe.wait_ge(ident1, 1)
                pe.wait_ge(w_in, 16)
                for g in range(NBLK):
                    pe.wait_ge(diff_ready, g + 1)
                    if g >= 2:
                        pe.wait_ge(diffT_ready, g - 1)
                    for t in range(TPB):
                        for j in range(KC):
                            last = pe.transpose(psT[0:KP, g % 2, j, t * P:(t + 1) * P],
                                                diff[:, g % 2, t, j * KP:(j + 1) * KP], k.ident[:, :])
                    last.then_inc(transposed, 1)
                    pe.wait_ge(diffT_ready, g + 1)
                    if g >= 2:
                        pe.wait_ge(gate_ready, g - 1)
                    for t in range(TPB):
                        for j in range(KC):
                            last = pe.matmul(psS[:, g % 2, t // 2, (t % 2) * D:(t % 2 + 1) * D],
                                             diffT[:, g % 2, j, t * P:(t + 1) * P], w[:, j, :],
                                             start=(j == 0), stop=(j == KC - 1))
                    last.then_inc(scores_ready, 1)

            @block.scalar
            def _(act):
                for g in range(NBLK):
                    act.wait_ge(transposed, g + 1)
                    if g >= 2:
                        act.wait_ge(scores_ready, g - 1)
                    act.activation(diffT[:, g % 2], psT[0:KP, g % 2], ACT.Copy).then_inc(diffT_ready, 1)
                    act.wait_ge(scores_ready, g + 1)
                    if g >= 2:
                        act.wait_ge(scaled_ready, g - 1)
                    act.activation(gate[:, g % 2].rearrange("p (a t) d -> p a (t d)", a=2), psS[:, g % 2, :, 0:2 * D],
                                   ACT.Sigmoid).then_inc(gate_ready, 1)


class Router:

    def __init__(self, kind, experts, w, select_bias=None, logit_bias=None, eps=0.0, hidden=None):
        self.kind, self.experts, self.w, self.eps, self.hidden = kind, experts, w, eps, hidden
        self.select_bias, self.logit_bias = select_bias, logit_bias


def norm_phase(nc, k, name, src, router=None, normalise=True):
    E = router.experts if router else 1
    R = router
    with Phase(nc, name) as phase:
        sb, ps, sem = phase.sbuf, phase.psum, phase.semaphore
        stats = sb("stats", [P, TILES, 6])
        moments = sb("moments", [P, TILES, 2])
        rstd0 = sb("rstd0", [P, TILES])
        rstd = sb("rstd", [P, TILES])
        psT = ps("psT", [P, 2, KC, BANK])
        own_sem, stats_ready, eps_added, rstd_ready = sem("own"), sem("stats_ready"), sem("eps_added"), sem("rstd_ready")
        moments_ready = sem("moments_ready")
        xn_ready, transposed, xnT_ready = sem("xn_ready"), sem("transposed"), sem("xnT_ready")
        if R:
            KR, CR = (KP, 1) if R.hidden else (KP, KC)
            wr = sb("wr", [KR, CR, E])
            sbias, lbias = sb("sbias", [P, E]), sb("lbias", [P, E])
            logits, probs, sel = sb("logits", [P, TILES, E]), sb("probs", [P, TILES, E]), sb("sel", [P, TILES, E])
            hit, first, second = sb("hit", [P, TILES, E]), sb("first", [P, TILES, E]), sb("second", [P, TILES, E])
            top, total, inverse = sb("top", [P, TILES]), sb("total", [P, TILES]), sb("inverse", [P, TILES])
            psR = ps("psR", [P, BANK])
            router_in, logits_ready, shifted, probs_ready = sem("router_in"), sem("logits_ready"), sem("shifted"), sem("probs_ready")
            if R.hidden:
                w1, b1 = sb("w1", [KP, KC, KP]), sb("b1", [KP, 1])
                hidT = sb("hidT", [KP, TOK])
                psH = ps("psH", [P, 2, BANK])
                hidden_ready, hidT_ready = sem("hidden_ready"), sem("hidT_ready")
        loads = 0
        if R:
            loads = 1 + (R.select_bias is not None) + (R.logit_bias is not None) + 2 * bool(R.hidden)

        with nc.Block() as block:
            if R:
                @block.sync
                def _(sp):
                    sp.dma_start(wr[:, :, :], R.w).then_inc(router_in, 16)
                    if R.select_bias is not None:
                        sp.dma_start(sbias[:, :], R.select_bias.partition_broadcast(P)).then_inc(router_in, 16)
                    if R.logit_bias is not None:
                        sp.dma_start(lbias[:, :], R.logit_bias.partition_broadcast(P)).then_inc(router_in, 16)
                    if R.hidden:
                        sp.dma_start(w1[:, :, :], R.hidden[0]).then_inc(router_in, 16)
                        sp.dma_start(b1[:, :], R.hidden[1]).then_inc(router_in, 16)

            if normalise:
                @block.gpsimd
                def _(pool):
                    pool.wait_ge(moments_ready, 1)
                    pool.tensor_scalar(rstd0[:, :], moments[:, :, 1], LN_EPS, None, ALU.add).then_inc(eps_added, 1)
                    pool.wait_ge(eps_added, 1)
                    pool.tensor_tensor(rstd[:, :], rstd0[:, :], k.minus_half[:, :], ALU.pow).then_inc(rstd_ready, 1)

            @block.vector
            def _(dve):
                own = Own(dve, own_sem)
                source, target, mom = flat(src), flat(k.xn), flat(moments)
                if normalise:
                    with dve.Fori(0, NBLK) as g:
                        for t in range(TPB):
                            tile = g * TPB + t
                            last = dve.bn_stats(flat(stats)[:, ds(tile * 6, 6)], source[:, ds(tile * D, D)])
                        last.then_inc(stats_ready, 1)
                    dve.wait_ge(stats_ready, NBLK)
                    for t in range(TILES):
                        last = dve.bn_aggr(moments[:, t, :], stats[:, t, :])
                    last.then_inc(moments_ready, 1)
                    dve.wait_ge(rstd_ready, 1)
                    with dve.Fori(0, NBLK) as g:
                        for t in range(TPB):
                            tile = g * TPB + t
                            dve.tensor_scalar(target[:, ds(tile * D, D)], source[:, ds(tile * D, D)],
                                              mom[:, ds(tile * 2, 1)], rstd[:, ds(tile, 1)],
                                              ALU.subtract, ALU.mult).then_inc(xn_ready, 1)
                if not R:
                    return
                dve.wait_ge(router_in, 16 * loads)
                dve.wait_ge(logits_ready, 1)
                raw = psR[:, 0:TILES * E].rearrange("p (t e) -> p t e", e=E)
                if R.logit_bias is not None:
                    own.step(dve.tensor_tensor(logits[:, :, :], raw, across(lbias[:, :], TILES), ALU.add))
                else:
                    own.step(dve.tensor_copy(logits[:, :, :], raw))
                if R.kind == "softmax":
                    own.step(dve.tensor_reduce(top[:, :], logits[:, :, :], AXX, ALU.max))
                    dve.tensor_tensor(logits[:, :, :], logits[:, :, :], wide(top[:, :], E), ALU.subtract).then_inc(shifted, 1)
                    dve.wait_ge(probs_ready, 1)
                    own.step(dve.tensor_reduce(total[:, :], probs[:, :, :], AXX, ALU.add))
                    own.step(dve.reciprocal(inverse[:, :], total[:, :]))
                    own.step(dve.tensor_tensor(probs[:, :, :], probs[:, :, :], wide(inverse[:, :], E), ALU.mult))
                else:
                    dve.tensor_copy(sel[:, :, :], logits[:, :, :]).then_inc(shifted, 1)
                    dve.wait_ge(probs_ready, 1)
                if R.select_bias is not None:
                    own.step(dve.tensor_tensor(sel[:, :, :], probs[:, :, :], across(sbias[:, :], TILES), ALU.add))
                else:
                    dve.wait_ge(shifted, 1)
                    own.step(dve.tensor_copy(sel[:, :, :], probs[:, :, :]))

                def highest(out):
                    own.step(dve.tensor_reduce(top[:, :], sel[:, :, :], AXX, ALU.max))
                    own.step(dve.tensor_tensor(hit[:, :, :], sel[:, :, :], wide(top[:, :], E), ALU.is_equal))
                    own.step(dve.tensor_tensor(hit[:, :, :], hit[:, :, :], across(k.rank[:, 0:E], TILES), ALU.mult))
                    own.step(dve.tensor_reduce(top[:, :], hit[:, :, :], AXX, ALU.max))
                    own.step(dve.tensor_tensor(out[:, :, :], hit[:, :, :], wide(top[:, :], E), ALU.is_equal))

                highest(first)
                own.step(dve.scalar_tensor_tensor(out=flat(sel), in0=flat(first), scalar=-1e30, in1=flat(sel),
                                                  op0=ALU.mult, op1=ALU.add))
                highest(second)
                own.step(dve.tensor_tensor(first[:, :, :], first[:, :, :], second[:, :, :], ALU.add))
                own.step(dve.tensor_tensor(probs[:, :, :], probs[:, :, :], first[:, :, :], ALU.mult))
                own.step(dve.tensor_reduce(total[:, :], probs[:, :, :], AXX, ALU.add))
                if R.eps:
                    own.step(dve.tensor_scalar(total[:, :], total[:, :], R.eps, None, ALU.add))
                own.step(dve.reciprocal(inverse[:, :], total[:, :]))
                own.step(dve.tensor_tensor(k.comb[:, 0:E, :].rearrange("p e t -> p t e"), probs[:, :, :],
                                           wide(inverse[:, :], E), ALU.mult))

            @block.tensor
            def _(pe):
                for g in range(NBLK):
                    if g >= 2:
                        pe.wait_ge(xnT_ready, g - 1)
                    for t in range(TPB):
                        if normalise:
                            pe.wait_ge(xn_ready, g * TPB + t + 1)
                        for j in range(KC):
                            last = pe.transpose(psT[0:KP, g % 2, j, t * P:(t + 1) * P],
                                                (k.xn if normalise else src)[:, g * TPB + t, j * KP:(j + 1) * KP], k.ident[:, :])
                    last.then_inc(transposed, 1)
                if not R:
                    return
                pe.wait_ge(router_in, 16 * loads)
                if R.hidden:
                    for g in range(NBLK):
                        pe.wait_ge(xnT_ready, g + 1)
                        if g >= 2:
                            pe.wait_ge(hidT_ready, g - 1)
                        for j in range(KC):
                            last = pe.matmul(psH[0:KP, g % 2, :], w1[:, j, :], k.xnT[:, j, g * BLOCK:(g + 1) * BLOCK],
                                             start=(j == 0), stop=(j == KC - 1))
                        last.then_inc(hidden_ready, 1)
                for t in range(TILES):
                    pe.wait_ge(hidT_ready if R.hidden else xnT_ready, t // TPB + 1)
                    for j in range(CR):
                        x = hidT[:, t * P:(t + 1) * P] if R.hidden else k.xnT[:, j, t * P:(t + 1) * P]
                        last = pe.matmul(psR[:, t * E:(t + 1) * E], x, wr[:, j, :], start=(j == 0), stop=(j == CR - 1))
                last.then_inc(logits_ready, 1)

            @block.scalar
            def _(act):
                for g in range(NBLK):
                    act.wait_ge(transposed, g + 1)
                    act.activation(k.xnT[:, :, g * BLOCK:(g + 1) * BLOCK], psT[0:KP, g % 2], ACT.Copy).then_inc(xnT_ready, 1)
                if not R:
                    return
                if R.hidden:
                    act.wait_ge(router_in, 16 * loads)
                    for g in range(NBLK):
                        act.wait_ge(hidden_ready, g + 1)
                        act.activation(hidT[:, g * BLOCK:(g + 1) * BLOCK], psH[0:KP, g % 2, :], ACT.Gelu,
                                       bias=b1[:, 0:1]).then_inc(hidT_ready, 1)
                act.wait_ge(shifted, 1)
                act.activation(flat(probs), flat(logits), ACT.Exp if R.kind == "softmax" else ACT.Sigmoid).then_inc(probs_ready, 1)


def experts_phase(nc, k, name, target, count, chunks, w_in_dram, w_out_dram, bias_dram=None, out_bias_dram=None,
                  gated=False, weighted=True):
    F = chunks * P
    FA = 2 * F if gated else F
    START = 8
    with Phase(nc, name) as phase:
        sb, ps, sem = phase.sbuf, phase.psum, phase.semaphore
        wa = sb("wa", [KP, 2, KC, FA])
        wb = sb("wb", [P, 2, chunks, D])
        ba = sb("ba", [P, 2, chunks])
        bo = sb("bo", [P, 2, D])
        weight = sb("weight", [P, 2, TILES])
        hid = sb("hid", [P, 2, chunks, BLOCK])
        silu = sb("silu", [P, 2, BLOCK])
        psA = ps("psA", [P, 4, BANK])
        psD = ps("psD", [P, 2, 2, BANK])
        loaded = [sem("loaded0"), sem("loaded1")]
        features, silu_ready, hidden, down, added, own_sem = (
            sem("features"), sem("silu_ready"), sem("hidden"), sem("down"), sem("added"), sem("own"))
        weight_ready = sem("weight_ready")
        nloads = 2 + (bias_dram is not None) + (out_bias_dram is not None)
        pairs, odd = count // 2, count % 2

        def each_expert(eng, body):
            if pairs:
                with eng.Fori(0, pairs) as it:
                    for e2 in range(2):
                        body(it * 2 + e2, e2, it + 1)
            if odd:
                body(2 * pairs, 0, pairs + 1)

        with nc.Block() as block:
            @block.sync
            def _(sp):
                def load(e, e2, turn):
                    if not (isinstance(e, int) and e < 2):
                        sp.wait_ge(down, START - 4 + e * NBLK)
                    for dst, dram in ((wa[:, e2], w_in_dram), (wb[:, e2], w_out_dram)):
                        sp.dma_start(dst, dram[ds(e, 1)].rearrange("o p a b -> p (o a) b")).then_inc(loaded[e2], 16)
                    if bias_dram is not None:
                        sp.dma_start(ba[:, e2], bias_dram[ds(e, 1)].rearrange("o p a -> p (o a)")).then_inc(loaded[e2], 16)
                    if out_bias_dram is not None:
                        sp.wait_ge(added, START - 4 + e * NBLK)
                        sp.dma_start(bo[:, e2], out_bias_dram[ds(e, 1)].rearrange("o b -> (o b)").partition_broadcast(P))\
                          .then_inc(loaded[e2], 16)
                sp.wait_ge(down, START)
                sp.wait_ge(added, START)
                each_expert(sp, load)

            @block.tensor
            def _(pe):
                pe.sem_inc(down, START)
                pe.wait_ge(hidden, START)

                def up(e, e2, b):
                    for f in range(chunks):
                        n = (e * NBLK + b) * chunks + f
                        local = b * chunks + f
                        if gated:
                            slot = 2 * ((e2 * NBLK * chunks + local) % 2)
                            pe.wait_ge(hidden, START - 1 + n)
                        else:
                            slot = (e2 * NBLK * chunks + local) % 4
                            pe.wait_ge(hidden, START - 3 + n)
                        for part in range(2 if gated else 1):
                            for j in range(KC):
                                last = pe.matmul(psA[:, slot + part, :], wa[:, e2, j, part * F + f * P:part * F + (f + 1) * P],
                                                 k.xnT[:, j, b * BLOCK:(b + 1) * BLOCK], start=(j == 0), stop=(j == KC - 1))
                        last.then_inc(features, 1)

                def go_down(e, e2, b):
                    s = e * NBLK + b
                    pe.wait_ge(hidden, START + (s + 1) * chunks)
                    pe.wait_ge(added, START - 1 + s)
                    for t in range(TPB):
                        for f in range(chunks):
                            last = pe.matmul(psD[:, b % 2, t // 2, (t % 2) * D:(t % 2 + 1) * D],
                                             hid[:, b % 2, f, t * P:(t + 1) * P], wb[:, e2, f, :],
                                             start=(f == 0), stop=(f == chunks - 1))
                    last.then_inc(down, 1)

                if pairs:
                    with pe.Fori(0, pairs) as it:
                        steps = [(it * 2 + e2, e2, b) for e2 in range(2) for b in range(NBLK)]
                        for n, st in enumerate(steps):
                            if st[2] == 0:
                                pe.wait_ge(loaded[st[1]], (it + 1) * 16 * nloads)
                            up(*st)
                            if n:
                                go_down(*steps[n - 1])
                        go_down(*steps[-1])
                if odd:
                    steps = [(2 * pairs, 0, b) for b in range(NBLK)]
                    pe.wait_ge(loaded[0], (pairs + 1) * 16 * nloads)
                    for n, st in enumerate(steps):
                        up(*st)
                        if n:
                            go_down(*steps[n - 1])
                    go_down(*steps[-1])

            @block.scalar
            def _(act):
                if not gated:
                    act.sem_inc(hidden, START)
                act.wait_ge(down, START)
                act.wait_ge(hidden, START)

                def activate(e, e2, turn):
                    if bias_dram is not None:
                        act.wait_ge(loaded[e2], turn * 16 * nloads)
                    for b in range(NBLK):
                        s = e * NBLK + b
                        if not gated:
                            act.wait_ge(down, START - 1 + s)
                        for f in range(chunks):
                            n, local = s * chunks + f, (e2 * NBLK + b) * chunks + f
                            act.wait_ge(features, n + 1)
                            if gated:
                                act.wait_ge(hidden, START - 1 + n)
                                act.activation(silu[:, local % 2, :], psA[:, 2 * (local % 2), :], ACT.Silu).then_inc(silu_ready, 1)
                            else:
                                act.activation(hid[:, b % 2, f, :], psA[:, local % 4, :], ACT.Gelu,
                                               bias=ba[:, e2, f:f + 1]).then_inc(hidden, 1)
                each_expert(act, activate)

            @block.vector
            def _(dve):
                if gated:
                    dve.sem_inc(hidden, START)
                dve.sem_inc(added, START)
                dve.wait_ge(down, START)
                dve.wait_ge(hidden, START)
                dve.wait_ge(added, START)
                own = Own(dve, own_sem)
                comb = flat(k.comb)

                def products(e, e2, b):
                    s = e * NBLK + b
                    dve.wait_ge(down, START - 1 + s)
                    for f in range(chunks):
                        n, local = s * chunks + f, (e2 * NBLK + b) * chunks + f
                        dve.wait_ge(silu_ready, n + 1)
                        dve.tensor_tensor(hid[:, b % 2, f, :], silu[:, local % 2, :], psA[:, 2 * (local % 2) + 1, :],
                                          ALU.mult).then_inc(hidden, 1)

                def add(e, e2, b):
                    s = e * NBLK + b
                    dve.wait_ge(down, START + s + 1)
                    dve.wait_ge(added, START + s)
                    if out_bias_dram is not None:
                        for t in range(TPB):
                            tile = b * TPB + t
                            if weighted:
                                last = dve.scalar_tensor_tensor(out=target[:, tile, :], in0=bo[:, e2, :], scalar=weight[:, e2, tile:tile + 1],
                                                                in1=target[:, tile, :], op0=ALU.mult, op1=ALU.add)
                            else:
                                last = dve.tensor_tensor(target[:, tile, :], bo[:, e2, :], target[:, tile, :], ALU.add)
                        own.step(last)
                    for t in range(TPB):
                        tile = b * TPB + t
                        part = psD[:, b % 2, t // 2, (t % 2) * D:(t % 2 + 1) * D]
                        if weighted:
                            last = dve.scalar_tensor_tensor(out=target[:, tile, :], in0=part, scalar=weight[:, e2, tile:tile + 1],
                                                            in1=target[:, tile, :], op0=ALU.mult, op1=ALU.add)
                        else:
                            last = dve.tensor_tensor(target[:, tile, :], part, target[:, tile, :], ALU.add)
                    last.then_inc(added, 1)

                def run(steps, turns):
                    for e, e2, b in steps:
                        if b == 0 and weighted:
                            own.step(dve.tensor_copy(weight[:, e2, :], comb[:, ds(e * TILES, TILES)]))
                    for n, (e, e2, b) in enumerate(steps):
                        if gated:
                            products(e, e2, b)
                        if n:
                            add_step(steps[n - 1], turns)
                    add_step(steps[-1], turns)

                def add_step(step, turns):
                    if step[2] == 0 and out_bias_dram is not None:
                        dve.wait_ge(loaded[step[1]], turns * 16 * nloads)
                    add(*step)

                extra = NBLK * (out_bias_dram is not None) + int(weighted)
                if pairs:
                    with dve.Fori(0, pairs) as it:
                        own.enter(it, 2 * extra)
                        dve.wait_ge(added, START + it * 2 * NBLK)
                        run([(it * 2 + e2, e2, b) for e2 in range(2) for b in range(NBLK)], it + 1)
                    own.leave(pairs)
                if odd:
                    dve.wait_ge(added, START + 2 * pairs * NBLK)
                    run([(2 * pairs, 0, b) for b in range(NBLK)], pairs + 1)


HEADS0, HD0 = 6, 32
SCALE0 = HD0 ** -0.5


def values_program(pe, psV, w, out_ready, freed, tiles=TILES, xnT=None, n=D):
    for t in range(0, tiles, 2):
        if t >= 4:
            pe.wait_ge(freed, t // 2 - 1)
        for u in (t, t + 1):
            for j in range(KC):
                last = pe.matmul(psV[:, (t // 2) % 2, (u - t) * n:(u - t + 1) * n], xnT[:, j, u * P:(u + 1) * P], w[:, j, :],
                                 start=(j == 0), stop=(j == KC - 1))
        last.then_inc(out_ready, 1)


def attention0_phase(nc, k, wqk_dram, wv_dram, wo_dram, anchor_w, anchors, lam):
    with Phase(nc, "a0_") as phase:
        sb, ps, sem = phase.sbuf, phase.psum, phase.semaphore
        wv = sb("wv", [KP, KC, D])
        values = sb("values", [P, TILES, D])
        aw, an, lm = sb("aw", [HD0, HEADS0, 6]), sb("an", [HD0, HEADS0, 6]), sb("lm", [HD0, HEADS0])
        anchor, head_anchor = sb("anchor", [HD0, HEADS0]), sb("head_anchor", [HD0, 1])
        wqk = sb("wqk", [KP, KC, 2, HD0])
        wo = sb("wo", [HD0, D])
        qk = sb("qk", [HD0, 2, SEQ])
        vh = sb("vh", [P, TPS, HD0])
        shift = sb("shift", [P, TPS])
        top, peak, bias = sb("top", [P, TPS]), sb("peak", [P, TPS]), sb("bias", [P, TPS])
        probs = sb("probs", [P, 2, SEQ])
        probsT = sb("probsT", [P, 2, TPS, BLOCK])
        total, inverse = sb("total", [P, TPS]), sb("inverse", [P, TPS])
        outT = sb("outT", [HD0, BLOCK])
        psS = ps("psS", [P, 4, BANK])
        psT = ps("psT", [P, 2, BANK])
        psO = ps("psO", [P, BANK])
        psW = ps("psW", [P, BANK])
        names = ("v_in anchor_in wqk_in wo_in v_ready v_copied anchor_own anchor_ready own qk_ready qk_copied shift_ready "
                 "shift_copied vh_ready scores_ready bias_ready probs_ready turned turned_act turned_dve out_ready out_copied "
                 "w_ready w_added").split()
        s = {n: sem(n) for n in names}
        UPH, HPH = 2 * TPS, 4

        with nc.Block() as block:
            @block.sync
            def _(sp):
                sp.dma_start(wv[:, :, :], wv_dram).then_inc(s["v_in"], 16)
                sp.dma_start(aw[:, :, :], anchor_w).then_inc(s["anchor_in"], 16)
                sp.dma_start(an[:, :, :], anchors.rearrange("h e -> (h e)").partition_broadcast(HD0)
                             .rearrange("p (h e) -> p h e", e=6)).then_inc(s["anchor_in"], 16)
                sp.dma_start(lm[:, :], lam.partition_broadcast(HD0)).then_inc(s["anchor_in"], 16)
                with sp.Fori(0, HEADS0) as h:
                    sp.wait_ge(s["qk_ready"], h * 2)
                    sp.dma_start(wqk[:, :, :, :], wqk_dram[ds(h, 1)].rearrange("o p a b c -> p (o a) b c")).then_inc(s["wqk_in"], 16)
                    sp.wait_ge(s["w_ready"], h * 2 * HPH)
                    sp.dma_start(wo[:, :], wo_dram[ds(h, 1)].rearrange("o p d -> (o p) d")).then_inc(s["wo_in"], 16)

            @block.tensor
            def _(pe):
                pe.wait_ge(s["v_in"], 16)
                values_program(pe, psT, wv, s["v_ready"], s["v_copied"], xnT=k.xnT)
                pe.wait_ge(s["v_copied"], TILES // 2)
                with pe.Fori(0, HEADS0) as h:
                    pe.wait_ge(s["wqk_in"], h * 16 + 16)
                    for b in range(BATCH):
                        u0, half0 = h * UPH + b * TPS, h * HPH + b * 2
                        pe.wait_ge(s["probs_ready"], u0)
                        for part in range(2):
                            for blk in range(2):
                                for j in range(KC):
                                    last = pe.matmul(psS[0:HD0, part * 2 + blk, :], wqk[:, j, part, :],
                                                     k.xnT[:, j, b * SEQ + blk * BLOCK:b * SEQ + (blk + 1) * BLOCK],
                                                     start=(j == 0), stop=(j == KC - 1))
                        last.then_inc(s["qk_ready"], 1)
                        pe.wait_ge(s["qk_copied"], h * 2 + b + 1)
                        pe.wait_ge(s["w_added"], h * 2 * HPH + b * 4)
                        pe.wait_ge(s["anchor_ready"], h + 2)
                        for t in range(TPS):
                            last = pe.matmul(psW[:, t:t + 1], qk[:, 0, t * P:(t + 1) * P], head_anchor[:, :], start=True, stop=True)
                        last.then_inc(s["shift_ready"], 1)

                        def turn(t):
                            pe.wait_ge(s["probs_ready"], u0 + t + 1)
                            pe.wait_ge(s["turned_act"], u0 + t)
                            pe.wait_ge(s["turned_dve"], u0 + t)
                            for kt in range(TPS):
                                last = pe.transpose(psT[:, kt // 4, (kt % 4) * P:(kt % 4 + 1) * P],
                                                    probs[:, t % 2, kt * P:(kt + 1) * P], k.ident[:, :])
                            last.then_inc(s["turned"], 1)

                        def weigh(half):
                            pe.wait_ge(s["vh_ready"], h * 2 + b + 1)
                            pe.wait_ge(s["turned_act"], u0 + half * 4 + 4)
                            pe.wait_ge(s["turned_dve"], u0 + half * 4 + 4)
                            pe.wait_ge(s["w_added"], h * 2 * HPH + b * 4 + half * 2)
                            for kt in range(TPS):
                                last = pe.matmul(psO[0:HD0, :], vh[:, kt, :], probsT[:, half, kt, :],
                                                 start=(kt == 0), stop=(kt == TPS - 1))
                            last.then_inc(s["out_ready"], 1)

                        def project(half):
                            pe.wait_ge(s["out_copied"], half0 + half + 1)
                            if half == 0 and b == 0:
                                pe.wait_ge(s["wo_in"], h * 16 + 16)
                            pe.wait_ge(s["shift_copied"], h * 2 + b + 1)
                            for pair, bank in enumerate((psW, psO)):
                                for t in range(2):
                                    col = (pair * 2 + t) * P
                                    last = pe.matmul(bank[:, t * D:(t + 1) * D], outT[:, col:col + P], wo[:, :], start=True, stop=True)
                                last.then_inc(s["w_ready"], 1)

                        for t in range(TPS):
                            if t >= 2:
                                pe.wait_ge(s["probs_ready"], u0 + t - 1)
                            for blk in range(2):
                                last = pe.matmul(psS[:, (t % 2) * 2 + blk, :], qk[:, 0, t * P:(t + 1) * P],
                                                 qk[:, 1, blk * BLOCK:(blk + 1) * BLOCK], start=True, stop=True)
                            last.then_inc(s["scores_ready"], 1)
                            if t:
                                turn(t - 1)
                            if t == 5:
                                weigh(0)
                            if t == 6:
                                project(0)
                        turn(TPS - 1)
                        weigh(1)
                        project(1)

            @block.scalar
            def _(act):
                for n in range(TILES // 2):
                    act.wait_ge(s["v_ready"], n + 1)
                    act.activation(values[:, 2 * n:2 * n + 2, :].rearrange("p a b -> p (a b)"), psT[:, n % 2, 0:2 * D],
                                   ACT.Copy).then_inc(s["v_copied"], 1)
                with act.Fori(0, HEADS0) as h:
                    for b in range(BATCH):
                        u0 = h * UPH + b * TPS
                        act.wait_ge(s["qk_ready"], h * 2 + b + 1)
                        for part in range(2):
                            last = act.activation(qk[:, part, :], psS[0:HD0, 2 * part:2 * part + 2, :].rearrange("p a b -> p (a b)"), ACT.Copy)
                        last.then_inc(s["qk_copied"], 1)

                        def copy_turned(t):
                            act.wait_ge(s["turned"], u0 + t + 1)
                            act.activation(probsT[:, t // 4, 0:4, (t % 4) * P:(t % 4 + 1) * P],
                                           psT[:, 0, :].rearrange("p (a b) -> p a b", b=P), ACT.Copy).then_inc(s["turned_act"], 1)

                        def copy_out(half):
                            act.wait_ge(s["out_ready"], h * HPH + b * 2 + half + 1)
                            act.wait_ge(s["w_ready"], h * 2 * HPH + b * 4 + half * 2)
                            act.activation(outT[:, :], psO[0:HD0, :], ACT.Copy).then_inc(s["out_copied"], 1)

                        for t in range(TPS):
                            act.wait_ge(s["bias_ready"], u0 + t + 1)
                            if t < 2:
                                act.wait_ge(s["turned"], u0)
                            else:
                                act.wait_ge(s["turned"], u0 + t - 1)
                            act.activation(probs[:, t % 2, :], psS[:, (t % 2) * 2:(t % 2) * 2 + 2, :].rearrange("p a b -> p (a b)"), ACT.Exp,
                                           bias=bias[:, t:t + 1], scale=SCALE0, accum_out=total[:, t:t + 1]).then_inc(s["probs_ready"], 1)
                            if t:
                                copy_turned(t - 1)
                            if t == 5:
                                copy_out(0)
                        copy_turned(TPS - 1)
                        copy_out(1)

            @block.vector
            def _(dve):
                own = Own(dve, s["own"])
                dve.wait_ge(s["anchor_in"], 48)
                own.step(dve.tensor_tensor(aw[:, :, :], aw[:, :, :], an[:, :, :], ALU.mult))
                own.step(dve.tensor_reduce(anchor[:, :], aw[:, :, :], AXX, ALU.add))
                dve.tensor_tensor(anchor[:, :], anchor[:, :], lm[:, :], ALU.mult).then_inc(s["anchor_ready"], 1)
                dve.wait_ge(s["v_copied"], TILES // 2)
                with dve.Fori(0, HEADS0) as h:
                    own.enter(h, 2 * (2 * TPS + 2))
                    dve.wait_ge(s["anchor_ready"], h + 1)
                    dve.wait_ge(s["shift_ready"], h * 2)
                    dve.tensor_copy(head_anchor[:, :], anchor[:, ds(h, 1)]).then_inc(s["anchor_ready"], 1)
                    for b in range(BATCH):
                        u0 = h * UPH + b * TPS
                        dve.wait_ge(s["w_added"], h * 2 * HPH + b * 4)
                        dve.wait_ge(s["out_ready"], h * HPH + b * 2)
                        dve.tensor_copy(vh[:, :, :], values[:, b * TPS:(b + 1) * TPS, ds(h * HD0, HD0)]).then_inc(s["vh_ready"], 1)
                        dve.wait_ge(s["shift_ready"], h * 2 + b + 1)
                        dve.wait_ge(s["bias_ready"], u0)
                        dve.tensor_copy(shift[:, :], psW[:, 0:TPS]).then_inc(s["shift_copied"], 1)
                        dve.wait_ge(s["shift_copied"], h * 2 + b + 1)

                        def copy_turned(t):
                            dve.wait_ge(s["turned"], u0 + t + 1)
                            dve.tensor_copy(probsT[:, t // 4, 4:8, (t % 4) * P:(t % 4 + 1) * P],
                                            psT[:, 1, :].rearrange("p (a b) -> p a b", b=P)).then_inc(s["turned_dve"], 1)

                        def add(half):
                            r = slice(half * 4, half * 4 + 4)
                            own.step(dve.reciprocal(inverse[:, r], total[:, r]))
                            for pair, bank in enumerate((psW, psO)):
                                dve.wait_ge(s["w_ready"], h * 2 * HPH + b * 4 + half * 2 + pair + 1)
                                for t in range(2):
                                    q = half * 4 + pair * 2 + t
                                    last = dve.scalar_tensor_tensor(out=k.h[:, b * TPS + q, :], in0=bank[:, t * D:(t + 1) * D],
                                                                    scalar=inverse[:, q:q + 1], in1=k.h[:, b * TPS + q, :],
                                                                    op0=ALU.mult, op1=ALU.add)
                                last.then_inc(s["w_added"], 1)

                        for t in range(TPS):
                            dve.wait_ge(s["scores_ready"], u0 + t + 1)
                            dve.wait_ge(s["probs_ready"], u0)
                            own.step(dve.tensor_reduce(top[:, t:t + 1], psS[:, (t % 2) * 2:(t % 2) * 2 + 2, :].rearrange("p a b -> p (a b)"),
                                                       AXX, ALU.max))
                            own.step(dve.scalar_tensor_tensor(out=peak[:, t:t + 1], in0=top[:, t:t + 1], scalar=SCALE0,
                                                              in1=shift[:, t:t + 1], op0=ALU.mult, op1=ALU.add))
                            dve.tensor_tensor(bias[:, t:t + 1], shift[:, t:t + 1], peak[:, t:t + 1], ALU.subtract).then_inc(s["bias_ready"], 1)
                            if t:
                                copy_turned(t - 1)
                            if t == 6:
                                add(0)
                        copy_turned(TPS - 1)
                        add(1)
                own.leave(HEADS0)


def attention1_phase(nc, k, w_dram, qk_bias, v_bias, decay_dram):
    PAD = 3 * P
    with Phase(nc, "a1_") as phase:
        sb, ps, sem = phase.sbuf, phase.psum, phase.semaphore
        w = sb("w", [KP, KC, 3, D])
        qkb, vb = sb("qkb", [KP, 2, KC]), sb("vb", [P, D])
        decay = sb("decay", [P, PAD + SEQ])
        values = sb("values", [P, TILES, D])
        qkT = sb("qkT", [KP, 2, KC, SEQ])
        scores = sb("scores", [P, 2, TPS, BLOCK])
        psQ, psS, psO = ps("psQ", [P, 2, BANK]), ps("psS", [P, 2, BANK]), ps("psO", [P, 2, 2, BANK])
        names = "loaded v_ready v_copied qk_ready qk_copied scores_ready scores_copied out_ready out_added".split()
        s = {n: sem(n) for n in names}
        blocks = SEQ // BLOCK
        keys = [(sb_ + 1) * TPB for sb_ in range(blocks)]
        first = [sum(keys[:n]) for n in range(blocks)]
        SPB, QPB = sum(keys), 2 * KC * blocks

        with nc.Block() as block:
            @block.sync
            def _(sp):
                sp.dma_start(w[:, :, :, :], w_dram).then_inc(s["loaded"], 16)
                sp.dma_start(qkb[:, :, :], qk_bias).then_inc(s["loaded"], 16)
                sp.dma_start(vb[:, :], v_bias.partition_broadcast(P)).then_inc(s["loaded"], 16)
                sp.dma_start(decay[:, :], decay_dram).then_inc(s["loaded"], 16)

            @block.tensor
            def _(pe):
                pe.wait_ge(s["loaded"], 64)
                values_program(pe, psQ, w[:, :, 2, :], s["v_ready"], s["v_copied"], xnT=k.xnT)
                pe.wait_ge(s["v_copied"], TILES // 2)
                xnT = k.xnT
                with pe.Fori(0, BATCH) as b:
                    for n in range(QPB):
                        part, m, blk = n // (KC * blocks), n // blocks % KC, n % blocks
                        pe.wait_ge(s["qk_copied"], b * QPB + max(n - 1, 0))
                        for j in range(KC):
                            last = pe.matmul(psQ[0:KP, n % 2, :], w[:, j, part, m * KP:(m + 1) * KP],
                                             xnT[:, j, ds(b * SEQ + blk * BLOCK, BLOCK)], start=(j == 0), stop=(j == KC - 1))
                        last.then_inc(s["qk_ready"], 1)
                    pe.wait_ge(s["qk_copied"], b * QPB + QPB)

                    def weigh(q):
                        pe.wait_ge(s["scores_copied"], b * SPB + first[q] + keys[q])
                        pe.wait_ge(s["out_added"], b * blocks + max(q - 1, 0))
                        for t in range(TPB):
                            seen = q * TPB + t + 1
                            for kt in range(seen):
                                last = pe.matmul(psO[:, q % 2, t // 2, (t % 2) * D:(t % 2 + 1) * D], scores[:, q % 2, kt, t * P:(t + 1) * P],
                                                 flat(values)[:, ds((b * TPS + kt) * D, D)], start=(kt == 0), stop=(kt == seen - 1))
                        last.then_inc(s["out_ready"], 1)

                    for q in range(blocks):
                        for kt in range(keys[q]):
                            n = first[q] + kt
                            pe.wait_ge(s["scores_copied"], b * SPB + max(n - 1, 0))
                            for j in range(KC):
                                last = pe.matmul(psS[:, n % 2, :], qkT[:, 1, j, kt * P:(kt + 1) * P],
                                                 qkT[:, 0, j, q * BLOCK:(q + 1) * BLOCK], start=(j == 0), stop=(j == KC - 1))
                            last.then_inc(s["scores_ready"], 1)
                        if q:
                            weigh(q - 1)
                    weigh(blocks - 1)

            @block.scalar
            def _(act):
                act.wait_ge(s["loaded"], 64)
                with act.Fori(0, BATCH) as b:
                    for n in range(QPB):
                        part, m, blk = n // (KC * blocks), n // blocks % KC, n % blocks
                        act.wait_ge(s["qk_ready"], b * QPB + n + 1)
                        act.activation(qkT[:, part, m, blk * BLOCK:(blk + 1) * BLOCK], psQ[0:KP, n % 2, :], ACT.Identity,
                                       bias=qkb[:, part, m:m + 1]).then_inc(s["qk_copied"], 1)

            @block.vector
            def _(dve):
                dve.wait_ge(s["loaded"], 64)
                for n in range(TILES // 2):
                    dve.wait_ge(s["v_ready"], n + 1)
                    dve.tensor_tensor(values[:, 2 * n:2 * n + 2, :], psQ[:, n % 2, 0:2 * D].rearrange("p (a b) -> p a b", b=D),
                                      across(vb[:, :], 2), ALU.add).then_inc(s["v_copied"], 1)
                h = flat(k.h)
                with dve.Fori(0, BATCH) as b:
                    def add(q):
                        dve.wait_ge(s["out_ready"], b * blocks + q + 1)
                        for t in range(TPB):
                            at = ds((b * TPS + q * TPB + t) * D, D)
                            last = dve.tensor_tensor(h[:, at], psO[:, q % 2, t // 2, (t % 2) * D:(t % 2 + 1) * D], h[:, at], ALU.add)
                        last.then_inc(s["out_added"], 1)

                    for q in range(blocks):
                        dve.wait_ge(s["out_ready"], b * blocks + max(q - 1, 0))
                        for kt in range(keys[q]):
                            n = first[q] + kt
                            dve.wait_ge(s["scores_ready"], b * SPB + n + 1)
                            at = PAD + q * BLOCK - kt * P
                            dve.tensor_tensor(scores[:, q % 2, kt, :], psS[:, n % 2, :], decay[:, at:at + BLOCK],
                                              ALU.mult).then_inc(s["scores_copied"], 1)
                        if q:
                            add(q - 1)
                    add(blocks - 1)


CENTRES, VC = 12, 16
NV = D + CENTRES


def attention2_phase(nc, k, w_dram, v_bias):
    with Phase(nc, "a2_") as phase:
        sb, ps, sem = phase.sbuf, phase.psum, phase.semaphore
        w, vb = sb("w", [KP, KC, NV]), sb("vb", [P, D])
        junk, norms = sb("junk", [P, D]), sb("norms", [P, TILES])
        raw = sb("raw", [P, TILES, CENTRES])
        top, peak = sb("top", [P, BATCH, CENTRES]), sb("peak", [P, BATCH, CENTRES])
        factor = sb("factor", [P, TILES, CENTRES])
        values = sb("values", [P, TILES, NV])
        xT = sb("xT", [KP, KC, SEQ])
        kern = sb("kern", [P, 2, TPS, BLOCK])
        inverse, chosen = sb("inverse", [P, TPB, CENTRES]), sb("chosen", [P, TPB, D])
        psE, psO = ps("psE", [P, 4, BANK]), ps("psO", [P, 2, 2, BANK])
        names = ("loaded norms_own norms_ready v_ready v_copied own tops_ready peak_ready shifted factor_ready values_ready xT_ready "
                 "products_ready kern_ready out_ready out_used").split()
        s = {n: sem(n) for n in names}
        blocks = SEQ // BLOCK
        UPB = blocks * TPS

        with nc.Block() as block:
            @block.sync
            def _(sp):
                sp.dma_start(w[:, :, :], w_dram).then_inc(s["loaded"], 16)
                sp.dma_start(vb[:, :], v_bias.partition_broadcast(P)).then_inc(s["loaded"], 16)

            @block.tensor
            def _(pe):
                pe.wait_ge(s["loaded"], 32)
                values_program(pe, psE, w, s["v_ready"], s["v_copied"], xnT=k.xnT, n=NV)
                pe.wait_ge(s["v_copied"], TILES // 2)
                with pe.Fori(0, BATCH) as b:
                    pe.wait_ge(s["xT_ready"], b + 1)

                    def weigh(q):
                        pe.wait_ge(s["values_ready"], 1)
                        pe.wait_ge(s["kern_ready"], b * UPB + (q + 1) * TPS)
                        pe.wait_ge(s["out_used"], b * blocks + max(q - 1, 0))
                        for t in range(TPB):
                            for m in range(TPS):
                                last = pe.matmul(psO[:, q % 2, t // 2, (t % 2) * NV:(t % 2 + 1) * NV], kern[:, q % 2, m, t * P:(t + 1) * P],
                                                 flat(values)[:, ds((b * TPS + m) * NV, NV)], start=(m == 0), stop=(m == TPS - 1))
                        last.then_inc(s["out_ready"], 1)

                    for q in range(blocks):
                        for m in range(TPS):
                            n = q * TPS + m
                            pe.wait_ge(s["kern_ready"], b * UPB + max(n - 3, 0))
                            for j in range(KC):
                                last = pe.matmul(psE[:, n % 4, :], xT[:, j, m * P:(m + 1) * P], xT[:, j, q * BLOCK:(q + 1) * BLOCK],
                                                 start=(j == 0), stop=(j == KC - 1))
                            last.then_inc(s["products_ready"], 1)
                        if q:
                            weigh(q - 1)
                    weigh(blocks - 1)

            @block.scalar
            def _(act):
                for t in range(TILES):
                    if t:
                        act.wait_ge(s["norms_own"], t)
                    act.activation(junk[:, :], k.xn[:, t, :], ACT.Square, accum_out=norms[:, t:t + 1]).then_inc(s["norms_own"], 1)
                act.wait_ge(s["shifted"], BATCH)
                act.activation(flat(factor), flat(raw), ACT.Exp, scale=1.0 / D).then_inc(s["factor_ready"], 1)
                with act.Fori(0, BATCH) as b:
                    for n in range(UPB):
                        q, m = n // TPS, n % TPS
                        act.wait_ge(s["products_ready"], b * UPB + n + 1)
                        if m == 0:
                            act.wait_ge(s["out_ready"], b * blocks + max(q - 1, 0))
                        act.activation(kern[:, q % 2, m, :], psE[:, n % 4, :], ACT.Exp, scale=2.0 / D).then_inc(s["kern_ready"], 1)

            @block.gpsimd
            def _(pool):
                pool.wait_ge(s["tops_ready"], BATCH)
                pool.partition_all_reduce(flat(peak), flat(top), P, bass.bass_isa.ReduceOp.max).then_inc(s["peak_ready"], 1)

            @block.vector
            def _(dve):
                own = Own(dve, s["own"])
                dve.wait_ge(s["loaded"], 32)
                for n in range(TILES // 2):
                    t = slice(2 * n, 2 * n + 2)
                    src = psE[:, n % 2, 0:2 * NV].rearrange("p (a b) -> p a b", b=NV)
                    dve.wait_ge(s["v_ready"], n + 1)
                    dve.wait_ge(s["norms_own"], 2 * n + 2)
                    dve.tensor_tensor(values[:, t, 0:D], src[:, :, 0:D], across(vb[:, :], 2), ALU.add)
                    dve.scalar_tensor_tensor(out=raw[:, t, :], in0=src[:, :, D:NV], scalar=2.0, in1=wide(norms[:, t], CENTRES),
                                             op0=ALU.mult, op1=ALU.subtract).then_inc(s["v_copied"], 1)
                dve.wait_ge(s["v_copied"], TILES // 2)
                for b in range(BATCH):
                    dve.tensor_reduce(top[:, b, :], raw[:, b * TPS:(b + 1) * TPS, :].rearrange("p t c -> p c t"), AXX, ALU.max)\
                       .then_inc(s["tops_ready"], 1)
                dve.wait_ge(s["peak_ready"], 1)
                for b in range(BATCH):
                    t = slice(b * TPS, (b + 1) * TPS)
                    dve.tensor_tensor(raw[:, t, :], raw[:, t, :], across(peak[:, b, :], TPS), ALU.subtract).then_inc(s["shifted"], 1)
                dve.wait_ge(s["factor_ready"], 1)
                for t in range(TILES):
                    v = values[:, t, 0:D].rearrange("p (c d) -> p c d", d=VC)
                    dve.tensor_tensor(v, v, wide(factor[:, t, :], VC), ALU.mult)
                dve.tensor_copy(values[:, :, D:NV], factor[:, :, :]).then_inc(s["values_ready"], 1)
                acc, xn = flat(k.acc), flat(k.xn)
                with dve.Fori(0, BATCH) as b:
                    own.enter(b, 2 * blocks)
                    dve.wait_ge(s["products_ready"], b * UPB)
                    dve.tensor_copy(xT[:, :, :], k.xnT[:, :, ds(b * SEQ, SEQ)]).then_inc(s["xT_ready"], 1)
                    for q in range(blocks):
                        dve.wait_ge(s["out_ready"], b * blocks + q + 1)
                        dve.wait_ge(s["out_used"], b * blocks + q)
                        for t in range(TPB):
                            part = psO[:, q % 2, t // 2, (t % 2) * NV:(t % 2 + 1) * NV]
                            last = dve.reciprocal(inverse[:, t, :], part[:, D:NV])
                        own.step(last)
                        for t in range(TPB):
                            part = psO[:, q % 2, t // 2, (t % 2) * NV:(t % 2 + 1) * NV]
                            last = dve.tensor_tensor(chosen[:, t, :].rearrange("p (c d) -> p c d", d=VC), part[:, 0:D].rearrange("p (c d) -> p c d", d=VC),
                                                     wide(inverse[:, t, :], VC), ALU.mult)
                        own.step(last)
                        at = ds((b * TPS + q * TPB) * D, TPB * D)
                        dve.tensor_tensor(acc[:, at], flat(chosen), xn[:, at], ALU.add).then_inc(s["out_used"], 1)
                own.leave(BATCH)


def affine_norm_phase(nc, k, name, src, eps, gamma_dram, beta_dram):
    with Phase(nc, name) as phase:
        sb, ps, sem = phase.sbuf, phase.psum, phase.semaphore
        stats, moments = sb("stats", [P, TILES, 6]), sb("moments", [P, TILES, 2])
        rstd0, rstd = sb("rstd0", [P, TILES]), sb("rstd", [P, TILES])
        gamma, beta = sb("gamma", [P, D]), sb("beta", [P, D])
        y = sb("y", [P, TPB, D])
        loaded, own_sem, stats_ready, eps_added, rstd_ready = (
            sem("loaded"), sem("own"), sem("stats_ready"), sem("eps_added"), sem("rstd_ready"))
        moments_ready = sem("moments_ready")

        with nc.Block() as block:
            @block.sync
            def _(sp):
                sp.dma_start(gamma[:, :], gamma_dram.partition_broadcast(P)).then_inc(loaded, 16)
                sp.dma_start(beta[:, :], beta_dram.partition_broadcast(P)).then_inc(loaded, 16)

            @block.gpsimd
            def _(pool):
                pool.wait_ge(moments_ready, 1)
                pool.tensor_scalar(rstd0[:, :], moments[:, :, 1], eps, None, ALU.add).then_inc(eps_added, 1)
                pool.wait_ge(eps_added, 1)
                pool.tensor_tensor(rstd[:, :], rstd0[:, :], k.minus_half[:, :], ALU.pow).then_inc(rstd_ready, 1)

            @block.vector
            def _(dve):
                own = Own(dve, own_sem)
                source, mom, h = flat(src), flat(moments), flat(k.h)
                with dve.Fori(0, NBLK) as g:
                    for t in range(TPB):
                        tile = g * TPB + t
                        last = dve.bn_stats(flat(stats)[:, ds(tile * 6, 6)], source[:, ds(tile * D, D)])
                    last.then_inc(stats_ready, 1)
                dve.wait_ge(stats_ready, NBLK)
                for t in range(TILES):
                    last = dve.bn_aggr(moments[:, t, :], stats[:, t, :])
                last.then_inc(moments_ready, 1)
                dve.wait_ge(rstd_ready, 1)
                dve.wait_ge(loaded, 32)
                with dve.Fori(0, NBLK) as g:
                    own.enter(g, 4)
                    for t in range(TPB):
                        tile = g * TPB + t
                        last = dve.tensor_scalar(y[:, t, :], source[:, ds(tile * D, D)], mom[:, ds(tile * 2, 1)], rstd[:, ds(tile, 1)],
                                                 ALU.subtract, ALU.mult)
                    own.step(last)
                    own.step(dve.tensor_tensor(y[:, :, :], y[:, :, :], across(gamma[:, :], TPB), ALU.mult))
                    own.step(dve.tensor_tensor(y[:, :, :], y[:, :, :], across(beta[:, :], TPB), ALU.add))
                    at = ds(g * TPB * D, TPB * D)
                    own.step(dve.tensor_tensor(h[:, at], h[:, at], flat(y), ALU.add))
                own.leave(NBLK)


HEADS3, HD3 = 12, 16
QMAX, QMIN = 127.0, -128.0
ROUND = 12582912.0
V_SCALE = 2.0 ** 60
P_SCALE = 2.0 ** 111
EXP_C0, EXP_C1 = 0.35815147, 0.96963238


def attention3_setup(nc, k, q, a):
    with Phase(nc, "s3_") as phase:
        sb, ps, sem = phase.sbuf, phase.psum, phase.semaphore
        w, scale = sb("w", [KP, KC, 3 * D]), sb("scale", [KP, 3 * D])
        inverse = sb("inverse", [KP, 3 * D])
        vscale, vf = sb("vscale", [P, D]), sb("vf", [P, D])
        qkscale = sb("qkscale", [HD3, HEADS3, 2])
        real = sb("real", [P, 2, D])
        whole = sb("whole", [P, 2, D], I16)
        tmp = sb("tmp", [P, 4])
        psV = ps("psV", [P, 2, BANK])
        loaded, own_sem, w_ready, v_ready, v_copied = (
            sem("loaded"), sem("own"), sem("w_ready"), sem("v_ready"), sem("v_copied"))

        with nc.Block() as block:
            @block.sync
            def _(sp):
                sp.dma_start(w[:, :, :], a["a3_w"]).then_inc(loaded, 16)
                sp.dma_start(scale[:, :], a["a3_scale"].partition_broadcast(KP)).then_inc(loaded, 16)
                sp.dma_start(vscale[:, :], a["a3_scale"][2 * D:3 * D].partition_broadcast(P)).then_inc(loaded, 16)
                sp.dma_start(qkscale[:, :, :], a["a3_qkscale"]).then_inc(loaded, 16)
                for n, s in enumerate(("a3_s_act1", "a3_s_attn", "a3_s_act2", "a3_s_act3")):
                    sp.dma_start(q.s[:, n:n + 1], a[s].partition_broadcast(P)).then_inc(loaded, 16)

            @block.vector
            def _(dve):
                own = Own(dve, own_sem)
                dve.wait_ge(loaded, 8 * 16)
                own.step(dve.reciprocal(inverse[:, :], scale[:, :]))
                own.step(dve.tensor_tensor(w[:, :, :], w[:, :, :], across(inverse[:, :], KC), ALU.mult))
                own.step(dve.tensor_scalar(flat(w), flat(w), QMAX, QMIN, ALU.min, ALU.max))
                dve.tensor_scalar(flat(q.w), flat(w), ROUND, ROUND, ALU.add, ALU.subtract).then_inc(w_ready, 1)
                own.step(dve.reciprocal(q.inv[:, :], q.s[:, :]))
                is1, isa, is2 = q.inv[:, 0:1], q.inv[:, 1:2], q.inv[:, 2:3]
                dve.tensor_scalar(vf[:, :], vscale[:, :], is1, None, ALU.mult)
                own.step(dve.memset(q.fqk[:, :, :], 0.0))
                dve.tensor_scalar(flat(q.fqk)[:, 0:HEADS3 * 2], flat(qkscale), q.inv[0:HD3, 0:1], None, ALU.mult)
                own.step(dve.tensor_scalar(q.fa[:, :], q.s[:, 0:1], q.s[:, 0:1], HD3 ** -0.5, ALU.mult, ALU.mult))
                own.step(dve.tensor_scalar(q.fa[:, :], q.fa[:, :], isa, None, ALU.mult))
                own.step(dve.tensor_scalar(q.fo[:, :], q.s[:, 0:1], is2, P_SCALE / V_SCALE, ALU.mult, ALU.mult))

                def floor(out, y, t):
                    own.step(dve.tensor_scalar(out, y, ROUND, ROUND, ALU.add, ALU.subtract))
                    own.step(dve.tensor_tensor(t, out, y, ALU.is_gt))
                    own.step(dve.tensor_tensor(out, out, t, ALU.subtract))

                y, t = tmp[:, 0:1], tmp[:, 1:2]
                own.step(dve.tensor_scalar(y, isa, -0.6931, None, ALU.mult))
                floor(q.x0[:, :], y, t)
                own.step(dve.tensor_scalar(y, isa, EXP_C1 / EXP_C0, None, ALU.mult))
                floor(q.half_b[:, :], y, t)
                own.step(dve.tensor_scalar(y, isa, isa, 1.0 / EXP_C0, ALU.mult, ALU.mult))
                floor(q.c[:, :], y, t)
                own.step(dve.tensor_scalar(t, q.c[:, :], 0.0, None, ALU.is_gt))
                own.step(dve.tensor_scalar(q.fo[:, :], q.fo[:, :], t, None, ALU.mult))
                own.step(dve.tensor_scalar(q.half_b[:, :], q.half_b[:, :], 0.5, None, ALU.mult))
                own.step(dve.tensor_scalar(y, q.half_b[:, :], q.half_b[:, :], -1.0, ALU.mult, ALU.mult))
                own.step(dve.tensor_scalar(q.c[:, :], q.c[:, :], 1.0, y, ALU.max, ALU.add))
                dve.tensor_scalar(q.low[:, :], q.x0[:, :], 30.0, None, ALU.mult)
                own.step(dve.reciprocal(q.inv_x0[:, :], q.x0[:, :]))
                own.step(dve.tensor_scalar(q.minus_inv_x0[:, :], q.inv_x0[:, :], -1.0, None, ALU.mult))
                own.step(dve.tensor_scalar(y, q.x0[:, :], -1.0, None, ALU.mult))
                own.step(dve.tensor_scalar(q.x0_ident[:, :], k.ident[:, :], y, None, ALU.mult))
                for n in range(TILES // 2):
                    dve.wait_ge(v_ready, n + 1)
                    own.step(dve.tensor_tensor(real[:, :, :], psV[:, n % 2, 0:2 * D].rearrange("p (a b) -> p a b", b=D),
                                               across(vf[:, :], 2), ALU.mult))
                    own.step(dve.tensor_scalar(flat(whole), flat(real), QMAX, QMIN, ALU.min, ALU.max))
                    dve.tensor_scalar(q.values[:, 2 * n:2 * n + 2, :].rearrange("p a b -> p (a b)"), flat(whole), V_SCALE, None, ALU.mult)\
                       .then_inc(v_copied, 1)
                    dve.wait_ge(v_copied, n + 1)

            @block.tensor
            def _(pe):
                pe.wait_ge(w_ready, 1)
                values_program(pe, psV, q.w[:, :, 2 * D:3 * D], v_ready, v_copied, xnT=k.xnT)


class Integer:

    def __init__(self, phase):
        sb = phase.sbuf
        self.w = sb("w", [KP, KC, 3 * D])
        self.s, self.inv = sb("s", [P, 4]), sb("inv", [P, 4])
        self.fqk = sb("fqk", [HD3, HEADS3 + 1, 2])
        self.fa, self.fo, self.x0, self.half_b, self.c = (sb(n, [P, 1]) for n in ("fa", "fo", "x0", "half_b", "c"))
        self.low, self.inv_x0, self.minus_inv_x0 = (sb(n, [P, 1]) for n in ("low", "inv_x0", "minus_inv_x0"))
        self.x0_ident = sb("x0_ident", [P, P], BF16)
        self.values = sb("values", [P, TILES, D], BF16)


def attention3_heads(nc, k, q, turned_out):
    with Phase(nc, "t3_") as phase:
        sb, ps, sem = phase.sbuf, phase.psum, phase.semaphore
        wh, fh = sb("wh", [KP, KC, 2, HD3]), sb("fh", [HD3, 2])
        qk = sb("qk", [HD3, BATCH, 2, SEQ], BF16)
        vh = sb("vh", [P, BATCH, TPS, HD3], BF16)
        n16 = sb("n16", [P, SEQ], I16)
        clipped_n = sb("clipped_n", [P, 2, SEQ], BF16)
        digit = sb("digit", [P, 2, SEQ], BF16)
        power = sb("power", [P, 2, SEQ], I32)
        square = sb("square", [P, 2, SEQ])
        expo = sb("expo", [P, 2, SEQ])
        log = sb("log", [P, SEQ])
        ratio = sb("ratio", [P, 2, SEQ])
        whole = sb("whole", [P, SEQ])
        big = sb("big", [P, SEQ], I16)
        weights = sb("weights", [P, 2, SEQ], I16)
        weightsT = sb("weightsT", [P, 2, TPS, BLOCK], BF16)
        UH = BATCH * TPS
        top, peak0, peak, lowest, offset, bsq, total, logtotal = (
            sb(n, [P, UH]) for n in ("top", "peak0", "peak", "lowest", "offset", "bsq", "total", "logtotal"))
        staged = sb("staged", [HD3, 2, BLOCK], I16)
        stored_o = sb("stored_o", [HD3, 2, BLOCK], I16)
        psS, psR = ps("psS", [P, 4, BANK]), ps("psR", [P, 2, BANK])
        psT = ps("psT", [P, SEQ], BF16)
        psO = ps("psO", [P, BANK])
        names = ("own act_own scores_ready n_ready digits_ready rest_ready square_ready power_ready exp_ready ratio_ready weights_ready "
                 "turned copied small_ready staged_ready clipped pool_turn wh_ready vh_ready stored0 stored1").split()
        s = {n: sem(n) for n in names}
        LAST = HEADS3 * BATCH * TPS

        def wait(eng, name, value):
            if not (isinstance(value, int) and value <= 0):
                eng.wait_ge(s[name], value)

        ORDER = ("proj0", "pv_before", "proj1", "proj2", "proj3", "pv")

        def use(H, what):
            if isinstance(H, int) and H == 0:
                return 4 + [o for o in ORDER if o != "pv_before"].index(what)
            return H * 6 + 3 + ORDER.index(what)

        USES = {1: "proj0", 2: "pv_before", 3: "proj1", 4: "proj2", 5: "proj3", 6: "pv"}

        def uses_of(H, t):
            what = USES.get(t)
            if what is None or (what == "pv_before" and isinstance(H, int) and H == 0):
                return None
            return what

        def all_heads(eng, head, own=None, per=0):
            for b in range(BATCH):
                head(0, b)
            if own:
                done = own.n
            with eng.Fori(0, HEADS3 - 1) as i:
                if own:
                    own.enter(i, per)
                for b in range(BATCH):
                    head(i + 1, b)
            if own:
                own.leave(HEADS3 - 1)

        nc.scalar.preload_act_table_set("natural_log_exp_and_others")
        with nc.Block() as block:
            @block.tensor
            def _(pe):
                def project(n, batch, index):
                    part, blk = n // 2, n % 2
                    wait(pe, "staged_ready", index)
                    for j in range(KC):
                        last = pe.matmul(psO[0:HD3, :], wh[:, j, part, :], k.xnT[:, j, batch * SEQ + blk * BLOCK:batch * SEQ + (blk + 1) * BLOCK],
                                         start=(j == 0), stop=(j == KC - 1))
                    last.then_inc(s["small_ready"], 1)

                def scores(g, b, t):
                    wait(pe, "n_ready", g - 1)
                    for blk in range(2):
                        last = pe.matmul(psS[:, (t % 2) * 2 + blk, :], qk[:, b, 0, t * P:(t + 1) * P],
                                         qk[:, b, 1, blk * BLOCK:(blk + 1) * BLOCK], start=True, stop=True)
                    last.then_inc(s["scores_ready"], 1)

                def rest(g, t):
                    wait(pe, "digits_ready", g + 1)
                    wait(pe, "square_ready", g)
                    for blk in range(2):
                        cols = slice(blk * BLOCK, (blk + 1) * BLOCK)
                        pe.matmul(psR[:, blk, :], k.ident16[:, :], clipped_n[:, t % 2, cols], start=True, stop=False)
                        last = pe.matmul(psR[:, blk, :], q.x0_ident[:, :], digit[:, t % 2, cols], start=False, stop=True)
                    last.then_inc(s["rest_ready"], 1)

                def turn(g, t):
                    wait(pe, "weights_ready", g + 1)
                    wait(pe, "copied", g)
                    for kt in range(TPS):
                        last = pe.transpose(psT[:, kt * P:(kt + 1) * P], weights[:, t % 2, kt * P:(kt + 1) * P].bitcast(BF16), k.ident16[:, :])
                    last.then_inc(s["turned"], 1)

                def product(H, b, half, index):
                    wait(pe, "staged_ready", index)
                    wait(pe, "copied", H * TPS + (half + 1) * TPB)
                    wait(pe, "vh_ready", H + 1)
                    for kt in range(TPS):
                        last = pe.matmul(psO[0:HD3, :], vh[:, b, kt, :], weightsT[:, half, kt, :], start=(kt == 0), stop=(kt == TPS - 1))
                    last.then_inc(s["small_ready"], 1)

                def head(h, b):
                    H = h * 2 + b
                    for t in range(TPS):
                        g = H * TPS + t
                        if t < TPS - 1:
                            scores(g + 1, b, t + 1)
                        else:
                            wait(pe, "clipped", use(H, "proj3") + 1)
                            scores(g + 1, 1 - b, 0)
                        rest(g, t)
                        if not (isinstance(g, int) and g < 2):
                            turn(g - 2, t % 2)
                        what = uses_of(H, t)
                        if what == "pv":
                            product(H, b, 0, use(H, what))
                        elif what == "pv_before":
                            product(H + -1 if not isinstance(H, int) else H - 1, 1 - b, 1, use(H, what))
                        elif what:
                            if what == "proj0":
                                wait(pe, "wh_ready", h + 1 + b)
                            project(int(what[-1]), 1 - b, use(H, what))

                wait(pe, "wh_ready", 1)
                for n in range(4):
                    project(n, 0, n)
                wait(pe, "clipped", 4)
                scores(0, 0, 0)
                all_heads(pe, head)
                turn(LAST - 2, 0)
                turn(LAST - 1, 1)
                H = HEADS3 * BATCH
                product(H - 1, 1, 1, use(H, "proj0"))

            @block.vector
            def _(dve):
                own = Own(dve, s["own"])

                def digits(g, c, t):
                    wait(dve, "scores_ready", g + 1)
                    dve.tensor_scalar(n16[:, :], psS[:, (t % 2) * 2:(t % 2) * 2 + 2, :].rearrange("p a b -> p (a b)"), q.fa[:, 0:1], -3e38,
                                      ALU.mult, ALU.max, accum_out=top[:, c:c + 1]).then_inc(s["n_ready"], 1)
                    wait(dve, "n_ready", g + 1)
                    own.step(dve.tensor_scalar(peak0[:, c:c + 1], top[:, c:c + 1], ROUND, ROUND, ALU.add, ALU.subtract))
                    own.step(dve.tensor_scalar(peak[:, c:c + 1], peak0[:, c:c + 1], QMAX, QMIN, ALU.min, ALU.max))
                    wait(dve, "square_ready", g - 1)
                    dve.tensor_scalar(lowest[:, c:c + 1], peak[:, c:c + 1], q.low[:, 0:1], QMIN, ALU.add, ALU.max)
                    dve.tensor_scalar(offset[:, c:c + 1], peak[:, c:c + 1], q.minus_inv_x0[:, 0:1], -0.5 + 2.0 ** -10, ALU.mult, ALU.add)
                    own.step(dve.scalar_tensor_tensor(out=bsq[:, c:c + 1], in0=peak[:, c:c + 1], scalar=-1.0, in1=q.half_b[:, 0:1],
                                                      op0=ALU.mult, op1=ALU.add))
                    wait(dve, "rest_ready", g - 1)
                    wait(dve, "power_ready", g - 1)
                    own.step(dve.tensor_scalar(clipped_n[:, t % 2, :], n16[:, :], QMAX, lowest[:, c:c + 1], ALU.min, ALU.max))
                    own.step(dve.tensor_scalar(big[:, :], clipped_n[:, t % 2, :], q.inv_x0[:, 0:1], offset[:, c:c + 1], ALU.mult, ALU.add))
                    dve.tensor_copy(digit[:, t % 2, :], big[:, :]).then_inc(s["digits_ready"], 1)

                def exponential(g, c, t):
                    wait(dve, "square_ready", g + 1)
                    wait(dve, "power_ready", g + 1)
                    wait(dve, "ratio_ready", g - 1)
                    dve.scalar_tensor_tensor(out=expo[:, t % 2, :], in0=square[:, t % 2, :], scalar=q.c[:, 0:1],
                                             in1=power[:, t % 2, :].bitcast(F32), op0=ALU.add, op1=ALU.mult,
                                             accum_out=total[:, c:c + 1]).then_inc(s["exp_ready"], 1)

                def weigh(g, t):
                    wait(dve, "ratio_ready", g + 1)
                    own.step(dve.tensor_scalar(whole[:, :], ratio[:, t % 2, :], ROUND, ROUND, ALU.add, ALU.subtract))
                    wait(dve, "digits_ready", g + 1)
                    high = whole[:, :].bitcast(I16).rearrange("p (n two) -> p n two", two=2)[:, :, 1]
                    own.step(dve.tensor_scalar(big[:, :], high, 1.0 / 128, 2.0 ** -9 - 127 - 16, ALU.mult, ALU.add))
                    wait(dve, "turned", g - 1)
                    dve.tensor_scalar(weights[:, t % 2, :], big[:, :], 0.0, -128.0, ALU.min, ALU.mult).then_inc(s["weights_ready"], 1)
                    wait(dve, "weights_ready", g + 1)

                def head(h, b):
                    for t in range(TPS):
                        g, c = (h * 2 + b) * TPS + t, b * TPS + t
                        whole_steps = not isinstance(g, int)
                        if whole_steps or g >= 0:
                            digits(g, c, t)
                            wait(dve, "digits_ready", g + 1)
                        if whole_steps or g >= 1:
                            exponential(g - 1, (c - 1) % UH, (t - 1) % 2)
                        if whole_steps or g >= 2:
                            weigh(g - 2, t % 2)

                all_heads(dve, head, own, UH * 7)
                exponential(LAST - 1, UH - 1, 1)
                weigh(LAST - 2, 0)
                weigh(LAST - 1, 1)

            @block.scalar
            def _(act):
                def squares(g, c, t):
                    wait(act, "rest_ready", g + 1)
                    wait(act, "exp_ready", g - 1)
                    act.activation(square[:, t % 2, :], psR[:, :, :].rearrange("p a b -> p (a b)"), ACT.Square, bias=bsq[:, c:c + 1])\
                       .then_inc(s["square_ready"], 1)

                def ratios(g, c, t):
                    wait(act, "exp_ready", g + 1)
                    wait(act, "ratio_ready", g)
                    act.activation(logtotal[:, c:c + 1], total[:, c:c + 1], ACT.Ln)
                    act.activation(log[:, :], expo[:, t % 2, :], ACT.Ln).then_inc(s["act_own"], 1)
                    wait(act, "act_own", g + 1)
                    wait(act, "weights_ready", g - 1)
                    act.activation(ratio[:, t % 2, :], log[:, :], ACT.Exp, bias=logtotal[:, c:c + 1], scale=-1.0).then_inc(s["ratio_ready"], 1)

                def copy_turned(g, col, half, before):
                    wait(act, "turned", g + 1)
                    if before is not None:
                        wait(act, "small_ready", before + 1)
                    act.activation(weightsT[:, half, :, col * P:(col + 1) * P], psT[:, :].rearrange("p (a b) -> p a b", b=P), ACT.Copy)\
                       .then_inc(s["copied"], 1)

                def stage(index, slot, factor):
                    wait(act, "small_ready", index + 1)
                    wait(act, "clipped", index - 1)
                    act.activation(staged[:, slot, :], psO[0:HD3, :], ACT.Copy, scale=factor).then_inc(s["staged_ready"], 1)

                def head(h, b):
                    H = h * 2 + b
                    for t in range(TPS):
                        g, c = H * TPS + t, b * TPS + t
                        known = isinstance(g, int)
                        squares(g, c, t)
                        if not known or g >= 1:
                            ratios(g - 1, (c - 1) % UH, (t - 1) % 2)
                        if not known or g >= 2:
                            u = (t - 2) % TPS
                            half = u // TPB
                            at = H if t >= 2 else (H - 1 if known else H + -1)
                            before = None
                            if u % TPB == 0 and not (known and at < 1):
                                before = use(at - 1 if isinstance(at, int) else at + -1, "pv") if half == 0 else use(at, "pv_before")
                            copy_turned(g - 2, u % TPB, half, before)
                        what = uses_of(H, t)
                        if what:
                            factor = q.fo[0:HD3, 0:1] if what.startswith("pv") else fh[:, int(what[-1]) // 2:int(what[-1]) // 2 + 1]
                            index = use(H, what)
                            slot = (ORDER.index(what) + 1) % 2 if not (isinstance(H, int) and H == 0) else index % 2
                            stage(index, slot, factor)

                wait(act, "wh_ready", 1)
                for n in range(4):
                    stage(n, n % 2, fh[:, n // 2:n // 2 + 1])
                all_heads(act, head)
                ratios(LAST - 1, UH - 1, 1)
                copy_turned(LAST - 2, 2, 1, None)
                copy_turned(LAST - 1, 3, 1, None)
                H = HEADS3 * BATCH
                index = use(H, "proj0")
                stage(index, index % 2, q.fo[0:HD3, 0:1])

            @block.gpsimd
            def _(pool):
                def powers(g, t):
                    wait(pool, "digits_ready", g + 1)
                    wait(pool, "exp_ready", g - 1)
                    pool.sem_inc(s["pool_turn"], 1)
                    pool.tensor_scalar(power[:, t % 2, :], digit[:, t % 2, :], -2.0 ** 23, 157 * 2.0 ** 23, ALU.mult, ALU.add)\
                        .then_inc(s["power_ready"], 1)

                def clip(index, slot, out):
                    wait(pool, "staged_ready", index + 1)
                    pool.sem_inc(s["pool_turn"], 1)
                    pool.tensor_scalar(out, staged[:, slot, :], QMAX, QMIN, ALU.min, ALU.max).then_inc(s["clipped"], 1)

                def weights_of(head_index):
                    source = flat(q.w)
                    for j in range(KC):
                        for part in range(2):
                            pool.tensor_copy(wh[:, j, part, :], source[:, ds(j * 3 * D + part * D + head_index * HD3, HD3)])
                    pool.tensor_copy(fh[:, :], flat(q.fqk)[:, ds(head_index * 2, 2)]).then_inc(s["wh_ready"], 1)

                def head(h, b):
                    H = h * 2 + b
                    for t in range(TPS):
                        g = H * TPS + t
                        if t == 0:
                            if not (isinstance(H, int) and H < 2):
                                wait(pool, "small_ready", use(H + -1 if not isinstance(H, int) else H - 1, "pv_before") + 1)
                            pool.tensor_copy(vh[:, b], q.values[:, b * TPS:(b + 1) * TPS, ds(h * HD3, HD3)]).then_inc(s["vh_ready"], 1)
                            if b == 1:
                                wait(pool, "staged_ready", use(H + -1 if not isinstance(H, int) else H - 1, "proj3") + 1)
                                weights_of(h + 1)
                        powers(g, t)
                        what = uses_of(H, t)
                        if what:
                            index = use(H, what)
                            slot = (ORDER.index(what) + 1) % 2 if not (isinstance(H, int) and H == 0) else index % 2
                            if what.startswith("pv"):
                                half = 0 if what == "pv" else 1
                                before = h * 2 + b + -int(what == "pv_before")
                                wait(pool, "stored%d" % half, before * 16)
                                clip(index, slot, stored_o[:, half, :])
                            else:
                                n = int(what[-1])
                                clip(index, slot, qk[:, 1 - b, n // 2, (n % 2) * BLOCK:(n % 2 + 1) * BLOCK])

                weights_of(0)
                for n in range(4):
                    clip(n, n % 2, qk[:, 0, n // 2, (n % 2) * BLOCK:(n % 2 + 1) * BLOCK])
                all_heads(pool, head)
                H = HEADS3 * BATCH
                index = use(H, "proj0")
                wait(pool, "stored1", (H - 1) * 16)
                clip(index, index % 2, stored_o[:, 1, :])

            @block.sync
            def _(sp):
                def store(h, b, half, index):
                    wait(sp, "clipped", index + 1)
                    cols = slice(b * SEQ + half * BLOCK, b * SEQ + (half + 1) * BLOCK)
                    sp.dma_start(turned_out[ds(h * HD3, HD3), cols], stored_o[:, half, :]).then_inc(s["stored%d" % half], 16)

                def head(h, b):
                    H = h * 2 + b
                    if not (isinstance(H, int) and H == 0):
                        store(h if b else (h - 1 if isinstance(h, int) else h + -1), 1 - b, 1, use(H, "pv_before"))
                    store(h, b, 0, use(H, "pv"))

                all_heads(sp, head)
                store(HEADS3 - 1, 1, 1, use(HEADS3 * BATCH, "proj0"))
                for half in range(2):
                    sp.wait_ge(s["stored%d" % half], HEADS3 * BATCH * 16)


def attention3_output(nc, k, q, a, turned_out):
    with Phase(nc, "o3_") as phase:
        sb, ps, sem = phase.sbuf, phase.psum, phase.semaphore
        o16, o = sb("o16", [KP, KC, TOK], I16), sb("o", [KP, KC, TOK], BF16)
        w, scale, inverse = sb("w", [KP, KC, D]), sb("scale", [KP, D]), sb("inverse", [KP, D])
        wi = sb("wi", [KP, KC, D], BF16)
        factor, bias = sb("factor", [P, D]), sb("bias", [P, D])
        y = sb("y", [P, TPB, D])
        psY = ps("psY", [P, 2, 2, BANK])
        loaded, own_sem, ready, y_ready, y_used = sem("loaded"), sem("own"), sem("ready"), sem("y_ready"), sem("y_used")

        with nc.Block() as block:
            @block.sync
            def _(sp):
                sp.dma_start(o16[:, :, :], turned_out.rearrange("(c p) t -> p c t", p=KP)).then_inc(loaded, 16)
                sp.dma_start(w[:, :, :], a["a3_wo"]).then_inc(loaded, 16)
                sp.dma_start(scale[:, :], a["a3_wo_scale"].partition_broadcast(KP)).then_inc(loaded, 16)
                sp.dma_start(factor[:, :], a["a3_wo_scale"].partition_broadcast(P)).then_inc(loaded, 16)
                sp.dma_start(bias[:, :], a["a3_wo_bias"].partition_broadcast(P)).then_inc(loaded, 16)

            @block.vector
            def _(dve):
                own = Own(dve, own_sem)
                dve.wait_ge(loaded, 5 * 16)
                own.step(dve.reciprocal(inverse[:, :], scale[:, :]))
                own.step(dve.tensor_tensor(w[:, :, :], w[:, :, :], across(inverse[:, :], KC), ALU.mult))
                own.step(dve.tensor_scalar(flat(w), flat(w), QMAX, QMIN, ALU.min, ALU.max))
                dve.tensor_scalar(flat(wi), flat(w), ROUND, ROUND, ALU.add, ALU.subtract)
                dve.tensor_scalar(factor[:, :], factor[:, :], q.s[:, 2:3], None, ALU.mult)
                dve.tensor_copy(flat(o), flat(o16)).then_inc(ready, 1)
                dve.wait_ge(ready, 1)
                h = flat(k.h)
                with dve.Fori(0, NBLK // 2) as i:
                    own.enter(i, 2 * 5)
                    for n in range(2):
                        dve.wait_ge(y_ready, i * 2 + n + 1)
                        dve.wait_ge(y_used, i * 2 + n)
                        for half in range(2):
                            last = dve.tensor_tensor(y[:, half * 2:half * 2 + 2, :], psY[:, n, half, 0:2 * D].rearrange("p (a b) -> p a b", b=D),
                                                     across(factor[:, :], 2), ALU.mult)
                        own.step(last)
                        own.step(dve.tensor_tensor(y[:, :, :], y[:, :, :], across(bias[:, :], TPB), ALU.add))
                        own.step(dve.tensor_scalar(flat(y), flat(y), q.inv[:, 3:4], QMAX, ALU.mult, ALU.min))
                        own.step(dve.tensor_scalar(flat(y), flat(y), QMIN, ROUND, ALU.max, ALU.add))
                        own.step(dve.tensor_scalar(flat(y), flat(y), ROUND, q.s[:, 3:4], ALU.subtract, ALU.mult))
                        at = ds((i * 2 + n) * TPB * D, TPB * D)
                        dve.tensor_tensor(h[:, at], h[:, at], flat(y), ALU.add).then_inc(y_used, 1)
                own.leave(NBLK // 2)

            @block.tensor
            def _(pe):
                pe.wait_ge(ready, 1)
                for g in range(NBLK):
                    if g >= 2:
                        pe.wait_ge(y_used, g - 1)
                    for t in range(TPB):
                        for j in range(KC):
                            at = (g * TPB + t) * P
                            last = pe.matmul(psY[:, g % 2, t // 2, (t % 2) * D:(t % 2 + 1) * D], o[:, j, at:at + P], wi[:, j, :],
                                             start=(j == 0), stop=(j == KC - 1))
                    last.then_inc(y_ready, 1)


def attention3_phase(nc, k, a):
    turned_out = nc.dram_tensor("turned_out", (D, TOK), I16, kind="Internal").ap()
    with Phase(nc, "i3_") as phase:
        q = Integer(phase)
        attention3_setup(nc, k, q, a)
        attention3_heads(nc, k, q, turned_out)
        attention3_output(nc, k, q, a, turned_out)


class Persistent:

    def __init__(self, nc, c):
        sb = lambda n, s, t=F32: c.enter_context(nc.sbuf_tensor(n, s, t))
        self.h = sb("h", [P, TILES, D])
        self.xn = sb("xn", [P, TILES, D])
        self.xnT = sb("xnT", [KP, KC, TOK])
        self.acc = sb("acc", [P, TILES, D])
        self.comb = sb("comb", [P, 9, TILES])
        self.ident = sb("ident", [P, P])
        self.ident16 = sb("ident16", [P, P], BF16)
        self.minus_half = sb("minus_half", [P, TILES])
        self.rank = sb("rank", [P, 8])


def audio_tower(nc, a, out, stop=99):
    with ExitStack() as c:
        k = Persistent(nc, c)
        stages = [
            lambda: pool_phase(nc, k, a["x"], a["tok_w"]),
            lambda: (norm_phase(nc, k, "n0_", k.h),
                     attention0_phase(nc, k, a["a0_wqk"], a["a0_wv"], a["a0_wo"], a["a0_anchor_w"], a["a0_anchors"], a["a0_lam"])),
            lambda: (norm_phase(nc, k, "n1_", k.h, Router("softmax", 8, a["f0_router"], select_bias=a["f0_bias"], eps=1e-9)),
                     ones_phase(nc, k, 8),
                     experts_phase(nc, k, "f0_", k.h, 9, 3, a["f0_in"], a["f0_out"], gated=True)),
            lambda: (norm_phase(nc, k, "n2_", k.h),
                     attention1_phase(nc, k, a["a1_w"], a["a1_qk_bias"], a["a1_v_bias"], a["a1_decay"])),
            lambda: (norm_phase(nc, k, "n3_", k.h, Router("sigmoid", 3, a["f1_router"], logit_bias=a["f1_bias"])),
                     ones_phase(nc, k, 3),
                     experts_phase(nc, k, "f1_", k.h, 4, 3, a["f1_in"], a["f1_out"], gated=True)),
            lambda: (norm_phase(nc, k, "n4_", k.h),
                     attention2_phase(nc, k, a["a2_w"], a["a2_v_bias"]),
                     norm_phase(nc, k, "n5_", k.acc, normalise=False),
                     experts_phase(nc, k, "g2_", k.acc, 1, 6, a["g2_in"], a["g2_out"], a["g2_in_bias"], a["g2_out_bias"], weighted=False),
                     affine_norm_phase(nc, k, "n6_", k.acc, 1e-12, a["a2_gamma"], a["a2_beta"])),
            lambda: (norm_phase(nc, k, "n7_", k.h, Router("softmax", 8, a["f2_router"], logit_bias=a["f2_bias"], eps=1e-8,
                                                         hidden=(a["f2_hidden"], a["f2_hidden_bias"]))),
                     experts_phase(nc, k, "f2_", k.xn, 8, 2, a["f2_in"], a["f2_out"], a["f2_in_bias"]),
                     affine_norm_phase(nc, k, "n8_", k.xn, LN_EPS, a["f2_gamma"], a["f2_beta"])),
            lambda: (norm_phase(nc, k, "n9_", k.h),
                     attention3_phase(nc, k, a)),
            lambda: (norm_phase(nc, k, "n10_", k.h, Router("softmax", 8, a["f3_router"], eps=1e-9)),
                     experts_phase(nc, k, "f3_", k.h, 8, 6, a["f3_in"], a["f3_out"], a["f3_in_bias"], a["f3_out_bias"])),
        ]
        for stage in stages[:stop]:
            stage()
        stored = c.enter_context(nc.semaphore("stored"))
        with nc.Block() as block:
            @block.sync
            def _(sp):
                sp.dma_start(out.rearrange("b (t p) d -> p (b t) d", p=P), k.h[:, :, :]).then_inc(stored, 16)
                sp.wait_ge(stored, 16)


def ones_phase(nc, k, e):
    with nc.Block() as block:
        @block.vector
        def _(dve):
            dve.memset(k.comb[:, e, :], 1.0)


def _laid_out(np, i):
    f = np.ascontiguousarray

    def rows(w, p=KP):
        w = np.asarray(w)
        lead = w.shape[:-2]
        w = w.reshape(*lead, w.shape[-2] // p, p, w.shape[-1])
        return f(np.swapaxes(w, -3, -2))

    def t(w):
        return np.swapaxes(np.asarray(w), -1, -2)

    def col(b, p=P):
        b = np.asarray(b)
        return f(np.swapaxes(b.reshape(*b.shape[:-1], b.shape[-1] // p, p), -1, -2))

    def both(*w):
        return np.concatenate(w, axis=-1)

    def more(w, shared):
        return np.concatenate([w, shared[None]], axis=0)

    j = np.arange(-3 * P, SEQ, dtype=np.float32)[None, :] - np.arange(P, dtype=np.float32)[:, None]
    decay = np.where(j >= 0, np.float32(0.99) ** np.maximum(j, 0), 0).astype(np.float32) / np.float32(D) ** np.float32(0.5)
    a = {"x": i["x"], "tok_w": rows(i["L0_tok_w"])}
    qk = np.stack([t(i["L0_attn_Wq"]), t(i["L0_attn_Wk"])], axis=1).reshape(D, 2, HEADS0, HD0).transpose(2, 0, 1, 3)
    a["a0_wqk"] = f(qk.reshape(HEADS0, KC, KP, 2, HD0).transpose(0, 2, 1, 3, 4))
    a["a0_wv"] = rows(t(i["L0_attn_Wv"]))
    a["a0_wo"] = f(t(i["L0_attn_Wo"]).reshape(HEADS0, HD0, D))
    a["a0_anchor_w"] = f(i["L0_attn_anchor_w"].transpose(1, 0, 2))
    a["a0_anchors"], a["a0_lam"] = i["L0_attn_anchors"], i["L0_attn_lam"]
    a["f0_router"], a["f0_bias"] = rows(t(i["L0_ffn_w_router"])), i["L0_ffn_expert_bias"]
    a["f0_in"] = rows(both(t(more(i["L0_ffn_Wg"], i["L0_ffn_sg"])), t(more(i["L0_ffn_Wu"], i["L0_ffn_su"]))))
    a["f0_out"] = rows(t(more(i["L0_ffn_Wd"], i["L0_ffn_sd"])), P)
    a["a1_w"] = rows(t(i["L1_attn_W_qkv"])).reshape(KP, KC, 3, D)
    b = i["L1_attn_b_qkv"]
    a["a1_qk_bias"], a["a1_v_bias"] = f(b[:2 * D].reshape(2, KC, KP).transpose(2, 0, 1)), f(b[2 * D:])
    a["a1_decay"] = decay
    a["f1_router"], a["f1_bias"] = rows(i["L1_ffn_router_w"]), i["L1_ffn_routing_bias"]
    a["f1_in"] = rows(both(more(i["L1_ffn_routed_gate"], i["L1_ffn_shared_gate"]), more(i["L1_ffn_routed_up"], i["L1_ffn_shared_up"])))
    a["f1_out"] = rows(more(i["L1_ffn_routed_down"], i["L1_ffn_shared_down"]), P)
    a["a2_w"], a["a2_v_bias"] = rows(both(i["L2_attn_val_w"], t(i["L2_attn_mu"]))), i["L2_attn_val_b"]
    a["g2_in"], a["g2_out"] = rows(i["L2_attn_w1"])[None], rows(i["L2_attn_w2"], P)[None]
    a["g2_in_bias"], a["g2_out_bias"] = col(i["L2_attn_b1"])[None], i["L2_attn_b2"][None]
    a["a2_gamma"], a["a2_beta"] = i["L2_attn_ln_g"], i["L2_attn_ln_b"]
    a["f2_hidden"], a["f2_hidden_bias"] = rows(i["L2_ffn_w1"]), f(i["L2_ffn_b1"][:, None])
    a["f2_router"], a["f2_bias"] = f(i["L2_ffn_w2"][:, None, :]), i["L2_ffn_b2"]
    a["f2_in"], a["f2_out"], a["f2_in_bias"] = rows(i["L2_ffn_down_w"]), rows(i["L2_ffn_up_w"], P), col(i["L2_ffn_down_b"])
    a["f2_gamma"], a["f2_beta"] = i["L2_ffn_gamma"], i["L2_ffn_beta"]
    a["a3_w"], a["a3_scale"] = rows(t(i["L3_attn_w_qkv"])), i["L3_attn_s_wqkv"]
    a["a3_qkscale"] = f(i["L3_attn_s_wqkv"][:2 * D].reshape(2, HEADS3, HD3).transpose(2, 1, 0))
    a["a3_wo"], a["a3_wo_scale"], a["a3_wo_bias"] = rows(t(i["L3_attn_w_proj"])), i["L3_attn_s_wproj"], i["L3_attn_b_proj"]
    for n in ("s_act1", "s_attn", "s_act2", "s_act3"):
        a["a3_" + n] = i["L3_attn_" + n]
    a["f3_router"] = rows(t(i["L3_ffn_gate_w"]))
    a["f3_in"], a["f3_out"] = rows(i["L3_ffn_w1"]), rows(i["L3_ffn_w2"], P)
    a["f3_in_bias"], a["f3_out_bias"] = col(i["L3_ffn_b1"]), i["L3_ffn_b2"]
    return {n: f(v) for n, v in a.items()}


STOP = 99


def kernel(**inputs):
    import numpy as _np
    import concourse.bacc as _bacc
    from concourse import mybir as _mybir
    from concourse.bass_utils import run_bass_kernel_spmd as _run

    nc = _bacc.Bacc("TRN2", target_bir_lowering=False, num_devices=1)
    arrays = _laid_out(_np, {n: _np.asarray(v) for n, v in inputs.items()})
    args = {n: nc.dram_tensor(f"in_{n}", v.shape, _mybir.dt.from_np(v.dtype), kind="ExternalInput").ap() for n, v in arrays.items()}
    out = nc.dram_tensor("out_h", (BATCH, SEQ, D), F32, kind="ExternalOutput").ap()
    audio_tower(nc, args, out, STOP)
    r = _run(nc, [{f"in_{n}": v for n, v in arrays.items()}], core_ids=[0])
    return r.results[0]["out_h"]
```

```python
from contextlib import ExitStack

import concourse.bass as bass
from concourse import mybir

ALU = mybir.AluOpType
ACT = mybir.ActivationFunctionType
AXX = mybir.AxisListType.X
F32 = mybir.dt.float32
BF16 = mybir.dt.bfloat16
I16 = mybir.dt.int16
I32 = mybir.dt.int32
F32R = mybir.dt.float32r
ds = bass.ds

P = 128
D = 192
KP, KC = 96, 2
BATCH, SEQ = 2, 1024
TOK = BATCH * SEQ
TILES = TOK // P
BLOCK = 512
NBLK = TOK // BLOCK
TPB = BLOCK // P
TPS = SEQ // P
BANK = 512
LN_EPS = 1e-5

TAIL = D - P


SAME = (1.0, 0.0, ALU.mult, ALU.add)


class Own:

    def __init__(self, eng, sem):
        self.eng, self.sem, self.start, self.base, self.n = eng, sem, 0, 0, 0

    def step(self, instruction):
        self.await_step(self.mark(instruction))

    def mark(self, instruction):
        instruction.then_inc(self.sem, 1)
        self.n += 1
        return self.base + self.n

    def await_step(self, count):
        self.eng.wait_ge(self.sem, count)

    def enter(self, i, per):
        self.start, self.base, self.n, self.per = self.start + self.n, self.start + self.n + i * per, 0, per

    def leave(self, times):
        assert self.n == self.per, (self.n, self.per)
        self.start += times * self.per
        self.base, self.n = self.start, 0


class Phase:

    def __init__(self, nc, name):
        self.nc, self.name, self.stack, self.sems = nc, name, ExitStack(), []

    def sbuf(self, name, shape, dtype=F32):
        return self.stack.enter_context(self.nc.sbuf_tensor(self.name + name, shape, dtype))

    def psum(self, name, shape, dtype=F32):
        return self.stack.enter_context(self.nc.psum_tensor(self.name + name, shape, dtype))

    def semaphore(self, name):
        self.sems.append(self.nc.alloc_semaphore(self.name + name))
        return self.sems[-1]

    def __enter__(self):
        return self

    def __exit__(self, *failure):
        if failure[0] is None:
            self.nc.clear_and_free_semaphores(self.sems)
            self.nc.all_engine_barrier()
        self.stack.close()


def flat(t):
    return t[:, :, :].rearrange("p a b -> p (a b)")


def wide(ap, n):
    a = ap.unsqueeze(2)
    return a.to_broadcast([a.shape[0], a.shape[1], n])


def across(ap, n):
    a = ap.unsqueeze(1)
    return a.to_broadcast([a.shape[0], n, a.shape[2]])


def pool_phase(nc, k, x, tok_w):
    with Phase(nc, "po_") as phase:
        sb, ps, sem = phase.sbuf, phase.psum, phase.semaphore
        pairs = sb("pairs", [P, TILES, 2, D])
        w = sb("w", [KP, KC, D])
        diff = sb("diff", [P, 2, TPB, D])
        diffT = sb("diffT", [KP, 2, KC, BLOCK])
        gate = sb("gate", [P, 2, TPB, D])
        scaled = sb("scaled", [P, 2, TPB, D])
        psT = ps("psT", [P, 2, KC, BANK])
        psS = ps("psS", [P, 2, 2, BANK])
        x_in = [sem(f"x_in{g}") for g in range(NBLK)]
        w_in, ident0, ident1 = sem("w_in"), sem("ident0"), sem("ident1")
        diff_ready, transposed, diffT_ready = sem("diff_ready"), sem("transposed"), sem("diffT_ready")
        scores_ready, gate_ready, scaled_ready, h_ready = (
            sem("scores_ready"), sem("gate_ready"), sem("scaled_ready"), sem("h_ready"))
        xv = x.rearrange("b (n i) d -> (b n) i d", i=2).rearrange("(t p) i d -> p t i d", p=P)

        with nc.Block() as block:
            @block.sync
            def _(sp):
                sp.dma_start(w[:, :, :], tok_w).then_inc(w_in, 16)
                for g in range(NBLK):
                    sp.dma_start(pairs[:, g * TPB:(g + 1) * TPB], xv[:, g * TPB:(g + 1) * TPB]).then_inc(x_in[g], 16)

            @block.gpsimd
            def _(pool):
                pool.memset(k.ident[:, :], 0.0).then_inc(ident0, 1)
                pool.wait_ge(ident0, 1)
                pool.affine_select(out=k.ident[:, :], in_=k.ident[:, :], compare_op=ALU.not_equal, fill=1.0, base=0,
                                   pattern=[[-1, P]], channel_multiplier=1).then_inc(ident1, 1)
                pool.memset(k.minus_half[:, :], -0.5).then_inc(ident0, 1)
                for e in range(8):
                    last = pool.memset(k.rank[:, e:e + 1], float(8 - e))
                last.then_inc(ident0, 1)
                pool.wait_ge(ident1, 1)
                pool.tensor_copy(k.ident16[:, :], k.ident[:, :]).then_inc(ident0, 1)
                pool.wait_ge(ident0, 4)

            @block.vector
            def _(dve):
                def difference(g):
                    dve.wait_ge(x_in[g], 16)
                    if g >= 2:
                        dve.wait_ge(transposed, g - 1)
                        dve.wait_ge(scaled_ready, g - 1)
                    t = slice(g * TPB, (g + 1) * TPB)
                    dve.tensor_tensor(diff[:, g % 2], pairs[:, t, 0], pairs[:, t, 1], ALU.subtract).then_inc(diff_ready, 1)

                def combine(g):
                    t = slice(g * TPB, (g + 1) * TPB)
                    dve.wait_ge(diff_ready, g + 1)
                    dve.wait_ge(gate_ready, g + 1)
                    if g >= 2:
                        dve.wait_ge(h_ready, g - 1)
                    dve.tensor_tensor(scaled[:, g % 2], gate[:, g % 2], diff[:, g % 2], ALU.mult).then_inc(scaled_ready, 1)
                    dve.wait_ge(scaled_ready, g + 1)
                    dve.tensor_tensor(k.h[:, t], scaled[:, g % 2], pairs[:, t, 1], ALU.add).then_inc(h_ready, 1)

                difference(0)
                for g in range(1, NBLK):
                    difference(g)
                    combine(g - 1)
                combine(NBLK - 1)

            @block.tensor
            def _(pe):
                pe.wait_ge(ident1, 1)
                pe.wait_ge(w_in, 16)
                for g in range(NBLK):
                    pe.wait_ge(diff_ready, g + 1)
                    if g >= 2:
                        pe.wait_ge(diffT_ready, g - 1)
                    for t in range(TPB):
                        for j in range(KC):
                            last = pe.transpose(psT[0:KP, g % 2, j, t * P:(t + 1) * P],
                                                diff[:, g % 2, t, j * KP:(j + 1) * KP], k.ident[:, :])
                    last.then_inc(transposed, 1)
                    pe.wait_ge(diffT_ready, g + 1)
                    if g >= 2:
                        pe.wait_ge(gate_ready, g - 1)
                    for t in range(TPB):
                        for j in range(KC):
                            last = pe.matmul(psS[:, g % 2, t // 2, (t % 2) * D:(t % 2 + 1) * D],
                                             diffT[:, g % 2, j, t * P:(t + 1) * P], w[:, j, :],
                                             start=(j == 0), stop=(j == KC - 1))
                    last.then_inc(scores_ready, 1)

            @block.scalar
            def _(act):
                for g in range(NBLK):
                    act.wait_ge(transposed, g + 1)
                    if g >= 2:
                        act.wait_ge(scores_ready, g - 1)
                    act.activation(diffT[:, g % 2], psT[0:KP, g % 2], ACT.Copy).then_inc(diffT_ready, 1)
                    act.wait_ge(scores_ready, g + 1)
                    if g >= 2:
                        act.wait_ge(scaled_ready, g - 1)
                    act.activation(gate[:, g % 2].rearrange("p (a t) d -> p a (t d)", a=2), psS[:, g % 2, :, 0:2 * D],
                                   ACT.Sigmoid).then_inc(gate_ready, 1)


class Router:

    def __init__(self, kind, experts, w, select_bias=None, logit_bias=None, eps=0.0, hidden=None):
        self.kind, self.experts, self.w, self.eps, self.hidden = kind, experts, w, eps, hidden
        self.select_bias, self.logit_bias = select_bias, logit_bias


def split_product(pe, out, w_high, w_low, k, cols, columns):
    passes = ((w_high, 0, k.x_high), (w_low, 0, k.x_high), (w_high, 0, k.x_low), (w_high, 1, k.x_tail), (w_low, 1, k.x_tail))
    for n, (w, chunk, x) in enumerate(passes):
        last = pe.matmul(out, w[:, chunk, cols], x[:, columns], start=(n == 0), stop=(n == len(passes) - 1))
    return last


def norm_phase(nc, k, name, src, router=None, normalise=True, split=False, weights=None):
    assert split or not router
    E = router.experts if router else 1
    R = router
    with Phase(nc, name) as phase:
        sb, ps, sem = phase.sbuf, phase.psum, phase.semaphore
        stats = sb("stats", [P, TILES, 6])
        moments = sb("moments", [P, TILES, 2])
        rstd0 = sb("rstd0", [P, TILES])
        rstd = sb("rstd", [P, TILES])
        psT = ps("psT", [P, 2, KC, BANK])
        twice = sb("twice", [P, TILES, 2, TAIL]) if split else None
        twice_ready, low_ready = sem("twice_ready"), sem("low_ready")
        own_sem, stats_ready, eps_added, rstd_ready = sem("own"), sem("stats_ready"), sem("eps_added"), sem("rstd_ready")
        moments_ready = sem("moments_ready")
        xn_ready, transposed, xnT_ready = sem("xn_ready"), sem("transposed"), sem("xnT_ready")
        if R:
            KR, CR = (KP, 1) if R.hidden else (P, 2)
            SPLIT = ((0, k.x_high), (0, k.x_low), (1, k.x_tail))
            wr = sb("wr", [KR, CR, E])
            sbias, lbias = sb("sbias", [P, E]), sb("lbias", [P, E])
            logits, probs, sel = sb("logits", [P, TILES, E]), sb("probs", [P, TILES, E]), sb("sel", [P, TILES, E])
            hit, first, second = sb("hit", [P, TILES, E]), sb("first", [P, TILES, E]), sb("second", [P, TILES, E])
            top, total, inverse = sb("top", [P, TILES]), sb("total", [P, TILES]), sb("inverse", [P, TILES])
            psR = ps("psR", [P, BANK])
            router_in, logits_ready, shifted, probs_ready = sem("router_in"), sem("logits_ready"), sem("shifted"), sem("probs_ready")
            if R.hidden:
                w1, b1 = sb("w1", [P, 2, KP]), sb("b1", [KP, 1])
                hidT = sb("hidT", [KP, TOK])
                psH = ps("psH", [P, 2, BANK])
                hidden_ready, hidT_ready = sem("hidden_ready"), sem("hidT_ready")
        loads = 0
        if R:
            loads = 1 + (R.select_bias is not None) + (R.logit_bias is not None) + 2 * bool(R.hidden)

        with nc.Block() as block:
            @block.sync
            def _(sp):
                if R:
                    sp.dma_start(wr[:, :, :], R.w).then_inc(router_in, 16)
                    if R.select_bias is not None:
                        sp.dma_start(sbias[:, :], R.select_bias.partition_broadcast(P)).then_inc(router_in, 16)
                    if R.logit_bias is not None:
                        sp.dma_start(lbias[:, :], R.logit_bias.partition_broadcast(P)).then_inc(router_in, 16)
                    if R.hidden:
                        sp.dma_start(w1[:, :, :], R.hidden[0]).then_inc(router_in, 16)
                        sp.dma_start(b1[:, :], R.hidden[1]).then_inc(router_in, 16)
                if weights:
                    weights.begin_load(sp)

            @block.gpsimd
            def _(pool):
                if normalise:
                    pool.wait_ge(moments_ready, 1)
                    pool.tensor_scalar(rstd0[:, :], moments[:, :, 1], LN_EPS, None, ALU.add).then_inc(eps_added, 1)
                    pool.wait_ge(eps_added, 1)
                    pool.tensor_tensor(rstd[:, :], rstd0[:, :], k.minus_half[:, :], ALU.pow).then_inc(rstd_ready, 1)
                if split:
                    for g in range(NBLK):
                        if normalise:
                            pool.wait_ge(xn_ready, (g + 1) * TPB)
                        tiles = slice(g * TPB, (g + 1) * TPB)
                        for half in range(2):
                            last = pool.tensor_scalar(twice[:, tiles, half, :], (k.xn if normalise else src)[:, tiles, P:D], *SAME)
                        last.then_inc(twice_ready, 1)
                if weights:
                    weights.begin_split(pool)

            @block.vector
            def _(dve):
                own = Own(dve, own_sem)
                source, target, mom = flat(src), flat(k.xn), flat(moments)
                if normalise:
                    with dve.Fori(0, NBLK) as g:
                        for t in range(TPB):
                            tile = g * TPB + t
                            last = dve.bn_stats(flat(stats)[:, ds(tile * 6, 6)], source[:, ds(tile * D, D)])
                        last.then_inc(stats_ready, 1)
                    dve.wait_ge(stats_ready, NBLK)
                    for t in range(TILES):
                        last = dve.bn_aggr(moments[:, t, :], stats[:, t, :])
                    last.then_inc(moments_ready, 1)
                    dve.wait_ge(rstd_ready, 1)
                    with dve.Fori(0, NBLK) as g:
                        for t in range(TPB):
                            tile = g * TPB + t
                            dve.tensor_scalar(target[:, ds(tile * D, D)], source[:, ds(tile * D, D)],
                                              mom[:, ds(tile * 2, 1)], rstd[:, ds(tile, 1)],
                                              ALU.subtract, ALU.mult).then_inc(xn_ready, 1)
                if split:
                    for g in range(NBLK):
                        cols = slice(g * BLOCK, (g + 1) * BLOCK)
                        dve.wait_ge(xnT_ready, g + 1)
                        dve.tensor_tensor(k.x_low[:, cols], psT[:, g % 2, 0, :], k.x_high[:, cols].bitcast(F32), ALU.subtract)
                        dve.tensor_tensor(k.x_tail[TAIL:P, cols], psT[TAIL:P, g % 2, 1, :], k.x_tail[TAIL:P, cols].bitcast(F32),
                                          ALU.subtract).then_inc(low_ready, 1)
                if not R:
                    return
                dve.wait_ge(router_in, 16 * loads)
                dve.wait_ge(logits_ready, 1)
                raw = psR[:, 0:TILES * E].rearrange("p (t e) -> p t e", e=E)
                if R.logit_bias is not None:
                    own.step(dve.tensor_tensor(logits[:, :, :], raw, across(lbias[:, :], TILES), ALU.add))
                else:
                    own.step(dve.tensor_copy(logits[:, :, :], raw))
                if R.kind == "softmax":
                    own.step(dve.tensor_reduce(top[:, :], logits[:, :, :], AXX, ALU.max))
                    dve.tensor_tensor(logits[:, :, :], logits[:, :, :], wide(top[:, :], E), ALU.subtract).then_inc(shifted, 1)
                    dve.wait_ge(probs_ready, 1)
                    own.step(dve.tensor_reduce(total[:, :], probs[:, :, :], AXX, ALU.add))
                    own.step(dve.reciprocal(inverse[:, :], total[:, :]))
                    own.step(dve.tensor_tensor(probs[:, :, :], probs[:, :, :], wide(inverse[:, :], E), ALU.mult))
                else:
                    dve.tensor_copy(sel[:, :, :], logits[:, :, :]).then_inc(shifted, 1)
                    dve.wait_ge(probs_ready, 1)
                if R.select_bias is not None:
                    own.step(dve.tensor_tensor(sel[:, :, :], probs[:, :, :], across(sbias[:, :], TILES), ALU.add))
                else:
                    dve.wait_ge(shifted, 1)
                    own.step(dve.tensor_copy(sel[:, :, :], probs[:, :, :]))

                def highest(out):
                    own.step(dve.tensor_reduce(top[:, :], sel[:, :, :], AXX, ALU.max))
                    own.step(dve.tensor_tensor(hit[:, :, :], sel[:, :, :], wide(top[:, :], E), ALU.is_equal))
                    own.step(dve.tensor_tensor(hit[:, :, :], hit[:, :, :], across(k.rank[:, 0:E], TILES), ALU.mult))
                    own.step(dve.tensor_reduce(top[:, :], hit[:, :, :], AXX, ALU.max))
                    own.step(dve.tensor_tensor(out[:, :, :], hit[:, :, :], wide(top[:, :], E), ALU.is_equal))

                highest(first)
                own.step(dve.scalar_tensor_tensor(out=flat(sel), in0=flat(first), scalar=-1e30, in1=flat(sel),
                                                  op0=ALU.mult, op1=ALU.add))
                highest(second)
                own.step(dve.tensor_tensor(first[:, :, :], first[:, :, :], second[:, :, :], ALU.add))
                own.step(dve.tensor_tensor(probs[:, :, :], probs[:, :, :], first[:, :, :], ALU.mult))
                own.step(dve.tensor_reduce(total[:, :], probs[:, :, :], AXX, ALU.add))
                if R.eps:
                    own.step(dve.tensor_scalar(total[:, :], total[:, :], R.eps, None, ALU.add))
                own.step(dve.reciprocal(inverse[:, :], total[:, :]))
                own.step(dve.tensor_tensor(k.comb[:, 0:E, :].rearrange("p e t -> p t e"), probs[:, :, :],
                                           wide(inverse[:, :], E), ALU.mult))

            @block.tensor
            def _(pe):
                for g in range(NBLK):
                    if g >= 2:
                        pe.wait_ge(low_ready if split else xnT_ready, g - 1)
                    if split:
                        pe.wait_ge(twice_ready, g + 1)
                    for t in range(TPB):
                        if normalise:
                            pe.wait_ge(xn_ready, g * TPB + t + 1)
                        if split:
                            tile = g * TPB + t
                            pe.transpose(psT[:, g % 2, 0, t * P:(t + 1) * P], (k.xn if normalise else src)[:, tile, 0:P], k.ident[:, :])
                            last = pe.transpose(psT[:, g % 2, 1, t * P:(t + 1) * P],
                                                twice[:, tile].rearrange("p a b -> p (a b)"), k.ident[:, :])
                            continue
                        for j in range(KC):
                            last = pe.transpose(psT[0:KP, g % 2, j, t * P:(t + 1) * P],
                                                (k.xn if normalise else src)[:, g * TPB + t, j * KP:(j + 1) * KP], k.ident[:, :])
                    last.then_inc(transposed, 1)
                if not R:
                    return
                pe.wait_ge(router_in, 16 * loads)
                if R.hidden:
                    for g in range(NBLK):
                        pe.wait_ge(low_ready, g + 1)
                        if g >= 2:
                            pe.wait_ge(hidT_ready, g - 1)
                        for n, (j, x) in enumerate(SPLIT):
                            last = pe.matmul(psH[0:KP, g % 2, :], w1[:, j, :], x[:, g * BLOCK:(g + 1) * BLOCK].bitcast(F32),
                                             start=(n == 0), stop=(n == 2))
                        last.then_inc(hidden_ready, 1)
                for t in range(TILES):
                    pe.wait_ge(hidT_ready if R.hidden else low_ready, t // TPB + 1)
                    cols = slice(t * P, (t + 1) * P)
                    terms = [(0, hidT[:, cols])] if R.hidden else [(j, x[:, cols].bitcast(F32)) for j, x in SPLIT]
                    for n, (j, x) in enumerate(terms):
                        last = pe.matmul(psR[:, t * E:(t + 1) * E], x, wr[:, j, :], start=(n == 0), stop=(n == len(terms) - 1))
                last.then_inc(logits_ready, 1)

            @block.scalar
            def _(act):
                for g in range(NBLK):
                    act.wait_ge(transposed, g + 1)
                    if split:
                        cols = slice(g * BLOCK, (g + 1) * BLOCK)
                        act.activation(k.x_high[:, cols], psT[:, g % 2, 0, :], ACT.Copy)
                        act.activation(k.x_tail[:, cols], psT[:, g % 2, 1, :], ACT.Copy).then_inc(xnT_ready, 1)
                        continue
                    act.activation(k.xnT[:, :, g * BLOCK:(g + 1) * BLOCK], psT[0:KP, g % 2], ACT.Copy).then_inc(xnT_ready, 1)
                if not R:
                    return
                if R.hidden:
                    act.wait_ge(router_in, 16 * loads)
                    for g in range(NBLK):
                        act.wait_ge(hidden_ready, g + 1)
                        act.activation(hidT[:, g * BLOCK:(g + 1) * BLOCK], psH[0:KP, g % 2, :], ACT.Gelu,
                                       bias=b1[:, 0:1]).then_inc(hidT_ready, 1)
                act.wait_ge(shifted, 1)
                act.activation(flat(probs), flat(logits), ACT.Exp if R.kind == "softmax" else ACT.Sigmoid).then_inc(probs_ready, 1)


class ExpertWeights:

    def __init__(self, phase, w_in_dram, w_out_dram, chunks, gated):
        sb, sem = phase.sbuf, phase.semaphore
        self.chunks, self.gated = chunks, gated
        self.count = w_in_dram.shape[0]
        self.w_in_dram, self.w_out_dram = w_in_dram, w_out_dram
        width = chunks * P * (2 if gated else 1)
        self.wa, self.wb = sb("wa", [P, 2, 2, width]), sb("wb", [P, 2, chunks, D])
        self.wa_high, self.wa_low = sb("wa_high", [P, 2, 2, width], F32R), sb("wa_low", [P, 2, 2, width], F32R)
        self.wb_split = sb("wb_split", [P, 2, chunks, 2, D], F32R)
        self.loaded = [sem("loaded_in0"), sem("loaded_in1")]
        self.split_in, self.split, self.own_in, self.own_out, self.turn = (
            sem("split_in"), sem("split"), sem("pool_own_in"), sem("pool_own_out"), sem("pool_turn"))

    def load(self, sp, e, slot):
        if not (isinstance(e, int) and e < 2):
            sp.wait_ge(self.split, e + -1)
        sp.dma_start(self.wa[:, slot], self.w_in_dram[ds(e, 1)].rearrange("o p a b -> p (o a) b")).then_inc(self.loaded[slot], 16)
        sp.dma_start(self.wb[:, slot], self.w_out_dram[ds(e, 1)].rearrange("o p a b -> p (o a) b")).then_inc(self.loaded[slot], 16)

    def split_expert(self, pool, e, slot, turn):
        wa_high, wb_high = self.wa_high[:, slot], self.wb_split[:, slot, :, 0, :]
        pool.wait_ge(self.loaded[slot], turn * 32)
        pool.sem_inc(self.turn, 1)
        pool.tensor_scalar(wa_high, self.wa[:, slot], *SAME).then_inc(self.own_in, 1)
        pool.wait_ge(self.own_in, e + 1)
        pool.tensor_tensor(self.wa_low[:, slot], self.wa[:, slot], wa_high.bitcast(F32), ALU.subtract).then_inc(self.split_in, 1)
        pool.wait_ge(self.split_in, e + 1)
        pool.sem_inc(self.turn, 1)
        pool.tensor_scalar(wb_high, self.wb[:, slot], *SAME).then_inc(self.own_out, 1)
        pool.wait_ge(self.own_out, e + 1)
        pool.tensor_tensor(self.wb_split[:, slot, :, 1, :], self.wb[:, slot], wb_high.bitcast(F32), ALU.subtract).then_inc(self.split, 1)

    def begin_load(self, sp):
        for e in range(min(2, self.count)):
            self.load(sp, e, e)

    def begin_split(self, pool):
        self.split_expert(pool, 0, 0, 1)


def experts_phase(nc, k, name, target, weights, bias_dram=None, out_bias_dram=None, weighted=True):
    count, chunks, gated = weights.count, weights.chunks, weights.gated
    wa_high, wa_low, wb_split, split_in, split = weights.wa_high, weights.wa_low, weights.wb_split, weights.split_in, weights.split
    F = chunks * P
    HID_SLOTS = 4
    START = 8
    with Phase(nc, name) as phase:
        sb, ps, sem = phase.sbuf, phase.psum, phase.semaphore
        ba = sb("ba", [P, 2, chunks])
        bo = sb("bo", [P, 2, D])
        weight = sb("weight", [P, 2, TILES])
        hid = sb("hid", [P, HID_SLOTS, BLOCK])
        hid_high, hid_low = sb("hid_high", [P, 2, chunks, BLOCK], F32R), sb("hid_low", [P, 2, chunks, BLOCK], F32R)
        silu = sb("silu", [P, 2, BLOCK])
        psA = ps("psA", [P, 4, BANK])
        psD = ps("psD", [P, TPB, BANK])
        loaded = [sem("loaded0"), sem("loaded1")]
        chunk_ready, high_ready = sem("chunk_ready"), sem("high_ready")
        features, silu_ready, hidden, down, added, own_sem = (
            sem("features"), sem("silu_ready"), sem("hidden"), sem("down"), sem("added"), sem("own"))
        nloads = (bias_dram is not None) + (out_bias_dram is not None)
        pairs, odd = count // 2, count % 2

        def each_expert(eng, body):
            if pairs:
                for e in range(2):
                    body(e, e, 1)
                with eng.Fori(0, pairs - 1) as i:
                    for e2 in range(2):
                        body((i + 1) * 2 + e2, e2, i + 2)
            if odd:
                body(2 * pairs, 0, pairs + 1)

        def pipelined(eng, up, down, own=None, per=0):
            def run(steps, before):
                for step in steps:
                    up(*step)
                    if before:
                        down(*before)
                    before = step
                return before

            def pair(it):
                return [(it * 2 + e2, e2, b, it + 1) for e2 in range(2) for b in range(NBLK)]

            before = None
            if pairs:
                before = run(pair(0), None)
                with eng.Fori(0, pairs - 1) as i:
                    if own:
                        own.enter(i, per)
                    run(pair(i + 1), ((i + 1) * 2 + -1, 1, NBLK - 1, i + 1))
                if own:
                    own.leave(pairs - 1)
                before = pair(pairs - 1)[-1]
            if odd:
                before = run([(2 * pairs, 0, b, pairs + 1) for b in range(NBLK)], before)
            down(*before)

        with nc.Block() as block:
            @block.sync
            def _(sp):
                def load(e, e2, turn):
                    if not (isinstance(e, int) and e < 2):
                        weights.load(sp, e, e2)
                    if bias_dram is not None:
                        if not (isinstance(e, int) and e < 2):
                            sp.wait_ge(down, START - 4 + e * NBLK)
                        sp.dma_start(ba[:, e2], bias_dram[ds(e, 1)].rearrange("o p a -> p (o a)")).then_inc(loaded[e2], 16)
                    if out_bias_dram is not None:
                        if not (isinstance(e, int) and e < 2):
                            sp.wait_ge(added, START - 2 * NBLK + e * 2 * NBLK)
                        sp.dma_start(bo[:, e2], out_bias_dram[ds(e, 1)].rearrange("o b -> (o b)").partition_broadcast(P))\
                          .then_inc(loaded[e2], 16)
                sp.wait_ge(down, START)
                sp.wait_ge(added, START)
                each_expert(sp, load)

            @block.gpsimd
            def _(pool):
                pool.wait_ge(down, START)

                def split_next(e, e2, turn):
                    if isinstance(e, int) and e == 0:
                        return
                    if not (isinstance(e, int) and e < 2):
                        pool.wait_ge(down, START - 4 + e * NBLK)
                    weights.split_expert(pool, e, e2, turn)
                each_expert(pool, split_next)

            @block.tensor
            def _(pe):
                pe.sem_inc(down, START)
                pe.wait_ge(hidden, START)
                pe.wait_ge(chunk_ready, START)
                pe.wait_ge(added, START)

                def up(e, e2, b, turn):
                    if b == 0:
                        pe.wait_ge(split_in, e + 1)
                    for f in range(chunks):
                        n = (e * NBLK + b) * chunks + f
                        local = b * chunks + f
                        if gated:
                            slot = 2 * ((e2 * NBLK * chunks + local) % 2)
                            pe.wait_ge(chunk_ready, START - 1 + n)
                        else:
                            slot = (e2 * NBLK * chunks + local) % 4
                            pe.wait_ge(chunk_ready, START - 3 + n)
                        for part in range(2 if gated else 1):
                            last = split_product(pe, psA[:, slot + part, :], wa_high[:, e2], wa_low[:, e2], k,
                                                 slice(part * F + f * P, part * F + (f + 1) * P), slice(b * BLOCK, (b + 1) * BLOCK))
                        last.then_inc(features, 1)

                def go_down(e, e2, b, turn):
                    s = e * NBLK + b
                    pe.wait_ge(hidden, START + (s + 1) * chunks)
                    if b == 0:
                        pe.wait_ge(split, e + 1)
                    for t in range(TPB):
                        if t % 2 == 0:
                            pe.wait_ge(added, START - 1 + 2 * s + t // 2)
                        for f in range(chunks):
                            cols = slice(t * P, (t + 1) * P)
                            pe.matmul(psD[:, t, 0:2 * D], hid_high[:, b % 2, f, cols], wb_split[:, e2, f].rearrange("p a b -> p (a b)"),
                                      start=(f == 0), stop=False)
                            last = pe.matmul(psD[:, t, 0:D], hid_low[:, b % 2, f, cols], wb_split[:, e2, f, 0, :],
                                             start=False, stop=(f == chunks - 1))
                    last.then_inc(down, 1)

                pipelined(pe, up, go_down)

            @block.scalar
            def _(act):
                if not gated:
                    act.sem_inc(chunk_ready, START)
                act.wait_ge(down, START)
                act.wait_ge(hidden, START)
                act.wait_ge(chunk_ready, START)

                def activate(e, e2, turn):
                    if bias_dram is not None:
                        act.wait_ge(loaded[e2], turn * 16 * nloads)
                    for b in range(NBLK):
                        s = e * NBLK + b
                        for f in range(chunks):
                            n, local = s * chunks + f, (e2 * NBLK + b) * chunks + f
                            act.wait_ge(features, n + 1)
                            if gated:
                                act.wait_ge(chunk_ready, START - 1 + n)
                                act.activation(silu[:, local % 2, :], psA[:, 2 * (local % 2), :], ACT.Silu).then_inc(silu_ready, 1)
                            else:
                                act.wait_ge(hidden, START + 1 - HID_SLOTS + n)
                                act.activation(hid[:, local % HID_SLOTS, :], psA[:, local % 4, :], ACT.Gelu,
                                               bias=ba[:, e2, f:f + 1]).then_inc(chunk_ready, 1)
                            if f == 0:
                                act.wait_ge(down, START - 1 + s)
                            act.wait_ge(chunk_ready, START + n + 1)
                            act.activation(hid_high[:, b % 2, f, :], hid[:, local % HID_SLOTS, :], ACT.Copy).then_inc(high_ready, 1)
                each_expert(act, activate)

            @block.vector
            def _(dve):
                dve.sem_inc(hidden, START)
                if gated:
                    dve.sem_inc(chunk_ready, START)
                dve.sem_inc(added, START)
                dve.wait_ge(down, START)
                dve.wait_ge(hidden, START)
                dve.wait_ge(added, START)
                own = Own(dve, own_sem)
                comb = flat(k.comb)

                def products(e, e2, b, turn):
                    s = e * NBLK + b
                    for f in range(chunks):
                        n, local = s * chunks + f, (e2 * NBLK + b) * chunks + f
                        if gated:
                            dve.wait_ge(silu_ready, n + 1)
                            dve.wait_ge(hidden, START + 1 - HID_SLOTS + n)
                            dve.tensor_tensor(hid[:, local % HID_SLOTS, :], silu[:, local % 2, :], psA[:, 2 * (local % 2) + 1, :],
                                              ALU.mult).then_inc(chunk_ready, 1)
                        if f:
                            low(n - 1 if isinstance(n, int) else n + -1, b, f - 1, (local - 1) % HID_SLOTS)
                    low(n, b, chunks - 1, local % HID_SLOTS)

                def low(n, b, f, slot):
                    dve.wait_ge(high_ready, n + 1)
                    dve.tensor_tensor(hid_low[:, b % 2, f, :], hid[:, slot, :], hid_high[:, b % 2, f, :].bitcast(F32),
                                      ALU.subtract).then_inc(hidden, 1)

                def add(e, e2, b, turn):
                    s = e * NBLK + b
                    if b == 0 and weighted:
                        own.step(dve.tensor_copy(weight[:, e2, :], comb[:, ds(e * TILES, TILES)]))
                    if b == 0 and out_bias_dram is not None:
                        dve.wait_ge(loaded[e2], turn * 16 * nloads)
                    dve.wait_ge(down, START + s + 1)
                    dve.wait_ge(added, START + 2 * s)
                    if out_bias_dram is not None:
                        for t in range(TPB):
                            tile = b * TPB + t
                            if weighted:
                                last = dve.scalar_tensor_tensor(out=target[:, tile, :], in0=bo[:, e2, :], scalar=weight[:, e2, tile:tile + 1],
                                                                in1=target[:, tile, :], op0=ALU.mult, op1=ALU.add)
                            else:
                                last = dve.tensor_tensor(target[:, tile, :], bo[:, e2, :], target[:, tile, :], ALU.add)
                        own.step(last)
                    for pair in range(2):
                        for half in range(2):
                            for t in range(2 * pair, 2 * pair + 2):
                                tile = b * TPB + t
                                part = psD[:, t, half * D:(half + 1) * D]
                                if weighted:
                                    last = dve.scalar_tensor_tensor(out=target[:, tile, :], in0=part, scalar=weight[:, e2, tile:tile + 1],
                                                                    in1=target[:, tile, :], op0=ALU.mult, op1=ALU.add)
                                else:
                                    last = dve.tensor_tensor(target[:, tile, :], part, target[:, tile, :], ALU.add)
                            if half == 0:
                                own.step(last)
                        last.then_inc(added, 1)

                pipelined(dve, products, add, own, 2 * (NBLK * (2 + (out_bias_dram is not None)) + int(weighted)))


HEADS0, HD0 = 6, 32
SCALE0 = HD0 ** -0.5


def values_program(pe, psV, w, out_ready, freed, tiles=TILES, xnT=None, n=D):
    for t in range(0, tiles, 2):
        if t >= 4:
            pe.wait_ge(freed, t // 2 - 1)
        for u in (t, t + 1):
            for j in range(KC):
                last = pe.matmul(psV[:, (t // 2) % 2, (u - t) * n:(u - t + 1) * n], xnT[:, j, u * P:(u + 1) * P], w[:, j, :],
                                 start=(j == 0), stop=(j == KC - 1))
        last.then_inc(out_ready, 1)


def attention0_phase(nc, k, wqk_dram, wv_dram, wo_dram, anchor_w, anchors, lam):
    STEPS = HEADS0 * BATCH
    Q3 = 3 * HD0
    VR = 2 * HD0 + 1
    SLOTS = 4
    with Phase(nc, "a0_") as phase:
        sb, ps, sem = phase.sbuf, phase.psum, phase.semaphore
        wv, wv_high, wv_low = sb("wv", [P, 2, D]), sb("wv_high", [P, 2, D], F32R), sb("wv_low", [P, 2, D], F32R)
        wqk = sb("wqk", [P, 2, 2 * Q3])
        wqk_high, wqk_low = sb("wqk_high", [P, 2, 2 * Q3], F32R), sb("wqk_low", [P, 2, 2 * Q3], F32R)
        wo = sb("wo", [VR, D + 1])
        values = sb("values", [P, TILES, D])
        aw, an, lm = sb("aw", [Q3, HEADS0, 6]), sb("an", [Q3, HEADS0, 6]), sb("lm", [Q3, HEADS0])
        anchor, head_anchor = sb("anchor", [Q3, HEADS0]), sb("head_anchor", [Q3, 1])
        q3, k3 = sb("q3", [Q3 + 1, 2, SEQ], F32R), sb("k3", [Q3 + 1, 2, SEQ], F32R)
        v2 = sb("v2", [P, 2, TPS, VR], F32R)
        shift, top, peak, bias = (sb(n, [P, TPS]) for n in ("shift", "top", "peak", "bias"))
        tops = sb("tops", [P, 2, TPS])
        bias_column = sb("bias_column", [P, TPS, Q3 + 1], F32R)
        expo = sb("expo", [P, SLOTS, SEQ])
        expo_high, expo_low = sb("expo_high", [P, SLOTS, SEQ], F32R), sb("expo_low", [P, SLOTS, SEQ], F32R)
        ident = sb("ident", [P, P], F32R)
        outT = sb("outT", [VR, 2, BLOCK])
        inverse = sb("inverse", [P, TPS])
        psX = ps("psX", [P, 4, BANK])
        psN = ps("psN", [P, 2, BANK])
        psO = ps("psO", [P, 2, BANK])
        names = ("setup v_in v_split v_ready v_copied anchor_in anchor_ready own pool_own pool_turn wqk_in wqk_split wo_in "
                 "proj_ready q_high q_low k_high k_low shift_ready shift_copied nat_ready top_ready column_ready row_ready "
                 "rows_copied v2_ready scores_ready exp_ready high_ready low_ready weighed out_copied w_ready w_added").split()
        s = {n: sem(n) for n in names}

        def wait(eng, name, value):
            if not (isinstance(value, int) and value <= 0):
                eng.wait_ge(s[name], value)

        def all_heads(eng, head, own=None, per=0):
            head(0)
            with eng.Fori(0, HEADS0 - 2) as i:
                if own:
                    own.enter(i, per)
                head(i + 1)
            if own:
                own.leave(HEADS0 - 2)
            head(HEADS0 - 1)

        def last(h, b):
            return isinstance(h, int) and h == HEADS0 - 1 and b == 1

        with nc.Block() as block:
            @block.sync
            def _(sp):
                sp.dma_start(wv[:, :, :], wv_dram).then_inc(s["v_in"], 16)
                sp.dma_start(wqk[:, :, :], wqk_dram[0]).then_inc(s["wqk_in"], 16)
                for part in range(3):
                    sp.dma_start(aw[part * HD0:(part + 1) * HD0], anchor_w).then_inc(s["anchor_in"], 16)
                sp.dma_start(an[:, :, :], anchors.rearrange("h e -> (h e)").partition_broadcast(Q3)
                             .rearrange("p (h e) -> p h e", e=6)).then_inc(s["anchor_in"], 16)
                sp.dma_start(lm[:, :], lam.partition_broadcast(Q3)).then_inc(s["anchor_in"], 16)
                wait(sp, "setup", 1)

                def head(h):
                    wait(sp, "w_ready", h * 8)
                    sp.dma_start(wo[0:2 * HD0, 0:D], wo_dram[ds(h, 1)].rearrange("o p d -> (o p) d")).then_inc(s["wo_in"], 16)
                    if not (isinstance(h, int) and h == HEADS0 - 1):
                        wait(sp, "wqk_split", h + 1)
                        sp.dma_start(wqk[:, :, :], wqk_dram[ds(h + 1, 1)].rearrange("o p a b -> p (o a) b")).then_inc(s["wqk_in"], 16)
                all_heads(sp, head)

            @block.tensor
            def _(pe):
                def project(n, nb, h, part, blk):
                    if part == 0:
                        if blk == 0:
                            wait(pe, "wqk_split", h + 1)
                            wait(pe, "rows_copied", n)
                    elif blk == 0:
                        wait(pe, "q_low", 2 * n + 1)
                    else:
                        wait(pe, "shift_copied", n + 1)
                    at = nb * SEQ + blk * BLOCK
                    split_product(pe, psN[0:Q3, blk, :], wqk_high, wqk_low, k, slice(part * Q3, (part + 1) * Q3),
                                  slice(at, at + BLOCK)).then_inc(s["proj_ready"], 1)

                def shifts(n, nb):
                    wait(pe, "q_low", 2 * n + 2)
                    wait(pe, "anchor_ready", n + 2)
                    for t in range(TPS):
                        done = pe.matmul(psN[:, 1, t:t + 1], q3[0:Q3, nb, t * P:(t + 1) * P].bitcast(F32), head_anchor[:, :], start=True, stop=True)
                    done.then_inc(s["shift_ready"], 1)

                def natural(n, nb, t):
                    for blk in range(2):
                        if t == 0:
                            wait(pe, "k_low", 2 * n + 1 + blk)
                        else:
                            wait(pe, "top_ready", (n * TPS + t) * 2 + blk - 1)
                        pe.matmul(psN[:, blk, :], q3[0:Q3, nb, t * P:(t + 1) * P], k3[0:Q3, nb, blk * BLOCK:(blk + 1) * BLOCK],
                                  start=True, stop=True).then_inc(s["nat_ready"], 1)

                def bias_row(n):
                    wait(pe, "column_ready", n + 1)
                    for t in range(TPS):
                        done = pe.matmul(psN[0:Q3 + 1, t // TPB, (t % TPB) * P:(t % TPB + 1) * P], bias_column[:, t, :],
                                         ident[:, :], start=True, stop=True)
                    done.then_inc(s["row_ready"], 1)

                def scores(n, b, kt):
                    if kt == 0:
                        wait(pe, "rows_copied", n + 1)
                    wait(pe, "exp_ready", n * TPS + kt - 1)
                    for blk in range(2):
                        done = pe.matmul(psX[:, (kt % 2) * 2 + blk, :], k3[:, b, kt * P:(kt + 1) * P], q3[:, b, blk * BLOCK:(blk + 1) * BLOCK],
                                         start=True, stop=True)
                    done.then_inc(s["scores_ready"], 1)

                def weigh(n, b, kt):
                    if kt == 0:
                        wait(pe, "v2_ready", n + 1)
                        wait(pe, "w_added", n * 4)
                    wait(pe, "low_ready", n * TPS + kt + 1)
                    for blk in range(2):
                        for nth, part in enumerate((expo_high, expo_low)):
                            done = pe.matmul(psO[0:VR, blk, :], v2[:, b, kt, :], part[:, kt % SLOTS, blk * BLOCK:(blk + 1) * BLOCK],
                                             start=(kt == 0 and nth == 0), stop=(kt == TPS - 1 and nth == 1))
                    done.then_inc(s["weighed"], 1)

                def project_out(n, h):
                    wait(pe, "wo_in", (h + 1) * 16)
                    for pair in range(4):
                        if pair < 2:
                            wait(pe, "out_copied", n * 2 + 1 + pair)
                        else:
                            wait(pe, "w_added", n * 4 + pair - 1)
                        for t in range(2):
                            col = ((pair % 2) * 2 + t) * P
                            done = pe.matmul(psO[:, pair % 2, t * (D + 1):(t + 1) * (D + 1)], outT[:, pair // 2, col:col + P], wo[:, :],
                                             start=True, stop=True)
                        done.then_inc(s["w_ready"], 1)

                def head(h):
                    for b in range(BATCH):
                        n, nb, nh = h * 2 + b, 1 - b, h + b
                        ahead = not last(h, b)
                        for what in ("q0 q1 s2 out s3 k0 w0 sh k1 w1 n0 s4 n1 n2 s5 n3 w2 n4 s6 n5 w3 n6 s7 n7 w4 w5 row w6 s0 s1 w7").split():
                            if what == "out":
                                if not (isinstance(n, int) and n == 0):
                                    project_out(n - 1 if isinstance(n, int) else n + -1, (h - 1 if isinstance(h, int) else h + -1) if b == 0 else h)
                            elif what[0] == "w":
                                weigh(n, b, int(what[1]))
                            elif what in ("s0", "s1"):
                                if ahead:
                                    scores(n + 1, nb, int(what[1]))
                            elif what[0] == "s" and what != "sh":
                                scores(n, b, int(what[1]))
                            elif not ahead:
                                continue
                            elif what[0] == "n":
                                natural(n + 1, nb, int(what[1]))
                            elif what == "sh":
                                shifts(n + 1, nb)
                            elif what == "row":
                                bias_row(n + 1)
                            else:
                                project(n + 1, nb, nh, int(what[0] == "k"), int(what[1]))

                wait(pe, "v_split", 1)
                wait(pe, "setup", 1)
                for n in range(TILES // 2):
                    if n >= 4:
                        wait(pe, "v_copied", n - 3)
                    for u in range(2):
                        cols = slice((2 * n + u) * P, (2 * n + u + 1) * P)
                        passes = ((k.x_high, wv_high, 0), (k.x_low, wv_high, 0), (k.x_high, wv_low, 0), (k.x_tail, wv_high, 1), (k.x_tail, wv_low, 1))
                        for nth, (x, w, chunk) in enumerate(passes):
                            done = pe.matmul(psX[:, n % 4, u * D:(u + 1) * D], x[:, cols], w[:, chunk, :], start=(nth == 0), stop=(nth == 4))
                    done.then_inc(s["v_ready"], 1)
                project(0, 0, 0, 0, 0)
                project(0, 0, 0, 0, 1)
                project(0, 0, 0, 1, 0)
                shifts(0, 0)
                project(0, 0, 0, 1, 1)
                for t in range(TPS):
                    natural(0, 0, t)
                bias_row(0)
                wait(pe, "v_copied", TILES // 2)
                for kt in range(2):
                    scores(0, 0, kt)
                all_heads(pe, head)
                project_out(STEPS - 1, HEADS0 - 1)

            @block.scalar
            def _(act):
                def high(n, nb, target, part):
                    for blk in range(2):
                        wait(act, "proj_ready", 4 * n + 2 * part + blk + 1)
                        act.activation(target[0:Q3, nb, blk * BLOCK:(blk + 1) * BLOCK], psN[0:Q3, blk, :], ACT.Copy)\
                           .then_inc(s["k_high" if part else "q_high"], 1)

                def row(n, nb):
                    wait(act, "row_ready", n + 1)
                    act.activation(q3[Q3:Q3 + 1, nb, :], psN[Q3:Q3 + 1, :, :].rearrange("p a b -> p (a b)"), ACT.Copy)\
                       .then_inc(s["rows_copied"], 1)

                def copy_out(n):
                    for half in range(2):
                        wait(act, "weighed", (n + 1) * TPS)
                        wait(act, "w_ready", n * 4)
                        act.activation(outT[:, half, :], psO[0:VR, half, :], ACT.Copy).then_inc(s["out_copied"], 1)

                def exponential(n, kt):
                    u = n * TPS + kt
                    wait(act, "scores_ready", u + 1)
                    wait(act, "low_ready", u - SLOTS + 1)
                    act.activation(expo[:, kt % SLOTS, :], psX[:, (kt % 2) * 2:(kt % 2) * 2 + 2, :].rearrange("p a b -> p (a b)"), ACT.Exp,
                                   scale=SCALE0).then_inc(s["exp_ready"], 1)
                    wait(act, "exp_ready", u + 1)
                    wait(act, "weighed", u - SLOTS + 1)
                    act.activation(expo_high[:, kt % SLOTS, :], expo[:, kt % SLOTS, :], ACT.Copy).then_inc(s["high_ready"], 1)

                def head(h):
                    for b in range(BATCH):
                        n, nb = h * 2 + b, 1 - b
                        ahead = not last(h, b)
                        for kt in range(TPS):
                            exponential(n, kt)
                            if kt == 0 and not (isinstance(n, int) and n == 0):
                                copy_out(n + -1 if not isinstance(n, int) else n - 1)
                            if kt == 0 and ahead:
                                high(n + 1, nb, q3, 0)
                            if kt == 2 and ahead:
                                high(n + 1, nb, k3, 1)
                        if ahead:
                            row(n + 1, nb)

                for n in range(TILES // 2):
                    wait(act, "v_ready", n + 1)
                    act.activation(values[:, 2 * n:2 * n + 2, :].rearrange("p a b -> p (a b)"), psX[:, n % 4, 0:2 * D],
                                   ACT.Copy).then_inc(s["v_copied"], 1)
                high(0, 0, q3, 0)
                high(0, 0, k3, 1)
                row(0, 0)
                all_heads(act, head)
                copy_out(STEPS - 1)

            @block.vector
            def _(dve):
                own = Own(dve, s["own"])

                def prepare(n, nb, h, before=None):
                    source = values[:, nb * TPS:(nb + 1) * TPS, ds(h * HD0, HD0)]
                    wait(dve, "weighed", (n - 1) * TPS)
                    own.step(dve.tensor_copy(v2[:, nb, :, 0:HD0], source))
                    dve.tensor_tensor(v2[:, nb, :, HD0:2 * HD0], source, v2[:, nb, :, 0:HD0].bitcast(F32), ALU.subtract).then_inc(s["v2_ready"], 1)
                    wait(dve, "shift_copied", n)
                    dve.tensor_copy(head_anchor[:, :], anchor[:, ds(h, 1)]).then_inc(s["anchor_ready"], 1)
                    for part, target, rows in ((0, q3, slice(2 * HD0, 3 * HD0)), (1, k3, slice(HD0, 2 * HD0))):
                        name = "k" if part else "q"
                        for blk in range(2):
                            cols = slice(blk * BLOCK, (blk + 1) * BLOCK)
                            wait(dve, name + "_high", 2 * n + blk + 1)
                            dve.tensor_tensor(target[rows, nb, cols], psN[rows, blk, :], target[rows, nb, cols].bitcast(F32),
                                              ALU.subtract).then_inc(s[name + "_low"], 1)
                            if not blk and not part and before is not None:
                                add(before, nb)
                            if part and not blk:
                                wait(dve, "shift_ready", n + 1)
                                wait(dve, "column_ready", n)
                                dve.tensor_copy(shift[:, :], psN[:, 1, 0:TPS]).then_inc(s["shift_copied"], 1)

                def maxima(n):
                    for t in range(TPS):
                        for blk in range(2):
                            wait(dve, "nat_ready", (n * TPS + t) * 2 + blk + 1)
                            dve.tensor_reduce(tops[:, blk, t:t + 1], psN[:, blk, :], AXX, ALU.max).then_inc(s["top_ready"], 1)
                    wait(dve, "top_ready", (n + 1) * TPS * 2)
                    own.step(dve.tensor_tensor(top[:, :], tops[:, 0, :], tops[:, 1, :], ALU.max))
                    wait(dve, "shift_copied", n + 1)
                    own.step(dve.scalar_tensor_tensor(out=peak[:, :], in0=top[:, :], scalar=SCALE0, in1=shift[:, :], op0=ALU.mult, op1=ALU.add))
                    own.step(dve.tensor_tensor(bias[:, :], shift[:, :], peak[:, :], ALU.subtract))
                    wait(dve, "row_ready", n)
                    dve.tensor_scalar(bias_column[:, :, Q3], bias[:, :], 1.0 / SCALE0, None, ALU.mult).then_inc(s["column_ready"], 1)

                def add(n, b):
                    for pair in range(4):
                        bank = psO[:, pair % 2, 0:2 * (D + 1)].rearrange("p (t d) -> p t d", d=D + 1)
                        wait(dve, "w_ready", n * 4 + pair + 1)
                        wait(dve, "w_added", n * 4 + pair)
                        own.step(dve.reciprocal(inverse[:, 2 * pair:2 * pair + 2], bank[:, :, D]))
                        for t in range(2):
                            tile = b * TPS + 2 * pair + t
                            done = dve.scalar_tensor_tensor(out=k.h[:, tile, :], in0=bank[:, t, 0:D], scalar=inverse[:, 2 * pair + t:2 * pair + t + 1],
                                                            in1=k.h[:, tile, :], op0=ALU.mult, op1=ALU.add)
                        done.then_inc(s["w_added"], 1)

                def head(h):
                    for b in range(BATCH):
                        n = h * 2 + b
                        before = (None if n == 0 else n - 1) if isinstance(n, int) else n + -1
                        if not last(h, b):
                            prepare(n + 1, 1 - b, h + b, before)
                            maxima(n + 1)
                        else:
                            add(before, 1 - b)

                ones = expo[:, 0, :]
                own.step(dve.memset(ones, 1.0))
                own.step(dve.memset(wo[:, :], 0.0))
                dve.memset(wo[2 * HD0:VR, D:D + 1], 1.0)
                dve.tensor_copy(ident[:, :], k.ident[:, :])
                dve.tensor_scalar(flat(bias_column), ones[:, 0:TPS * (Q3 + 1)], 0.0, None, ALU.mult)
                for b in range(BATCH):
                    dve.tensor_copy(k3[Q3:Q3 + 1, b, :], ones[Q3:Q3 + 1, :])
                dve.tensor_copy(v2[:, :, :, 2 * HD0], ones[:, 0:BATCH * TPS].rearrange("p (a b) -> p a b", b=TPS)).then_inc(s["setup"], 1)
                wait(dve, "anchor_in", 80)
                own.step(dve.tensor_tensor(aw[:, :, :], aw[:, :, :], an[:, :, :], ALU.mult))
                own.step(dve.tensor_reduce(anchor[:, :], aw[:, :, :], AXX, ALU.add))
                own.step(dve.tensor_tensor(anchor[:, :], anchor[:, :], lm[:, :], ALU.mult))
                dve.memset(anchor[HD0:2 * HD0, :], 0.0).then_inc(s["anchor_ready"], 1)
                wait(dve, "anchor_ready", 1)
                wait(dve, "v_copied", TILES // 2)
                prepare(0, 0, 0)
                maxima(0)
                all_heads(dve, head, own, 2 * (1 + 3 + 4))
                add(STEPS - 1, 1)

            @block.gpsimd
            def _(pool):
                def split_wqk(h):
                    wait(pool, "wqk_in", (h + 1) * 16)
                    wait(pool, "proj_ready", 8 * h)
                    pool.sem_inc(s["pool_turn"], 1)
                    pool.tensor_scalar(wqk_high[:, :, :], wqk[:, :, :], *SAME).then_inc(s["pool_own"], 1)
                    wait(pool, "pool_own", h + 2)
                    pool.tensor_tensor(wqk_low[:, :, :], wqk[:, :, :], wqk_high[:, :, :].bitcast(F32), ALU.subtract).then_inc(s["wqk_split"], 1)

                def head(h):
                    for b in range(BATCH):
                        n = h * 2 + b
                        for kt in range(TPS):
                            wait(pool, "high_ready", n * TPS + kt + 1)
                            pool.tensor_tensor(expo_low[:, kt % SLOTS, :], expo[:, kt % SLOTS, :], expo_high[:, kt % SLOTS, :].bitcast(F32),
                                               ALU.subtract).then_inc(s["low_ready"], 1)
                            if b == 0 and kt == 4 and not (isinstance(h, int) and h == HEADS0 - 1):
                                split_wqk(h + 1)

                wait(pool, "v_in", 16)
                pool.tensor_scalar(wv_high[:, :, :], wv[:, :, :], *SAME).then_inc(s["pool_own"], 1)
                wait(pool, "pool_own", 1)
                pool.tensor_tensor(wv_low[:, :, :], wv[:, :, :], wv_high[:, :, :].bitcast(F32), ALU.subtract).then_inc(s["v_split"], 1)
                split_wqk(0)
                all_heads(pool, head)


def attention1_phase(nc, k, w_dram, qk_bias, v_bias, decay_dram):
    PAD = 3 * P
    with Phase(nc, "a1_") as phase:
        sb, ps, sem = phase.sbuf, phase.psum, phase.semaphore
        w = sb("w", [KP, KC, 3, D])
        qkb, vb = sb("qkb", [KP, 2, KC]), sb("vb", [P, D])
        decay = sb("decay", [P, PAD + SEQ])
        values = sb("values", [P, TILES, D])
        qkT = sb("qkT", [KP, 2, KC, SEQ])
        scores = sb("scores", [P, 2, TPS, BLOCK])
        psQ, psS, psO = ps("psQ", [P, 2, BANK]), ps("psS", [P, 2, BANK]), ps("psO", [P, 2, 2, BANK])
        names = "loaded v_ready v_copied qk_ready qk_copied scores_ready scores_copied out_ready out_added".split()
        s = {n: sem(n) for n in names}
        blocks = SEQ // BLOCK
        keys = [(sb_ + 1) * TPB for sb_ in range(blocks)]
        first = [sum(keys[:n]) for n in range(blocks)]
        SPB, QPB = sum(keys), 2 * KC * blocks

        with nc.Block() as block:
            @block.sync
            def _(sp):
                sp.dma_start(w[:, :, :, :], w_dram).then_inc(s["loaded"], 16)
                sp.dma_start(qkb[:, :, :], qk_bias).then_inc(s["loaded"], 16)
                sp.dma_start(vb[:, :], v_bias.partition_broadcast(P)).then_inc(s["loaded"], 16)
                sp.dma_start(decay[:, :], decay_dram).then_inc(s["loaded"], 16)

            @block.tensor
            def _(pe):
                pe.wait_ge(s["loaded"], 64)
                values_program(pe, psQ, w[:, :, 2, :], s["v_ready"], s["v_copied"], xnT=k.xnT)
                pe.wait_ge(s["v_copied"], TILES // 2)
                xnT = k.xnT
                with pe.Fori(0, BATCH) as b:
                    for n in range(QPB):
                        part, m, blk = n // (KC * blocks), n // blocks % KC, n % blocks
                        pe.wait_ge(s["qk_copied"], b * QPB + max(n - 1, 0))
                        for j in range(KC):
                            last = pe.matmul(psQ[0:KP, n % 2, :], w[:, j, part, m * KP:(m + 1) * KP],
                                             xnT[:, j, ds(b * SEQ + blk * BLOCK, BLOCK)], start=(j == 0), stop=(j == KC - 1))
                        last.then_inc(s["qk_ready"], 1)
                    pe.wait_ge(s["qk_copied"], b * QPB + QPB)

                    def weigh(q):
                        pe.wait_ge(s["scores_copied"], b * SPB + first[q] + keys[q])
                        pe.wait_ge(s["out_added"], b * blocks + max(q - 1, 0))
                        for t in range(TPB):
                            seen = q * TPB + t + 1
                            for kt in range(seen):
                                last = pe.matmul(psO[:, q % 2, t // 2, (t % 2) * D:(t % 2 + 1) * D], scores[:, q % 2, kt, t * P:(t + 1) * P],
                                                 flat(values)[:, ds((b * TPS + kt) * D, D)], start=(kt == 0), stop=(kt == seen - 1))
                        last.then_inc(s["out_ready"], 1)

                    for q in range(blocks):
                        for kt in range(keys[q]):
                            n = first[q] + kt
                            pe.wait_ge(s["scores_copied"], b * SPB + max(n - 1, 0))
                            for j in range(KC):
                                last = pe.matmul(psS[:, n % 2, :], qkT[:, 1, j, kt * P:(kt + 1) * P],
                                                 qkT[:, 0, j, q * BLOCK:(q + 1) * BLOCK], start=(j == 0), stop=(j == KC - 1))
                            last.then_inc(s["scores_ready"], 1)
                        if q:
                            weigh(q - 1)
                    weigh(blocks - 1)

            @block.scalar
            def _(act):
                act.wait_ge(s["loaded"], 64)
                with act.Fori(0, BATCH) as b:
                    for n in range(QPB):
                        part, m, blk = n // (KC * blocks), n // blocks % KC, n % blocks
                        act.wait_ge(s["qk_ready"], b * QPB + n + 1)
                        act.activation(qkT[:, part, m, blk * BLOCK:(blk + 1) * BLOCK], psQ[0:KP, n % 2, :], ACT.Identity,
                                       bias=qkb[:, part, m:m + 1]).then_inc(s["qk_copied"], 1)

            @block.vector
            def _(dve):
                dve.wait_ge(s["loaded"], 64)
                for n in range(TILES // 2):
                    dve.wait_ge(s["v_ready"], n + 1)
                    dve.tensor_tensor(values[:, 2 * n:2 * n + 2, :], psQ[:, n % 2, 0:2 * D].rearrange("p (a b) -> p a b", b=D),
                                      across(vb[:, :], 2), ALU.add).then_inc(s["v_copied"], 1)
                h = flat(k.h)
                with dve.Fori(0, BATCH) as b:
                    def add(q):
                        dve.wait_ge(s["out_ready"], b * blocks + q + 1)
                        for t in range(TPB):
                            at = ds((b * TPS + q * TPB + t) * D, D)
                            last = dve.tensor_tensor(h[:, at], psO[:, q % 2, t // 2, (t % 2) * D:(t % 2 + 1) * D], h[:, at], ALU.add)
                        last.then_inc(s["out_added"], 1)

                    for q in range(blocks):
                        dve.wait_ge(s["out_ready"], b * blocks + max(q - 1, 0))
                        for kt in range(keys[q]):
                            n = first[q] + kt
                            dve.wait_ge(s["scores_ready"], b * SPB + n + 1)
                            at = PAD + q * BLOCK - kt * P
                            dve.tensor_tensor(scores[:, q % 2, kt, :], psS[:, n % 2, :], decay[:, at:at + BLOCK],
                                              ALU.mult).then_inc(s["scores_copied"], 1)
                        if q:
                            add(q - 1)
                    add(blocks - 1)


CENTRES, VC = 12, 16
NV = D + CENTRES


def attention2_phase(nc, k, w_dram, v_bias):
    with Phase(nc, "a2_") as phase:
        sb, ps, sem = phase.sbuf, phase.psum, phase.semaphore
        w, vb = sb("w", [KP, KC, NV]), sb("vb", [P, D])
        junk, norms = sb("junk", [P, D]), sb("norms", [P, TILES])
        raw = sb("raw", [P, TILES, CENTRES])
        top, peak = sb("top", [P, BATCH, CENTRES]), sb("peak", [P, BATCH, CENTRES])
        factor = sb("factor", [P, TILES, CENTRES])
        values = sb("values", [P, TILES, NV])
        xT = sb("xT", [KP, KC, SEQ])
        kern = sb("kern", [P, 2, TPS, BLOCK])
        inverse, chosen = sb("inverse", [P, TPB, CENTRES]), sb("chosen", [P, TPB, D])
        psE, psO = ps("psE", [P, 4, BANK]), ps("psO", [P, 2, 2, BANK])
        names = ("loaded norms_own norms_ready v_ready v_copied own tops_ready peak_ready shifted factor_ready values_ready xT_ready "
                 "products_ready kern_ready out_ready out_used").split()
        s = {n: sem(n) for n in names}
        blocks = SEQ // BLOCK
        UPB = blocks * TPS

        with nc.Block() as block:
            @block.sync
            def _(sp):
                sp.dma_start(w[:, :, :], w_dram).then_inc(s["loaded"], 16)
                sp.dma_start(vb[:, :], v_bias.partition_broadcast(P)).then_inc(s["loaded"], 16)

            @block.tensor
            def _(pe):
                pe.wait_ge(s["loaded"], 32)
                values_program(pe, psE, w, s["v_ready"], s["v_copied"], xnT=k.xnT, n=NV)
                pe.wait_ge(s["v_copied"], TILES // 2)
                with pe.Fori(0, BATCH) as b:
                    pe.wait_ge(s["xT_ready"], b + 1)

                    def weigh(q):
                        pe.wait_ge(s["values_ready"], 1)
                        pe.wait_ge(s["kern_ready"], b * UPB + (q + 1) * TPS)
                        pe.wait_ge(s["out_used"], b * blocks + max(q - 1, 0))
                        for t in range(TPB):
                            for m in range(TPS):
                                last = pe.matmul(psO[:, q % 2, t // 2, (t % 2) * NV:(t % 2 + 1) * NV], kern[:, q % 2, m, t * P:(t + 1) * P],
                                                 flat(values)[:, ds((b * TPS + m) * NV, NV)], start=(m == 0), stop=(m == TPS - 1))
                        last.then_inc(s["out_ready"], 1)

                    for q in range(blocks):
                        for m in range(TPS):
                            n = q * TPS + m
                            pe.wait_ge(s["kern_ready"], b * UPB + max(n - 3, 0))
                            for j in range(KC):
                                last = pe.matmul(psE[:, n % 4, :], xT[:, j, m * P:(m + 1) * P], xT[:, j, q * BLOCK:(q + 1) * BLOCK],
                                                 start=(j == 0), stop=(j == KC - 1))
                            last.then_inc(s["products_ready"], 1)
                        if q:
                            weigh(q - 1)
                    weigh(blocks - 1)

            @block.scalar
            def _(act):
                for t in range(TILES):
                    if t:
                        act.wait_ge(s["norms_own"], t)
                    act.activation(junk[:, :], k.xn[:, t, :], ACT.Square, accum_out=norms[:, t:t + 1]).then_inc(s["norms_own"], 1)
                act.wait_ge(s["shifted"], BATCH)
                act.activation(flat(factor), flat(raw), ACT.Exp, scale=1.0 / D).then_inc(s["factor_ready"], 1)
                with act.Fori(0, BATCH) as b:
                    for n in range(UPB):
                        q, m = n // TPS, n % TPS
                        act.wait_ge(s["products_ready"], b * UPB + n + 1)
                        if m == 0:
                            act.wait_ge(s["out_ready"], b * blocks + max(q - 1, 0))
                        act.activation(kern[:, q % 2, m, :], psE[:, n % 4, :], ACT.Exp, scale=2.0 / D).then_inc(s["kern_ready"], 1)

            @block.gpsimd
            def _(pool):
                pool.wait_ge(s["tops_ready"], BATCH)
                pool.partition_all_reduce(flat(peak), flat(top), P, bass.bass_isa.ReduceOp.max).then_inc(s["peak_ready"], 1)

            @block.vector
            def _(dve):
                own = Own(dve, s["own"])
                dve.wait_ge(s["loaded"], 32)
                for n in range(TILES // 2):
                    t = slice(2 * n, 2 * n + 2)
                    src = psE[:, n % 2, 0:2 * NV].rearrange("p (a b) -> p a b", b=NV)
                    dve.wait_ge(s["v_ready"], n + 1)
                    dve.wait_ge(s["norms_own"], 2 * n + 2)
                    dve.tensor_tensor(values[:, t, 0:D], src[:, :, 0:D], across(vb[:, :], 2), ALU.add)
                    dve.scalar_tensor_tensor(out=raw[:, t, :], in0=src[:, :, D:NV], scalar=2.0, in1=wide(norms[:, t], CENTRES),
                                             op0=ALU.mult, op1=ALU.subtract).then_inc(s["v_copied"], 1)
                dve.wait_ge(s["v_copied"], TILES // 2)
                for b in range(BATCH):
                    dve.tensor_reduce(top[:, b, :], raw[:, b * TPS:(b + 1) * TPS, :].rearrange("p t c -> p c t"), AXX, ALU.max)\
                       .then_inc(s["tops_ready"], 1)
                dve.wait_ge(s["peak_ready"], 1)
                for b in range(BATCH):
                    t = slice(b * TPS, (b + 1) * TPS)
                    dve.tensor_tensor(raw[:, t, :], raw[:, t, :], across(peak[:, b, :], TPS), ALU.subtract).then_inc(s["shifted"], 1)
                dve.wait_ge(s["factor_ready"], 1)
                for t in range(TILES):
                    v = values[:, t, 0:D].rearrange("p (c d) -> p c d", d=VC)
                    dve.tensor_tensor(v, v, wide(factor[:, t, :], VC), ALU.mult)
                dve.tensor_copy(values[:, :, D:NV], factor[:, :, :]).then_inc(s["values_ready"], 1)
                acc, xn = flat(k.acc), flat(k.xn)
                with dve.Fori(0, BATCH) as b:
                    own.enter(b, 2 * blocks)
                    dve.wait_ge(s["products_ready"], b * UPB)
                    dve.tensor_copy(xT[:, :, :], k.xnT[:, :, ds(b * SEQ, SEQ)]).then_inc(s["xT_ready"], 1)
                    for q in range(blocks):
                        dve.wait_ge(s["out_ready"], b * blocks + q + 1)
                        dve.wait_ge(s["out_used"], b * blocks + q)
                        for t in range(TPB):
                            part = psO[:, q % 2, t // 2, (t % 2) * NV:(t % 2 + 1) * NV]
                            last = dve.reciprocal(inverse[:, t, :], part[:, D:NV])
                        own.step(last)
                        for t in range(TPB):
                            part = psO[:, q % 2, t // 2, (t % 2) * NV:(t % 2 + 1) * NV]
                            last = dve.tensor_tensor(chosen[:, t, :].rearrange("p (c d) -> p c d", d=VC), part[:, 0:D].rearrange("p (c d) -> p c d", d=VC),
                                                     wide(inverse[:, t, :], VC), ALU.mult)
                        own.step(last)
                        at = ds((b * TPS + q * TPB) * D, TPB * D)
                        dve.tensor_tensor(acc[:, at], flat(chosen), xn[:, at], ALU.add).then_inc(s["out_used"], 1)
                own.leave(BATCH)


def affine_norm_phase(nc, k, name, src, eps, gamma_dram, beta_dram):
    with Phase(nc, name) as phase:
        sb, ps, sem = phase.sbuf, phase.psum, phase.semaphore
        stats, moments = sb("stats", [P, TILES, 6]), sb("moments", [P, TILES, 2])
        rstd0, rstd = sb("rstd0", [P, TILES]), sb("rstd", [P, TILES])
        gamma, beta = sb("gamma", [P, D]), sb("beta", [P, D])
        y = sb("y", [P, TPB, D])
        loaded, own_sem, stats_ready, eps_added, rstd_ready = (
            sem("loaded"), sem("own"), sem("stats_ready"), sem("eps_added"), sem("rstd_ready"))
        moments_ready = sem("moments_ready")

        with nc.Block() as block:
            @block.sync
            def _(sp):
                sp.dma_start(gamma[:, :], gamma_dram.partition_broadcast(P)).then_inc(loaded, 16)
                sp.dma_start(beta[:, :], beta_dram.partition_broadcast(P)).then_inc(loaded, 16)

            @block.gpsimd
            def _(pool):
                pool.wait_ge(moments_ready, 1)
                pool.tensor_scalar(rstd0[:, :], moments[:, :, 1], eps, None, ALU.add).then_inc(eps_added, 1)
                pool.wait_ge(eps_added, 1)
                pool.tensor_tensor(rstd[:, :], rstd0[:, :], k.minus_half[:, :], ALU.pow).then_inc(rstd_ready, 1)

            @block.vector
            def _(dve):
                own = Own(dve, own_sem)
                source, mom, h = flat(src), flat(moments), flat(k.h)
                with dve.Fori(0, NBLK) as g:
                    for t in range(TPB):
                        tile = g * TPB + t
                        last = dve.bn_stats(flat(stats)[:, ds(tile * 6, 6)], source[:, ds(tile * D, D)])
                    last.then_inc(stats_ready, 1)
                dve.wait_ge(stats_ready, NBLK)
                for t in range(TILES):
                    last = dve.bn_aggr(moments[:, t, :], stats[:, t, :])
                last.then_inc(moments_ready, 1)
                dve.wait_ge(rstd_ready, 1)
                dve.wait_ge(loaded, 32)
                with dve.Fori(0, NBLK) as g:
                    own.enter(g, 4)
                    for t in range(TPB):
                        tile = g * TPB + t
                        last = dve.tensor_scalar(y[:, t, :], source[:, ds(tile * D, D)], mom[:, ds(tile * 2, 1)], rstd[:, ds(tile, 1)],
                                                 ALU.subtract, ALU.mult)
                    own.step(last)
                    own.step(dve.tensor_tensor(y[:, :, :], y[:, :, :], across(gamma[:, :], TPB), ALU.mult))
                    own.step(dve.tensor_tensor(y[:, :, :], y[:, :, :], across(beta[:, :], TPB), ALU.add))
                    at = ds(g * TPB * D, TPB * D)
                    own.step(dve.tensor_tensor(h[:, at], h[:, at], flat(y), ALU.add))
                own.leave(NBLK)


HEADS3, HD3 = 12, 16
QMAX, QMIN = 127.0, -128.0
ROUND = 12582912.0
V_SCALE = 2.0 ** 60
P_SCALE = 2.0 ** 111
EXP_C0, EXP_C1 = 0.35815147, 0.96963238


def attention3_setup(nc, k, q, a):
    with Phase(nc, "s3_") as phase:
        sb, ps, sem = phase.sbuf, phase.psum, phase.semaphore
        w, scale = sb("w", [KP, KC, 3 * D]), sb("scale", [KP, 3 * D])
        inverse = sb("inverse", [KP, 3 * D])
        vscale, vf = sb("vscale", [P, D]), sb("vf", [P, D])
        qkscale = sb("qkscale", [HD3, HEADS3, 2])
        real = sb("real", [P, 2, D])
        whole = sb("whole", [P, 2, D], I16)
        tmp = sb("tmp", [P, 4])
        psV = ps("psV", [P, 2, BANK])
        loaded, own_sem, w_ready, v_ready, v_copied = (
            sem("loaded"), sem("own"), sem("w_ready"), sem("v_ready"), sem("v_copied"))

        with nc.Block() as block:
            @block.sync
            def _(sp):
                sp.dma_start(w[:, :, :], a["a3_w"]).then_inc(loaded, 16)
                sp.dma_start(scale[:, :], a["a3_scale"].partition_broadcast(KP)).then_inc(loaded, 16)
                sp.dma_start(vscale[:, :], a["a3_scale"][2 * D:3 * D].partition_broadcast(P)).then_inc(loaded, 16)
                sp.dma_start(qkscale[:, :, :], a["a3_qkscale"]).then_inc(loaded, 16)
                for n, s in enumerate(("a3_s_act1", "a3_s_attn", "a3_s_act2", "a3_s_act3")):
                    sp.dma_start(q.s[:, n:n + 1], a[s].partition_broadcast(P)).then_inc(loaded, 16)

            @block.vector
            def _(dve):
                own = Own(dve, own_sem)
                dve.wait_ge(loaded, 8 * 16)
                own.step(dve.reciprocal(inverse[:, :], scale[:, :]))
                own.step(dve.tensor_tensor(w[:, :, :], w[:, :, :], across(inverse[:, :], KC), ALU.mult))
                own.step(dve.tensor_scalar(flat(w), flat(w), QMAX, QMIN, ALU.min, ALU.max))
                dve.tensor_scalar(flat(q.w), flat(w), ROUND, ROUND, ALU.add, ALU.subtract).then_inc(w_ready, 1)
                own.step(dve.reciprocal(q.inv[:, :], q.s[:, :]))
                is1, isa, is2 = q.inv[:, 0:1], q.inv[:, 1:2], q.inv[:, 2:3]
                dve.tensor_scalar(vf[:, :], vscale[:, :], is1, None, ALU.mult)
                own.step(dve.memset(q.fqk[:, :, :], 0.0))
                dve.tensor_scalar(flat(q.fqk)[:, 0:HEADS3 * 2], flat(qkscale), q.inv[0:HD3, 0:1], None, ALU.mult)
                own.step(dve.tensor_scalar(q.fa[:, :], q.s[:, 0:1], q.s[:, 0:1], HD3 ** -0.5, ALU.mult, ALU.mult))
                own.step(dve.tensor_scalar(q.fa[:, :], q.fa[:, :], isa, None, ALU.mult))
                own.step(dve.tensor_scalar(q.fo[:, :], q.s[:, 0:1], is2, P_SCALE / V_SCALE, ALU.mult, ALU.mult))

                def floor(out, y, t):
                    own.step(dve.tensor_scalar(out, y, ROUND, ROUND, ALU.add, ALU.subtract))
                    own.step(dve.tensor_tensor(t, out, y, ALU.is_gt))
                    own.step(dve.tensor_tensor(out, out, t, ALU.subtract))

                y, t = tmp[:, 0:1], tmp[:, 1:2]
                own.step(dve.tensor_scalar(y, isa, -0.6931, None, ALU.mult))
                floor(q.x0[:, :], y, t)
                own.step(dve.tensor_scalar(y, isa, EXP_C1 / EXP_C0, None, ALU.mult))
                floor(q.half_b[:, :], y, t)
                own.step(dve.tensor_scalar(y, isa, isa, 1.0 / EXP_C0, ALU.mult, ALU.mult))
                floor(q.c[:, :], y, t)
                own.step(dve.tensor_scalar(t, q.c[:, :], 0.0, None, ALU.is_gt))
                own.step(dve.tensor_scalar(q.fo[:, :], q.fo[:, :], t, None, ALU.mult))
                own.step(dve.tensor_scalar(q.half_b[:, :], q.half_b[:, :], 0.5, None, ALU.mult))
                own.step(dve.tensor_scalar(y, q.half_b[:, :], q.half_b[:, :], -1.0, ALU.mult, ALU.mult))
                own.step(dve.tensor_scalar(q.c[:, :], q.c[:, :], 1.0, y, ALU.max, ALU.add))
                dve.tensor_scalar(q.low_near[:, :], q.x0[:, :], 30.0, -ROUND, ALU.mult, ALU.add)
                own.step(dve.reciprocal(q.inv_x0[:, :], q.x0[:, :]))
                own.step(dve.tensor_scalar(q.minus_inv_x0[:, :], q.inv_x0[:, :], -1.0, None, ALU.mult))
                own.step(dve.tensor_scalar(y, q.x0[:, :], -1.0, None, ALU.mult))
                own.step(dve.tensor_scalar(q.x0_ident[:, :], k.ident[:, :], y, None, ALU.mult))
                for n in range(TILES // 2):
                    dve.wait_ge(v_ready, n + 1)
                    own.step(dve.tensor_tensor(real[:, :, :], psV[:, n % 2, 0:2 * D].rearrange("p (a b) -> p a b", b=D),
                                               across(vf[:, :], 2), ALU.mult))
                    own.step(dve.tensor_scalar(flat(whole), flat(real), QMAX, QMIN, ALU.min, ALU.max))
                    dve.tensor_scalar(q.values[:, 2 * n:2 * n + 2, :].rearrange("p a b -> p (a b)"), flat(whole), V_SCALE, None, ALU.mult)\
                       .then_inc(v_copied, 1)
                    dve.wait_ge(v_copied, n + 1)

            @block.tensor
            def _(pe):
                pe.wait_ge(w_ready, 1)
                values_program(pe, psV, q.w[:, :, 2 * D:3 * D], v_ready, v_copied, xnT=k.xnT)


class Integer:

    def __init__(self, phase):
        sb = phase.sbuf
        self.w = sb("w", [KP, KC, 3 * D])
        self.s, self.inv = sb("s", [P, 4]), sb("inv", [P, 4])
        self.fqk = sb("fqk", [HD3, HEADS3 + 1, 2])
        self.fa, self.fo, self.x0, self.half_b, self.c = (sb(n, [P, 1]) for n in ("fa", "fo", "x0", "half_b", "c"))
        self.low_near, self.inv_x0, self.minus_inv_x0 = (sb(n, [P, 1]) for n in ("low_near", "inv_x0", "minus_inv_x0"))
        self.x0_ident = sb("x0_ident", [P, P], BF16)
        self.values = sb("values", [P, TILES, D], BF16)


def attention3_heads(nc, k, q, turned_out):
    with Phase(nc, "t3_") as phase:
        sb, ps, sem = phase.sbuf, phase.psum, phase.semaphore
        wh, fh = sb("wh", [KP, KC, 2, HD3]), sb("fh", [HD3, 2])
        qk = sb("qk", [HD3, BATCH, 2, SEQ], BF16)
        vh = sb("vh", [P, BATCH, TPS, HD3], BF16)
        n16 = sb("n16", [P, SEQ], I16)
        clipped_n = sb("clipped_n", [P, 2, SEQ], BF16)
        digit = sb("digit", [P, 2, SEQ], BF16)
        power = sb("power", [P, 2, SEQ], I32)
        square = sb("square", [P, 2, SEQ])
        expo = sb("expo", [P, 2, SEQ])
        log = sb("log", [P, SEQ])
        ratio = sb("ratio", [P, 2, SEQ], I32)
        whole = sb("whole", [P, 2, SEQ])
        digit16 = sb("digit16", [P, 2, SEQ], I16)
        big = sb("big", [P, SEQ], I16)
        weights = sb("weights", [P, 2, SEQ], I16)
        weightsT = sb("weightsT", [P, 2, TPS, BLOCK], BF16)
        UH = BATCH * TPS
        top, near, peak, lowest, offset, bsq, total, logtotal = (
            sb(n, [P, UH]) for n in ("top", "near", "peak", "lowest", "offset", "bsq", "total", "logtotal"))
        staged = sb("staged", [HD3, 2, BLOCK], I16)
        stored_o = sb("stored_o", [HD3, 2, BLOCK], I16)
        psS, psR = ps("psS", [P, 4, BANK]), ps("psR", [P, 2, BANK])
        psT = ps("psT", [P, SEQ], BF16)
        psO = ps("psO", [P, BANK])
        names = ("own act_own scores_ready n_ready digit16_ready whole_ready digits_ready rest_ready square_ready power_ready exp_ready ratio_ready weights_ready "
                 "turned copied small_ready staged_ready clipped pool_turn wh_ready vh_ready stored0 stored1").split()
        s = {n: sem(n) for n in names}
        LAST = HEADS3 * BATCH * TPS

        def wait(eng, name, value):
            if not (isinstance(value, int) and value <= 0):
                eng.wait_ge(s[name], value)

        ORDER = ("proj0", "pv_before", "proj1", "proj2", "proj3", "pv")

        def use(H, what):
            if isinstance(H, int) and H == 0:
                return 4 + [o for o in ORDER if o != "pv_before"].index(what)
            return H * 6 + 3 + ORDER.index(what)

        USES = {1: "proj0", 2: "pv_before", 3: "proj1", 4: "proj2", 5: "proj3", 6: "pv"}

        def uses_of(H, t):
            what = USES.get(t)
            if what is None or (what == "pv_before" and isinstance(H, int) and H == 0):
                return None
            return what

        def all_heads(eng, head, own=None, per=0):
            for b in range(BATCH):
                head(0, b)
            if own:
                done = own.n
            with eng.Fori(0, HEADS3 - 1) as i:
                if own:
                    own.enter(i, per)
                for b in range(BATCH):
                    head(i + 1, b)
            if own:
                own.leave(HEADS3 - 1)

        nc.scalar.preload_act_table_set("natural_log_exp_and_others")
        with nc.Block() as block:
            @block.tensor
            def _(pe):
                def project(n, batch, index):
                    part, blk = n // 2, n % 2
                    wait(pe, "staged_ready", index)
                    for j in range(KC):
                        last = pe.matmul(psO[0:HD3, :], wh[:, j, part, :], k.xnT[:, j, batch * SEQ + blk * BLOCK:batch * SEQ + (blk + 1) * BLOCK],
                                         start=(j == 0), stop=(j == KC - 1))
                    last.then_inc(s["small_ready"], 1)

                def scores(g, b, t):
                    wait(pe, "n_ready", g - 1)
                    for blk in range(2):
                        last = pe.matmul(psS[:, (t % 2) * 2 + blk, :], qk[:, b, 0, t * P:(t + 1) * P],
                                         qk[:, b, 1, blk * BLOCK:(blk + 1) * BLOCK], start=True, stop=True)
                    last.then_inc(s["scores_ready"], 1)

                def rest(g, t):
                    wait(pe, "digits_ready", g + 1)
                    wait(pe, "square_ready", g)
                    for blk in range(2):
                        cols = slice(blk * BLOCK, (blk + 1) * BLOCK)
                        pe.matmul(psR[:, blk, :], k.ident16[:, :], clipped_n[:, t % 2, cols], start=True, stop=False)
                        last = pe.matmul(psR[:, blk, :], q.x0_ident[:, :], digit[:, t % 2, cols], start=False, stop=True)
                    last.then_inc(s["rest_ready"], 1)

                def turn(g, t):
                    wait(pe, "weights_ready", g + 1)
                    wait(pe, "copied", g)
                    for kt in range(TPS):
                        last = pe.transpose(psT[:, kt * P:(kt + 1) * P], weights[:, t % 2, kt * P:(kt + 1) * P].bitcast(BF16), k.ident16[:, :])
                    last.then_inc(s["turned"], 1)

                def product(H, b, half, index):
                    wait(pe, "staged_ready", index)
                    wait(pe, "copied", H * TPS + (half + 1) * TPB)
                    wait(pe, "vh_ready", H + 1)
                    for kt in range(TPS):
                        last = pe.matmul(psO[0:HD3, :], vh[:, b, kt, :], weightsT[:, half, kt, :], start=(kt == 0), stop=(kt == TPS - 1))
                    last.then_inc(s["small_ready"], 1)

                def head(h, b):
                    H = h * 2 + b
                    for t in range(TPS):
                        g = H * TPS + t
                        if t < TPS - 1:
                            scores(g + 1, b, t + 1)
                        else:
                            wait(pe, "clipped", use(H, "proj3") + 1)
                            scores(g + 1, 1 - b, 0)
                        rest(g, t)
                        if not (isinstance(g, int) and g < 2):
                            turn(g - 2, t % 2)
                        what = uses_of(H, t)
                        if what == "pv":
                            product(H, b, 0, use(H, what))
                        elif what == "pv_before":
                            product(H + -1 if not isinstance(H, int) else H - 1, 1 - b, 1, use(H, what))
                        elif what:
                            if what == "proj0":
                                wait(pe, "wh_ready", h + 1 + b)
                            project(int(what[-1]), 1 - b, use(H, what))

                wait(pe, "wh_ready", 1)
                for n in range(4):
                    project(n, 0, n)
                wait(pe, "clipped", 4)
                scores(0, 0, 0)
                all_heads(pe, head)
                turn(LAST - 2, 0)
                turn(LAST - 1, 1)
                H = HEADS3 * BATCH
                product(H - 1, 1, 1, use(H, "proj0"))

            @block.vector
            def _(dve):
                own = Own(dve, s["own"])

                def clip(index, slot, out):
                    wait(dve, "staged_ready", index + 1)
                    dve.tensor_scalar(out, staged[:, slot, :], QMAX, QMIN, ALU.min, ALU.max).then_inc(s["clipped"], 1)

                def clip_use(h, b, H, what):
                    index = use(H, what)
                    slot = (ORDER.index(what) + 1) % 2 if not (isinstance(H, int) and H == 0) else index % 2
                    if what.startswith("pv"):
                        half = 0 if what == "pv" else 1
                        before = h * 2 + b + -int(what == "pv_before")
                        wait(dve, "stored%d" % half, before * 16)
                        clip(index, slot, stored_o[:, half, :])
                    else:
                        n = int(what[-1])
                        clip(index, slot, qk[:, 1 - b, n // 2, (n % 2) * BLOCK:(n % 2 + 1) * BLOCK])

                def exponential(g, c, t):
                    wait(dve, "square_ready", g + 1)
                    wait(dve, "power_ready", g + 1)
                    wait(dve, "ratio_ready", g - 1)
                    dve.scalar_tensor_tensor(out=expo[:, t % 2, :], in0=square[:, t % 2, :], scalar=q.c[:, 0:1],
                                             in1=power[:, t % 2, :].bitcast(F32), op0=ALU.add, op1=ALU.mult,
                                             accum_out=total[:, c:c + 1]).then_inc(s["exp_ready"], 1)

                def exponents(g, t):
                    wait(dve, "whole_ready", g + 1)
                    wait(dve, "weights_ready", g)
                    high = whole[:, t % 2, :].bitcast(I16).rearrange("p (n two) -> p n two", two=2)[:, :, 1]
                    return own.mark(dve.tensor_scalar(big[:, :], high, 1.0 / 128, 2.0 ** -9 - 127 - 16, ALU.mult, ALU.add))

                def weigh(g, t, exponents_done):
                    own.await_step(exponents_done)
                    wait(dve, "turned", g - 1)
                    dve.tensor_scalar(weights[:, t % 2, :], big[:, :], 0.0, -128.0, ALU.min, ALU.mult).then_inc(s["weights_ready"], 1)

                def unit(g, c, t):
                    known = isinstance(g, int)
                    wait(dve, "scores_ready", g + 1)
                    dve.tensor_scalar(n16[:, :], psS[:, (t % 2) * 2:(t % 2) * 2 + 2, :].rearrange("p a b -> p (a b)"), q.fa[:, 0:1], QMIN,
                                      ALU.mult, ALU.max, accum_out=top[:, c:c + 1]).then_inc(s["n_ready"], 1)
                    wait(dve, "n_ready", g + 1)
                    own.step(dve.tensor_scalar(near[:, c:c + 1], top[:, c:c + 1], QMAX, ROUND, ALU.min, ALU.add))
                    dve.tensor_scalar(lowest[:, c:c + 1], near[:, c:c + 1], q.low_near[:, 0:1], QMIN, ALU.add, ALU.max)
                    own.step(dve.tensor_scalar(peak[:, c:c + 1], near[:, c:c + 1], ROUND, None, ALU.subtract))
                    wait(dve, "rest_ready", g - 1)
                    wait(dve, "power_ready", g - 1)
                    dve.tensor_scalar(clipped_n[:, t % 2, :], n16[:, :], QMAX, lowest[:, c:c + 1], ALU.min, ALU.max)
                    dve.tensor_scalar(offset[:, c:c + 1], peak[:, c:c + 1], q.minus_inv_x0[:, 0:1], -0.5 + 2.0 ** -10, ALU.mult, ALU.add)
                    wait(dve, "square_ready", g - 1)
                    own.step(dve.scalar_tensor_tensor(out=bsq[:, c:c + 1], in0=peak[:, c:c + 1], scalar=-1.0, in1=q.half_b[:, 0:1],
                                                      op0=ALU.mult, op1=ALU.add))
                    dve.tensor_scalar(digit16[:, t % 2, :], clipped_n[:, t % 2, :], q.inv_x0[:, 0:1], offset[:, c:c + 1], ALU.mult, ALU.add)\
                       .then_inc(s["digit16_ready"], 1)
                    if not known or g >= 2:
                        exponents_done = exponents(g - 2, t % 2)
                    if not known or g >= 1:
                        exponential(g - 1, (c - 1) % UH, (t - 1) % 2)
                    if not known or g >= 2:
                        weigh(g - 2, t % 2, exponents_done)

                def head(h, b):
                    for t in range(TPS):
                        unit((h * 2 + b) * TPS + t, b * TPS + t, t)
                        what = uses_of(h * 2 + b, t - 1)
                        if what:
                            clip_use(h, b, h * 2 + b, what)

                for n in range(4):
                    clip(n, n % 2, qk[:, 0, n // 2, (n % 2) * BLOCK:(n % 2 + 1) * BLOCK])
                all_heads(dve, head, own, UH * 4)
                exponential(LAST - 1, UH - 1, 1)
                for g in (LAST - 2, LAST - 1):
                    weigh(g, g % 2, exponents(g, g % 2))
                H = HEADS3 * BATCH
                index = use(H, "proj0")
                wait(dve, "stored1", (H - 1) * 16)
                clip(index, index % 2, stored_o[:, 1, :])

            @block.scalar
            def _(act):
                def squares(g, c, t):
                    wait(act, "rest_ready", g + 1)
                    wait(act, "exp_ready", g - 1)
                    act.activation(square[:, t % 2, :], psR[:, :, :].rearrange("p a b -> p (a b)"), ACT.Square, bias=bsq[:, c:c + 1])\
                       .then_inc(s["square_ready"], 1)

                def ratios(g, c, t):
                    wait(act, "exp_ready", g + 1)
                    wait(act, "ratio_ready", g)
                    act.activation(logtotal[:, c:c + 1], total[:, c:c + 1], ACT.Ln)
                    act.activation(log[:, :], expo[:, t % 2, :], ACT.Ln).then_inc(s["act_own"], 1)
                    wait(act, "act_own", g + 1)
                    wait(act, "whole_ready", g - 1)
                    act.activation(ratio[:, t % 2, :], log[:, :], ACT.Exp, bias=logtotal[:, c:c + 1], scale=-1.0).then_inc(s["ratio_ready"], 1)

                def copy_turned(g, col, half, before):
                    wait(act, "turned", g + 1)
                    if before is not None:
                        wait(act, "small_ready", before + 1)
                    act.activation(weightsT[:, half, :, col * P:(col + 1) * P], psT[:, :].rearrange("p (a b) -> p a b", b=P), ACT.Copy)\
                       .then_inc(s["copied"], 1)

                def stage(index, slot, factor):
                    wait(act, "small_ready", index + 1)
                    wait(act, "clipped", index - 1)
                    act.activation(staged[:, slot, :], psO[0:HD3, :], ACT.Copy, scale=factor).then_inc(s["staged_ready"], 1)

                def head(h, b):
                    H = h * 2 + b
                    for t in range(TPS):
                        g, c = H * TPS + t, b * TPS + t
                        known = isinstance(g, int)
                        if not known or g >= 1:
                            ratios(g - 1, (c - 1) % UH, (t - 1) % 2)
                        squares(g, c, t)
                        if not known or g >= 2:
                            u = (t - 2) % TPS
                            half = u // TPB
                            at = H if t >= 2 else (H - 1 if known else H + -1)
                            before = None
                            if u % TPB == 0 and not (known and at < 1):
                                before = use(at - 1 if isinstance(at, int) else at + -1, "pv") if half == 0 else use(at, "pv_before")
                            copy_turned(g - 2, u % TPB, half, before)
                        what = uses_of(H, t)
                        if what:
                            factor = q.fo[0:HD3, 0:1] if what.startswith("pv") else fh[:, int(what[-1]) // 2:int(what[-1]) // 2 + 1]
                            index = use(H, what)
                            slot = (ORDER.index(what) + 1) % 2 if not (isinstance(H, int) and H == 0) else index % 2
                            stage(index, slot, factor)

                wait(act, "wh_ready", 1)
                for n in range(4):
                    stage(n, n % 2, fh[:, n // 2:n // 2 + 1])
                all_heads(act, head)
                ratios(LAST - 1, UH - 1, 1)
                copy_turned(LAST - 2, 2, 1, None)
                copy_turned(LAST - 1, 3, 1, None)
                H = HEADS3 * BATCH
                index = use(H, "proj0")
                stage(index, index % 2, q.fo[0:HD3, 0:1])

            @block.gpsimd
            def _(pool):
                def wholes(g, t):
                    wait(pool, "ratio_ready", g + 1)
                    wait(pool, "weights_ready", g - 1)
                    pool.sem_inc(s["pool_turn"], 1)
                    pool.tensor_scalar(whole[:, t % 2, :], ratio[:, t % 2, :], *SAME).then_inc(s["whole_ready"], 1)

                def digits(g, t):
                    wait(pool, "digit16_ready", g + 1)
                    wait(pool, "rest_ready", g - 1)
                    pool.sem_inc(s["pool_turn"], 1)
                    pool.tensor_scalar(digit[:, t % 2, :], digit16[:, t % 2, :], *SAME).then_inc(s["digits_ready"], 1)

                def powers(g, t):
                    wait(pool, "exp_ready", g - 1)
                    pool.sem_inc(s["pool_turn"], 1)
                    pool.tensor_scalar(power[:, t % 2, :], digit16[:, t % 2, :], -2.0 ** 23, 157 * 2.0 ** 23, ALU.mult, ALU.add)\
                        .then_inc(s["power_ready"], 1)

                def weights_of(head_index):
                    source = flat(q.w)
                    for j in range(KC):
                        for part in range(2):
                            pool.tensor_copy(wh[:, j, part, :], source[:, ds(j * 3 * D + part * D + head_index * HD3, HD3)])
                    pool.tensor_copy(fh[:, :], flat(q.fqk)[:, ds(head_index * 2, 2)]).then_inc(s["wh_ready"], 1)

                def head(h, b):
                    H = h * 2 + b
                    for t in range(TPS):
                        g = H * TPS + t
                        if t == 0:
                            if not (isinstance(H, int) and H < 2):
                                wait(pool, "small_ready", use(H + -1 if not isinstance(H, int) else H - 1, "pv_before") + 1)
                            pool.tensor_copy(vh[:, b], q.values[:, b * TPS:(b + 1) * TPS, ds(h * HD3, HD3)]).then_inc(s["vh_ready"], 1)
                            if b == 1:
                                wait(pool, "staged_ready", use(H + -1 if not isinstance(H, int) else H - 1, "proj3") + 1)
                                weights_of(h + 1)
                        if not isinstance(g, int) or g >= 2:
                            wholes(g - 2, t % 2)
                        digits(g, t)
                        powers(g, t)

                weights_of(0)
                all_heads(pool, head)
                wholes(LAST - 2, 0)
                wholes(LAST - 1, 1)

            @block.sync
            def _(sp):
                def store(h, b, half, index):
                    wait(sp, "clipped", index + 1)
                    cols = slice(b * SEQ + half * BLOCK, b * SEQ + (half + 1) * BLOCK)
                    sp.dma_start(turned_out[ds(h * HD3, HD3), cols], stored_o[:, half, :]).then_inc(s["stored%d" % half], 16)

                def head(h, b):
                    H = h * 2 + b
                    if not (isinstance(H, int) and H == 0):
                        store(h if b else (h - 1 if isinstance(h, int) else h + -1), 1 - b, 1, use(H, "pv_before"))
                    store(h, b, 0, use(H, "pv"))

                all_heads(sp, head)
                store(HEADS3 - 1, 1, 1, use(HEADS3 * BATCH, "proj0"))
                for half in range(2):
                    sp.wait_ge(s["stored%d" % half], HEADS3 * BATCH * 16)


def attention3_output(nc, k, q, a, turned_out):
    with Phase(nc, "o3_") as phase:
        sb, ps, sem = phase.sbuf, phase.psum, phase.semaphore
        o16, o = sb("o16", [KP, KC, TOK], I16), sb("o", [KP, KC, TOK], BF16)
        w, scale, inverse = sb("w", [KP, KC, D]), sb("scale", [KP, D]), sb("inverse", [KP, D])
        wi = sb("wi", [KP, KC, D], BF16)
        factor, bias = sb("factor", [P, D]), sb("bias", [P, D])
        y = sb("y", [P, TPB, D])
        psY = ps("psY", [P, 2, 2, BANK])
        loaded, own_sem, ready, y_ready, y_used = sem("loaded"), sem("own"), sem("ready"), sem("y_ready"), sem("y_used")

        with nc.Block() as block:
            @block.sync
            def _(sp):
                sp.dma_start(o16[:, :, :], turned_out.rearrange("(c p) t -> p c t", p=KP)).then_inc(loaded, 16)
                sp.dma_start(w[:, :, :], a["a3_wo"]).then_inc(loaded, 16)
                sp.dma_start(scale[:, :], a["a3_wo_scale"].partition_broadcast(KP)).then_inc(loaded, 16)
                sp.dma_start(factor[:, :], a["a3_wo_scale"].partition_broadcast(P)).then_inc(loaded, 16)
                sp.dma_start(bias[:, :], a["a3_wo_bias"].partition_broadcast(P)).then_inc(loaded, 16)

            @block.vector
            def _(dve):
                own = Own(dve, own_sem)
                dve.wait_ge(loaded, 5 * 16)
                own.step(dve.reciprocal(inverse[:, :], scale[:, :]))
                own.step(dve.tensor_tensor(w[:, :, :], w[:, :, :], across(inverse[:, :], KC), ALU.mult))
                own.step(dve.tensor_scalar(flat(w), flat(w), QMAX, QMIN, ALU.min, ALU.max))
                dve.tensor_scalar(flat(wi), flat(w), ROUND, ROUND, ALU.add, ALU.subtract)
                dve.tensor_scalar(factor[:, :], factor[:, :], q.s[:, 2:3], None, ALU.mult)
                dve.tensor_copy(flat(o), flat(o16)).then_inc(ready, 1)
                dve.wait_ge(ready, 1)
                h = flat(k.h)
                with dve.Fori(0, NBLK // 2) as i:
                    own.enter(i, 2 * 5)
                    for n in range(2):
                        dve.wait_ge(y_ready, i * 2 + n + 1)
                        dve.wait_ge(y_used, i * 2 + n)
                        for half in range(2):
                            last = dve.tensor_tensor(y[:, half * 2:half * 2 + 2, :], psY[:, n, half, 0:2 * D].rearrange("p (a b) -> p a b", b=D),
                                                     across(factor[:, :], 2), ALU.mult)
                        own.step(last)
                        own.step(dve.tensor_tensor(y[:, :, :], y[:, :, :], across(bias[:, :], TPB), ALU.add))
                        own.step(dve.tensor_scalar(flat(y), flat(y), q.inv[:, 3:4], QMAX, ALU.mult, ALU.min))
                        own.step(dve.tensor_scalar(flat(y), flat(y), QMIN, ROUND, ALU.max, ALU.add))
                        own.step(dve.tensor_scalar(flat(y), flat(y), ROUND, q.s[:, 3:4], ALU.subtract, ALU.mult))
                        at = ds((i * 2 + n) * TPB * D, TPB * D)
                        dve.tensor_tensor(h[:, at], h[:, at], flat(y), ALU.add).then_inc(y_used, 1)
                own.leave(NBLK // 2)

            @block.tensor
            def _(pe):
                pe.wait_ge(ready, 1)
                for g in range(NBLK):
                    if g >= 2:
                        pe.wait_ge(y_used, g - 1)
                    for t in range(TPB):
                        for j in range(KC):
                            at = (g * TPB + t) * P
                            last = pe.matmul(psY[:, g % 2, t // 2, (t % 2) * D:(t % 2 + 1) * D], o[:, j, at:at + P], wi[:, j, :],
                                             start=(j == 0), stop=(j == KC - 1))
                    last.then_inc(y_ready, 1)


def attention3_phase(nc, k, a):
    turned_out = nc.dram_tensor("turned_out", (D, TOK), I16, kind="Internal").ap()
    with Phase(nc, "i3_") as phase:
        q = Integer(phase)
        attention3_setup(nc, k, q, a)
        attention3_heads(nc, k, q, turned_out)
        attention3_output(nc, k, q, a, turned_out)


class Persistent:

    def __init__(self, nc, c):
        sb = lambda n, s, t=F32: c.enter_context(nc.sbuf_tensor(n, s, t))
        self.h = sb("h", [P, TILES, D])
        self.xn = sb("xn", [P, TILES, D])
        self.xnT = sb("xnT", [KP, KC, TOK])
        self.x_high, self.x_low = sb("x_high", [P, TOK], F32R), sb("x_low", [P, TOK], F32R)
        self.x_tail = sb("x_tail", [P, TOK], F32R)
        self.acc = sb("acc", [P, TILES, D])
        self.comb = sb("comb", [P, 9, TILES])
        self.ident = sb("ident", [P, P])
        self.ident16 = sb("ident16", [P, P], BF16)
        self.minus_half = sb("minus_half", [P, TILES])
        self.rank = sb("rank", [P, 8])


def audio_tower(nc, a, out):
    with ExitStack() as c:
        k = Persistent(nc, c)
        stages = [
            lambda: pool_phase(nc, k, a["x"], a["tok_w"]),
            lambda: (norm_phase(nc, k, "n0_", k.h, split=True),
                     attention0_phase(nc, k, a["a0_wqk"], a["a0_wv"], a["a0_wo"], a["a0_anchor_w"], a["a0_anchors"], a["a0_lam"])),
            lambda: expert_layer(nc, k, "f0_", k.h, a["f0_in"], a["f0_out"], 3, gated=True,
                                 router=Router("softmax", 8, a["f0_router"], select_bias=a["f0_bias"], eps=1e-9)),
            lambda: (norm_phase(nc, k, "n2_", k.h),
                     attention1_phase(nc, k, a["a1_w"], a["a1_qk_bias"], a["a1_v_bias"], a["a1_decay"])),
            lambda: expert_layer(nc, k, "f1_", k.h, a["f1_in"], a["f1_out"], 3, gated=True,
                                 router=Router("sigmoid", 3, a["f1_router"], logit_bias=a["f1_bias"])),
            lambda: (norm_phase(nc, k, "n4_", k.h),
                     attention2_phase(nc, k, a["a2_w"], a["a2_v_bias"]),
                     expert_layer(nc, k, "g2_", k.acc, a["g2_in"], a["g2_out"], 6, a["g2_in_bias"], a["g2_out_bias"]),
                     affine_norm_phase(nc, k, "n6_", k.acc, 1e-12, a["a2_gamma"], a["a2_beta"])),
            lambda: (expert_layer(nc, k, "f2_", k.xn, a["f2_in"], a["f2_out"], 2, a["f2_in_bias"],
                                  router=Router("softmax", 8, a["f2_router"], logit_bias=a["f2_bias"], eps=1e-8,
                                                hidden=(a["f2_hidden"], a["f2_hidden_bias"]))),
                     affine_norm_phase(nc, k, "n8_", k.xn, LN_EPS, a["f2_gamma"], a["f2_beta"])),
            lambda: (norm_phase(nc, k, "n9_", k.h),
                     attention3_phase(nc, k, a)),
            lambda: expert_layer(nc, k, "f3_", k.h, a["f3_in"], a["f3_out"], 6, a["f3_in_bias"], a["f3_out_bias"],
                                 router=Router("softmax", 8, a["f3_router"], eps=1e-9)),
        ]
        for stage in stages:
            stage()
        stored = c.enter_context(nc.semaphore("stored"))
        with nc.Block() as block:
            @block.sync
            def _(sp):
                sp.dma_start(out.rearrange("b (t p) d -> p (b t) d", p=P), k.h[:, :, :]).then_inc(stored, 16)
                sp.wait_ge(stored, 16)


def expert_layer(nc, k, name, target, w_in, w_out, chunks, bias=None, out_bias=None, gated=False, router=None):
    with Phase(nc, name + "w_") as phase:
        weights = ExpertWeights(phase, w_in, w_out, chunks, gated)
        norm_phase(nc, k, name + "n_", k.h if router else target, router, normalise=router is not None, split=True, weights=weights)
        if gated:
            ones_phase(nc, k, router.experts)
        experts_phase(nc, k, name, target, weights, bias, out_bias, weighted=router is not None)


def ones_phase(nc, k, e):
    with nc.Block() as block:
        @block.vector
        def _(dve):
            dve.memset(k.comb[:, e, :], 1.0)


def _laid_out(np, i):
    f = np.ascontiguousarray

    def rows(w, p=KP):
        w = np.asarray(w)
        lead = w.shape[:-2]
        w = w.reshape(*lead, w.shape[-2] // p, p, w.shape[-1])
        return f(np.swapaxes(w, -3, -2))

    def twice(w):
        w = np.asarray(w)
        return f(np.stack([w[..., :P, :], np.concatenate([w[..., P:, :]] * 2, axis=-2)], axis=-2))

    def t(w):
        return np.swapaxes(np.asarray(w), -1, -2)

    def col(b, p=P):
        b = np.asarray(b)
        return f(np.swapaxes(b.reshape(*b.shape[:-1], b.shape[-1] // p, p), -1, -2))

    def both(*w):
        return np.concatenate(w, axis=-1)

    def more(w, shared):
        return np.concatenate([w, shared[None]], axis=0)

    j = np.arange(-3 * P, SEQ, dtype=np.float32)[None, :] - np.arange(P, dtype=np.float32)[:, None]
    decay = np.where(j >= 0, np.float32(0.99) ** np.maximum(j, 0), 0).astype(np.float32) / np.float32(D) ** np.float32(0.5)
    a = {"x": i["x"], "tok_w": rows(i["L0_tok_w"])}
    qk = np.stack([t(i["L0_attn_Wq"]), t(i["L0_attn_Wk"])], axis=1).reshape(D, 2, HEADS0, 1, HD0)
    qk = np.broadcast_to(qk, (D, 2, HEADS0, 3, HD0)).transpose(2, 0, 1, 3, 4)
    a["a0_wqk"] = twice(qk.reshape(HEADS0, D, 6 * HD0))
    a["a0_wv"] = twice(t(i["L0_attn_Wv"]))
    wo = t(i["L0_attn_Wo"]).reshape(HEADS0, HD0, D)
    a["a0_wo"] = np.concatenate([wo, wo], axis=1)
    a["a0_anchor_w"] = f(i["L0_attn_anchor_w"].transpose(1, 0, 2))
    a["a0_anchors"], a["a0_lam"] = i["L0_attn_anchors"], i["L0_attn_lam"]
    a["f0_router"], a["f0_bias"] = twice(t(i["L0_ffn_w_router"])), i["L0_ffn_expert_bias"]
    a["f0_in"] = twice(both(t(more(i["L0_ffn_Wg"], i["L0_ffn_sg"])), t(more(i["L0_ffn_Wu"], i["L0_ffn_su"]))))
    a["f0_out"] = rows(t(more(i["L0_ffn_Wd"], i["L0_ffn_sd"])), P)
    a["a1_w"] = rows(t(i["L1_attn_W_qkv"])).reshape(KP, KC, 3, D)
    b = i["L1_attn_b_qkv"]
    a["a1_qk_bias"], a["a1_v_bias"] = f(b[:2 * D].reshape(2, KC, KP).transpose(2, 0, 1)), f(b[2 * D:])
    a["a1_decay"] = decay
    a["f1_router"], a["f1_bias"] = twice(i["L1_ffn_router_w"]), i["L1_ffn_routing_bias"]
    a["f1_in"] = twice(both(more(i["L1_ffn_routed_gate"], i["L1_ffn_shared_gate"]), more(i["L1_ffn_routed_up"], i["L1_ffn_shared_up"])))
    a["f1_out"] = rows(more(i["L1_ffn_routed_down"], i["L1_ffn_shared_down"]), P)
    a["a2_w"], a["a2_v_bias"] = rows(both(i["L2_attn_val_w"], t(i["L2_attn_mu"]))), i["L2_attn_val_b"]
    a["g2_in"], a["g2_out"] = twice(i["L2_attn_w1"])[None], rows(i["L2_attn_w2"], P)[None]
    a["g2_in_bias"], a["g2_out_bias"] = col(i["L2_attn_b1"])[None], i["L2_attn_b2"][None]
    a["a2_gamma"], a["a2_beta"] = i["L2_attn_ln_g"], i["L2_attn_ln_b"]
    a["f2_hidden"], a["f2_hidden_bias"] = twice(i["L2_ffn_w1"]), f(i["L2_ffn_b1"][:, None])
    a["f2_router"], a["f2_bias"] = f(i["L2_ffn_w2"][:, None, :]), i["L2_ffn_b2"]
    a["f2_in"], a["f2_out"], a["f2_in_bias"] = twice(i["L2_ffn_down_w"]), rows(i["L2_ffn_up_w"], P), col(i["L2_ffn_down_b"])
    a["f2_gamma"], a["f2_beta"] = i["L2_ffn_gamma"], i["L2_ffn_beta"]
    a["a3_w"], a["a3_scale"] = rows(t(i["L3_attn_w_qkv"])), i["L3_attn_s_wqkv"]
    a["a3_qkscale"] = f(i["L3_attn_s_wqkv"][:2 * D].reshape(2, HEADS3, HD3).transpose(2, 1, 0))
    a["a3_wo"], a["a3_wo_scale"], a["a3_wo_bias"] = rows(t(i["L3_attn_w_proj"])), i["L3_attn_s_wproj"], i["L3_attn_b_proj"]
    for n in ("s_act1", "s_attn", "s_act2", "s_act3"):
        a["a3_" + n] = i["L3_attn_" + n]
    a["f3_router"] = twice(t(i["L3_ffn_gate_w"]))
    a["f3_in"], a["f3_out"] = twice(i["L3_ffn_w1"]), rows(i["L3_ffn_w2"], P)
    a["f3_in_bias"], a["f3_out_bias"] = col(i["L3_ffn_b1"]), i["L3_ffn_b2"]
    return {n: f(v) for n, v in a.items()}


def kernel(**inputs):
    import numpy as _np
    import concourse.bacc as _bacc
    from concourse import mybir as _mybir
    from concourse.bass_utils import run_bass_kernel_spmd as _run

    nc = _bacc.Bacc("TRN2", target_bir_lowering=False, num_devices=1)
    arrays = _laid_out(_np, {n: _np.asarray(v) for n, v in inputs.items()})
    args = {n: nc.dram_tensor(f"in_{n}", v.shape, _mybir.dt.from_np(v.dtype), kind="ExternalInput").ap() for n, v in arrays.items()}
    out = nc.dram_tensor("out_h", (BATCH, SEQ, D), F32, kind="ExternalOutput").ap()
    audio_tower(nc, args, out)
    r = _run(nc, [{f"in_{n}": v for n, v in arrays.items()}], core_ids=[0])
    return r.results[0]["out_h"]
```
